# Optimizing a Trainium2 kernel written in Bass

```python
import numpy as np
import jax
import jax.numpy as jnp

def _softmax(x, axis=-1):
    return jax.nn.softmax(x, axis=axis)

def _gelu(x):
    return jax.nn.gelu(x, approximate=True)

def _silu(x):
    return jax.nn.silu(x)

def _sigmoid(x):
    return jax.nn.sigmoid(x)

def _layernorm(x, axis=-1, eps=1e-05):
    m = jnp.mean(x, axis=axis, keepdims=True)
    v = jnp.var(x, axis=axis, keepdims=True)
    return (x - m) / jnp.sqrt(v + eps)

def _scatter_add(tgt, idx, src, axis=0):
    return tgt.at[idx].add(src)

def _segment_sum(src, seg, n):
    return jax.ops.segment_sum(src, seg, n)
kernel_name = 'mk_hybrid_d1_jaxref_r8_9cba43'

def setup_inputs(seed: int=0):
    np.random.seed(seed)
    _w = jnp.asarray

    def _L0_attn_a_setup():
        import math
        import jax, jax.numpy as jnp
        import numpy as np
        E = 128
        H = 16
        D = E // H

        def _l2norm(t, eps=1e-12):
            n = jnp.sqrt(jnp.sum(t * t, axis=-1, keepdims=True))
            return t / jnp.maximum(n, eps)
        key = jax.random.key(seed)
        ks = jax.random.split(key, 10)
        s = 0.02
        x = jax.random.normal(ks[0], (2, 512, E), dtype=jnp.float32)
        Wq = jax.random.normal(ks[1], (E, E), dtype=jnp.float32) * s
        Wk = jax.random.normal(ks[2], (E, E), dtype=jnp.float32) * s
        Wv = jax.random.normal(ks[3], (E, E), dtype=jnp.float32) * s
        Walpha = jax.random.normal(ks[4], (E, H), dtype=jnp.float32) * s
        Wbeta = jax.random.normal(ks[5], (E, H), dtype=jnp.float32) * s
        A_log = jnp.linspace(0.0, math.log(16.0), H).astype(jnp.float32)
        dt_bias = jnp.zeros((H,), dtype=jnp.float32)
        Wgate = jax.random.normal(ks[6], (E, E), dtype=jnp.float32) * s
        Wout = jax.random.normal(ks[7], (E, E), dtype=jnp.float32) * s
        rms_w = jnp.ones((D,), dtype=jnp.float32)
        return {'x': x, 'Wq': Wq, 'Wk': Wk, 'Wv': Wv, 'Walpha': Walpha, 'Wbeta': Wbeta, 'A_log': A_log, 'dt_bias': dt_bias, 'Wgate': Wgate, 'Wout': Wout, 'rms_w': rms_w}
    _L0_attn_a_in = _L0_attn_a_setup()

    def _L0_attn_b_setup():
        import jax, jax.numpy as jnp
        import numpy as np
        B, T, D = (2, 256, 128)
        H, RANK = (16, 32)
        DH = D // H
        key = jax.random.key(seed)
        ks = jax.random.split(key, 6)
        sd = 1.0 / np.sqrt(D)
        sdh = 1.0 / np.sqrt(DH)
        return {'x': jax.random.normal(ks[0], (B, T, D), dtype=jnp.float32), 'W_qkv': jax.random.normal(ks[1], (D, 3 * D), dtype=jnp.float32) * sd, 'W_q_lsr': jax.random.normal(ks[2], (H, DH, RANK), dtype=jnp.float32) * sdh, 'W_k_lsr': jax.random.normal(ks[3], (H, DH, RANK), dtype=jnp.float32) * sdh, 'lsr_core': jnp.ones((H, RANK), dtype=jnp.float32), 'W_o': jax.random.normal(ks[4], (D, D), dtype=jnp.float32) * sd}
    _L0_attn_b_in = _L0_attn_b_setup()

    def _L0_ffn_setup():
        import jax, jax.numpy as jnp
        import numpy as np
        D_MODEL, D_FF, N_EXPERTS, TOP_K = (128, 512, 8, 2)
        key = jax.random.key(seed)
        k0, k1, k2, k3 = jax.random.split(key, 4)
        x = jax.random.normal(k0, (2, 256, D_MODEL), dtype=jnp.float32)
        Wg = jax.random.normal(k1, (D_MODEL, N_EXPERTS), dtype=jnp.float32) * 0.02
        W1 = jax.random.normal(k2, (N_EXPERTS, D_MODEL, D_FF), dtype=jnp.float32) * 0.02
        b1 = jnp.zeros((N_EXPERTS, D_FF), dtype=jnp.float32)
        W2 = jax.random.normal(k3, (N_EXPERTS, D_FF, D_MODEL), dtype=jnp.float32) * 0.02
        b2 = jnp.zeros((N_EXPERTS, D_MODEL), dtype=jnp.float32)
        return {'x': x, 'Wg': Wg, 'W1': W1, 'b1': b1, 'W2': W2, 'b2': b2}
    _L0_ffn_in = _L0_ffn_setup()
    _d = {'L0_attn_a_x': _L0_attn_a_in['x'], 'L0_attn_a_Wq': _L0_attn_a_in['Wq'], 'L0_attn_a_Wk': _L0_attn_a_in['Wk'], 'L0_attn_a_Wv': _L0_attn_a_in['Wv'], 'L0_attn_a_Walpha': _L0_attn_a_in['Walpha'], 'L0_attn_a_Wbeta': _L0_attn_a_in['Wbeta'], 'L0_attn_a_A_log': _L0_attn_a_in['A_log'], 'L0_attn_a_dt_bias': _L0_attn_a_in['dt_bias'], 'L0_attn_a_Wgate': _L0_attn_a_in['Wgate'], 'L0_attn_a_Wout': _L0_attn_a_in['Wout'], 'L0_attn_a_rms_w': _L0_attn_a_in['rms_w'], 'L0_attn_b_W_qkv': _L0_attn_b_in['W_qkv'], 'L0_attn_b_W_q_lsr': _L0_attn_b_in['W_q_lsr'], 'L0_attn_b_W_k_lsr': _L0_attn_b_in['W_k_lsr'], 'L0_attn_b_lsr_core': _L0_attn_b_in['lsr_core'], 'L0_attn_b_W_o': _L0_attn_b_in['W_o'], 'L0_ffn_Wg': _L0_ffn_in['Wg'], 'L0_ffn_W1': _L0_ffn_in['W1'], 'L0_ffn_b1': _L0_ffn_in['b1'], 'L0_ffn_W2': _L0_ffn_in['W2'], 'L0_ffn_b2': _L0_ffn_in['b2']}
    _x0 = _d['L0_attn_a_x']
    _d['L0_attn_a_x'] = jax.random.normal(jax.random.fold_in(jax.random.key(seed), 1), (32, 256, 128), dtype=_x0.dtype)
    del _x0
    return _d

def reference(L0_attn_a_x, L0_attn_a_Wq, L0_attn_a_Wk, L0_attn_a_Wv, L0_attn_a_Walpha, L0_attn_a_Wbeta, L0_attn_a_A_log, L0_attn_a_dt_bias, L0_attn_a_Wgate, L0_attn_a_Wout, L0_attn_a_rms_w, L0_attn_b_W_qkv, L0_attn_b_W_q_lsr, L0_attn_b_W_k_lsr, L0_attn_b_lsr_core, L0_attn_b_W_o, L0_ffn_Wg, L0_ffn_W1, L0_ffn_b1, L0_ffn_W2, L0_ffn_b2):

    def _L0_attn_a_ref(x, Wq, Wk, Wv, Walpha, Wbeta, A_log, dt_bias, Wgate, Wout, rms_w):
        import math
        import jax, jax.numpy as jnp
        import numpy as np
        E = 128
        H = 16
        D = E // H

        def _l2norm(t, eps=1e-12):
            n = jnp.sqrt(jnp.sum(t * t, axis=-1, keepdims=True))
            return t / jnp.maximum(n, eps)
        b, s, _ = x.shape
        q = (x @ Wq).reshape(b, s, H, D)
        k = (x @ Wk).reshape(b, s, H, D)
        v = (x @ Wv).reshape(b, s, H, D)
        q = _l2norm(q) / math.sqrt(D)
        k = _l2norm(k)
        dt = jax.nn.softplus(x @ Walpha + dt_bias)
        alpha = jnp.exp(-jnp.exp(A_log) * dt)
        beta = jax.nn.sigmoid(x @ Wbeta)
        qT = jnp.moveaxis(q, 1, 0)
        kT = jnp.moveaxis(k, 1, 0)
        vT = jnp.moveaxis(v, 1, 0)
        aT = jnp.moveaxis(alpha, 1, 0)
        bT = jnp.moveaxis(beta, 1, 0)
        state0 = jnp.zeros((b, H, D, D), dtype=x.dtype)

        def step(state, inp):
            q_t, k_t, v_t, a_t, b_t = inp
            state = a_t[..., None, None] * state
            stored = jnp.einsum('bhij,bhj->bhi', state, k_t)
            delta = b_t[..., None] * (v_t - stored)
            state = state + jnp.einsum('bhi,bhj->bhij', delta, k_t)
            o_t = jnp.einsum('bhij,bhj->bhi', state, q_t)
            return (state, o_t)
        qs = jnp.swapaxes(qT, 1, 2).swapaxes(1, 1)
        _, outs = jax.lax.scan(step, state0, (qT, kT, vT, aT, bT))
        out = jnp.moveaxis(outs, 0, 1)
        var = jnp.mean(out * out, axis=-1, keepdims=True)
        out = out * jax.lax.rsqrt(var + 1e-06) * rms_w
        out = out.reshape(b, s, E)
        gate = jax.nn.silu(x @ Wgate)
        return out * gate @ Wout

    def _L0_attn_b_ref(x, W_qkv, W_q_lsr, W_k_lsr, lsr_core, W_o):
        import jax, jax.numpy as jnp
        import numpy as np
        B, T, D = (2, 256, 128)
        H, RANK = (16, 32)
        DH = D // H
        b, t, d = x.shape
        qkv = x @ W_qkv
        q, k, v = jnp.split(qkv, 3, axis=-1)
        q = q.reshape(b, t, H, DH).transpose(0, 2, 1, 3)
        k = k.reshape(b, t, H, DH).transpose(0, 2, 1, 3)
        v = v.reshape(b, t, H, DH).transpose(0, 2, 1, 3)
        ql = jnp.einsum('bhtd,hdr->bhtr', q, W_q_lsr)
        kl = jnp.einsum('bhsd,hdr->bhsr', k, W_k_lsr)
        scale = 1.0 / jnp.sqrt(jnp.asarray(RANK, dtype=x.dtype))
        scores = jnp.einsum('bhtr,bhsr->bhts', ql * lsr_core[None, :, None, :], kl) * scale
        causal = jnp.tril(jnp.ones((t, t), dtype=bool))
        scores = jnp.where(causal[None, None], scores, jnp.asarray(-jnp.inf, dtype=scores.dtype))
        attn = jax.nn.softmax(scores, axis=-1)
        y = jnp.einsum('bhts,bhsd->bhtd', attn, v)
        y = y.transpose(0, 2, 1, 3).reshape(b, t, d)
        return y @ W_o

    def _L0_ffn_ref(x, Wg, W1, b1, W2, b2):
        import jax, jax.numpy as jnp
        import numpy as np
        D_MODEL, D_FF, N_EXPERTS, TOP_K = (128, 512, 8, 2)
        B = x.shape[:-1]
        xs = x.reshape(-1, x.shape[-1])
        T = xs.shape[0]
        gate_logits = xs @ Wg
        weights, sel = jax.lax.top_k(gate_logits, TOP_K)
        weights = jax.nn.softmax(weights.astype(jnp.float32), axis=1).astype(x.dtype)
        h = jax.nn.relu(jnp.einsum('td,edf->etf', xs, W1) + b1[:, None, :])
        out_e = jnp.einsum('etf,efd->etd', h, W2) + b2[:, None, :]
        tok = jnp.arange(T)
        picked = out_e[sel, tok[:, None]]
        out = jnp.einsum('tk,tkd->td', weights, picked)
        return out.reshape(*B, x.shape[-1])
    x = L0_attn_a_x
    x = x + _L0_attn_a_ref(_layernorm(x, axis=-1), L0_attn_a_Wq, L0_attn_a_Wk, L0_attn_a_Wv, L0_attn_a_Walpha, L0_attn_a_Wbeta, L0_attn_a_A_log, L0_attn_a_dt_bias, L0_attn_a_Wgate, L0_attn_a_Wout, L0_attn_a_rms_w)
    x = x + _L0_ffn_ref(_layernorm(x, axis=-1), L0_ffn_Wg, L0_ffn_W1, L0_ffn_b1, L0_ffn_W2, L0_ffn_b2)
    x = x + _L0_attn_b_ref(_layernorm(x, axis=-1), L0_attn_b_W_qkv, L0_attn_b_W_q_lsr, L0_attn_b_W_k_lsr, L0_attn_b_lsr_core, L0_attn_b_W_o)
    x = x + _L0_ffn_ref(_layernorm(x, axis=-1), L0_ffn_Wg, L0_ffn_W1, L0_ffn_b1, L0_ffn_W2, L0_ffn_b2)
    return x

_drawn_inputs = setup_inputs


def setup_inputs(seed=0):
    import zlib

    import numpy as np

    out = dict(_drawn_inputs(seed))
    spreads = {'L0_attn_a_dt_bias': (0.0, 2.0),
     'L0_attn_a_rms_w': (1.0, 0.6),
     'L0_attn_b_lsr_core': (1.0, 0.2),
     'L0_ffn_b1': (0.0, 0.1),
     'L0_ffn_b2': (0.0, 0.1)}
    factors = {'L0_attn_a_Walpha': 35.827, 'L0_attn_a_Wbeta': 29.868, 'L0_attn_a_A_log': 11.636}
    for name, (base, spread) in spreads.items():
        noise = np.random.default_rng([zlib.crc32(name.encode()), seed]).standard_normal(out[name].shape)
        drawn = base * np.exp(spread * noise) if base else spread * noise
        out[name] = jnp.asarray(drawn.astype(out[name].dtype))
    for name, factor in factors.items():
        out[name] = (out[name] * factor).astype(out[name].dtype)
    return out
```

```python
import math
from contextlib import ExitStack

import concourse.bass as bass
from concourse import mybir

F32 = mybir.dt.float32
F16 = mybir.dt.float16
BF16 = mybir.dt.bfloat16
ALU = mybir.AluOpType
ACT = mybir.ActivationFunctionType
AX_X = mybir.AxisListType.X

P = 128
E = 128
H = 16
D = E // H
B = 32
T = 256
HG = 4
HL = H // HG
TC = 16
NC = T // TC
Q = 4
W = TC * B
SD = HL * D * D
LN_EPS = 1e-5
RMS_EPS = 1e-6
LOG_SHIFT = 20

PREP_SLOT = dict(
    stats0=0, stats1=1, stats2=2, stats3=3, aggr0=4, aggr1=5, aggr2=6, aggr3=7, xn0=12, xn1=13, xn2=14, xn3=15,
    v_scan=27, gate_log=31, k_clamp=29, q_clamp=33, ab_scan=37, z=38, minus_z=39, minus_abs_z=40, k_unit=36,
    k_scan=42, q_unit=43, q_scan=44, beta_den=45, minus_beta=46, z_pos=41, u_plus_2=47,
    u_rec=48, s=49, s2=50, h15=51, h13=52, h11=53, h9=54, h7=55, h5=56, h3=57, log1p=58, dt=59, decay_log=60)
PREP = sorted(PREP_SLOT, key=PREP_SLOT.get)
POST = ["o_rows"]
POST_SLOT = dict(o_rows=17)
PREP_ACT_STEP = dict(rstd_log=1, rstd=2, xT=3, k_sq=4, q_sq=5, v_rows=5, gate_abs=6, gate_exp=6, gate_ln=7,
                     k_log=8, k_rinv=8, gate_sig=9, gate_rows=9, q_log=10, q_rinv=10, beta_exp=11, u=11, alpha=15)
PREP_ACT = list(PREP_ACT_STEP)
POST_ACT_STEP = dict(o_sq=5, o_log=7, o_rinv=7, x1=13)
POST_ACT = list(POST_ACT_STEP)
PREP_POOL_STEP = dict(gate=10, beta_v=12, minus_alpha_beta=15, k_scaled=15)
PREP_POOL = list(PREP_POOL_STEP)
POST_POOL_STEP = dict(o_unit=8, o_gated=9)
POST_POOL = list(POST_POOL_STEP)
PREP_PE = ["xT", "k", "q", "v", "g", "k_norm", "q_norm", "ab"]
POST_PE = ["o_sum", "o_norm", "out"]


class Semaphores:

    def __init__(self, nc):
        self.nc, self.stack, self.all = nc, ExitStack(), []

    def get(self, name):
        self.all.append(self.stack.enter_context(self.nc.semaphore(name)))
        return self.all[-1]

    def release(self):
        with self.nc.Block() as block:
            @block.gpsimd
            def _(pool):
                for s in self.all:
                    pool.sem_clear(s)
        self.stack.close()


def setup_masks(nc, ctx, ident, head_ones):
    masks = ctx.enter_context(nc.semaphore("masks"))
    with nc.Block() as block:
        @block.gpsimd
        def _(pool):
            pool.memset(ident[:, :], 0.0).then_inc(masks, 1)
            pool.memset(head_ones[:, :], 1.0).then_inc(masks, 1)
            pool.wait_ge(masks, 2)
            pool.affine_select(out=ident[:, :], in_=ident[:, :], compare_op=ALU.not_equal, fill=1.0, base=0,
                               pattern=[[-1, P]], channel_multiplier=1).then_inc(masks, 1)
            ho = head_ones[:, :].rearrange("p (h d) -> p h d", d=D)
            pool.affine_select(out=ho, in_=ho, compare_op=ALU.is_ge, fill=0.0, base=0,
                               pattern=[[-D, H], [0, D]], channel_multiplier=1).then_inc(masks, 1)
            pool.wait_ge(masks, 4)
            pool.affine_select(out=ho, in_=ho, compare_op=ALU.is_ge, fill=0.0, base=D - 1,
                               pattern=[[D, H], [0, D]], channel_multiplier=-1).then_inc(masks, 1)


def scan(nc, ctx, A, ident, head_ones, bank):
    with ExitStack() as tmp:
        def sb(name, shape, dt=F32):
            return tmp.enter_context(nc.sbuf_tensor(name, shape, dt))

        def sem(name):
            return ctx.enter_context(nc.semaphore(name))

        ps_t, ps_k, ps_q, ps_v, ps_a, ps_g, ps_n, ps_o = bank

        eps_ln = sb("eps_ln", [P, 1])
        eps_rms = sb("eps_rms", [P, 1])
        one = sb("one", [P, 1])
        wout_rms = sb("wout_rms", [P, E])
        k_bias = sb("k_bias", [P, 1])
        q_bias = sb("q_bias", [P, 1])
        wk, wq, wv, wg, wab, wout = (sb(n, [P, E]) for n in ("wk", "wq", "wv", "wg", "wab", "wout"))
        rmsw = sb("rmsw", [P, 1])
        dt_bias = sb("dt_bias", [P, HL])
        a_log = sb("a_log", [P, HL])
        neg_a = sb("neg_a", [P, HL])

        xin = [sb(f"xin{p}", [P, Q, E]) for p in range(2)]
        xres = [sb(f"xres{p}", [P, Q, E]) for p in range(2)]
        x1 = [sb(f"x1_{p}", [P, Q, E]) for p in range(2)]
        st = sb("st", [P, Q, 6])
        mv = sb("mv", [P, Q, 2])
        lnv = sb("lnv", [P, Q])
        rstd = sb("rstd", [P, Q])
        xn = sb("xn", [P, Q, E])
        xT = sb("xT", [P, W])
        ksq, qsq, klog, qlog, krinv, qrinv, kE, qE, vE, aS = (
            sb(n, [P, W]) for n in ("ksq", "qsq", "klog", "qlog", "krinv", "qrinv", "kE", "qE", "vE", "aS"))
        vS = sb("vS", [P, W])
        kS, qS, gE = ([sb(f"{n}{p}", [P, W]) for p in range(2)] for n in ("kS", "qS", "gE"))
        gabs, gexp, gln, glog, gsig, gR = (sb(n, [P, W]) for n in ("gabs", "gexp", "gln", "glog", "gsig", "gR"))
        kabS = [sb(f"kabS{p}", [P, W]) for p in range(2)]
        (z, nz, nab, u, u2, urec, s1, s2, poly, zp, dtt, dlog, eb, eb1, mbeta) = (
            sb(n, [P, TC, HL]) for n in ("z", "nz", "nab", "u", "u2", "urec", "s1", "s2", "poly", "zp", "dtt",
                                         "dlog", "eb", "eb1", "mbeta"))
        polyb = sb("polyb", [P, TC, HL])
        alpha, mab = ([sb(f"{n}{p}", [P, TC, HL]) for p in range(2)] for n in ("alpha", "mab"))
        states = sb("states", [P, TC, SD])
        prod = [sb(f"prod{p}", [P, TC, HL * D, D + 1]) for p in range(2)]
        delta = sb("delta", [P, HL * D])
        outer = sb("outer", [P, SD])
        decayed = sb("decayed", [P, SD])
        sq = sb("sq", [P, TC, SD])
        osq = sb("osq", [P, W])
        olog, orinv, ounit, oE, og = (sb(n, [P, W]) for n in ("olog", "orinv", "ounit", "oE", "og"))

        consts = sem("consts")
        weights = sem("weights")
        neg_a_exp = sem("neg_a_exp")
        neg_a_ready = sem("neg_a_ready")
        wout_ready = sem("wout_ready")
        x_in = [sem(f"x_in{p}") for p in range(2)]
        x_res = [sem(f"x_res{p}") for p in range(2)]
        x1_out = [sem(f"x1_out{p}") for p in range(2)]
        stats_seen = sem("stats_seen")
        prep_dve, post_dve, prep_act, post_act, prep_pe, post_pe, prep_pool, post_pool = (
            sem(n) for n in ("prep_dve", "post_dve", "prep_act", "post_act", "prep_pe", "post_pe",
                             "prep_pool", "post_pool"))
        chain = sem("chain")
        state_ready = sem("state_ready")
        decay_ready = sem("decay_ready")
        sq_ready = sem("sq_ready")

        def prep_at(names, c, name):
            return c * len(names) + names.index(name) + 1

        def wait(eng, s, value):
            if not (isinstance(value, int) and value <= 0):
                eng.wait_ge(s, value)

        def run_chunks(eng, chunk):
            for p in range(2):
                chunk(0, p)
            with eng.Fori(1, NC // 2 - 1) as i:
                for p in range(2):
                    chunk(i, p)
            for p in range(2):
                chunk(NC // 2 - 1, p)

        def ahead(i, p):
            if isinstance(i, int) and i == NC // 2 - 1 and p:
                return None
            return (i, 1) if p == 0 else (i + 1, 0)

        def behind(i, p):
            if isinstance(i, int) and i == 0 and p == 0:
                return None
            return (i - 1, 1) if p == 0 else (i, 0)

        xc = A["x"].rearrange("b (c q l) e -> c l b q e", q=Q, l=4)
        x1c = A["x1"].rearrange("b (c q l) e -> c l b q e", q=Q, l=4)

        block = tmp.enter_context(nc.Block())

        @block.sync
        def _(sp):
            for dst, src in ((wk, "Wk"), (wq, "Wq"), (wv, "Wv"), (wg, "Wgate"), (wout, "Wout")):
                sp.dma_start(dst[:, :], A[src]).then_inc(weights, 16)
            for hh in range(H):
                sp.dma_start(rmsw[D * hh:D * hh + D, :], A["rms_w"].rearrange("(p o) -> p o", o=1)).then_inc(weights, 16)
            for g in range(HG):
                sp.dma_start(dt_bias[32 * g:32 * g + 32, :],
                             A["dt_bias"][HL * g:HL * g + HL].partition_broadcast(32)).then_inc(weights, 16)
                sp.dma_start(a_log[32 * g:32 * g + 32, :],
                             A["A_log"][HL * g:HL * g + HL].partition_broadcast(32)).then_inc(weights, 16)
            sp.wait_ge(consts, 1)
            wabv = wab[:, :].rearrange("p (g r) -> p g r", g=HG)
            sp.dma_start(wabv[:, :, 0:HL], A["Walpha"].rearrange("e (g r) -> e g r", g=HG)).then_inc(weights, 16)
            sp.dma_start(wabv[:, :, HL:2 * HL], A["Wbeta"].rearrange("e (g r) -> e g r", g=HG)).then_inc(weights, 16)

            def load(i, p):
                c = 2 * i + p
                wait(sp, prep_dve, prep_at(PREP, c - 2, "xn3") if not (isinstance(c, int) and c < 2) else 0)
                for l in range(4):
                    sp.dma_start(xin[p][32 * l:32 * l + 32, :, :], xc[c, l]).then_inc(x_in[p], 16)

            def load_res(i, p):
                c = 2 * i + p
                wait(sp, post_pe, prep_at(POST_PE, c - 2, "out") if not (isinstance(c, int) and c < 2) else 0)
                for l in range(4):
                    sp.dma_start(xres[p][32 * l:32 * l + 32, :, :], xc[c, l]).then_inc(x_res[p], 16)

            def store(i, p):
                c = 2 * i + p
                sp.wait_ge(post_act, prep_at(POST_ACT, c, "x1"))
                for l in range(4):
                    sp.dma_start(x1c[c, l], x1[p][32 * l:32 * l + 32, :, :]).then_inc(x1_out[p], 16)

            load(0, 0)

            def chunk(i, p):
                if ahead(i, p):
                    load(*ahead(i, p))
                load_res(i, p)
                if behind(i, p):
                    store(*behind(i, p))

            run_chunks(sp, chunk)
            store(NC // 2 - 1, 1)
            for p in range(2):
                sp.wait_ge(x1_out[p], 64 * (NC // 2))

        @block.gpsimd
        def _(pool):
            pool.memset(wab[:, :], 0.0).then_inc(consts, 1)
            pool.memset(eps_ln[:, :], LN_EPS).then_inc(consts, 1)
            pool.memset(eps_rms[:, :], RMS_EPS).then_inc(consts, 1)
            pool.memset(one[:, :], 1.0).then_inc(consts, 1)
            pool.memset(k_bias[:, :], 0.5 * LOG_SHIFT * math.log(2.0)).then_inc(consts, 1)
            pool.memset(q_bias[:, :], 0.5 * LOG_SHIFT * math.log(2.0) - 0.5 * math.log(D)).then_inc(consts, 1)
            pool.memset(states[:, TC - 1, :], 0.0).then_inc(consts, 1)
            def prep(name, i, p):
                c = 2 * i + p
                g = nc.gpsimd
                if name == "gate":
                    pool.wait_ge(prep_act, prep_at(PREP_ACT, c, "gate_rows"))
                    if not (isinstance(c, int) and c < 2):
                        pool.wait_ge(post_pool, prep_at(POST_POOL, c - 2, "o_gated"))
                    ins = g.tensor_tensor(gE[p][:, :], gR[:, :], gsig[:, :], ALU.mult)
                elif name == "beta_v":
                    pool.wait_ge(prep_dve, prep_at(PREP, c, "minus_beta"))
                    ins = g.tensor_tensor(prod[p][:, :, :, D].rearrange("p t (h i) -> p (t h) i", i=D),
                                          vS[:, :].rearrange("p (th i) -> p th i", i=D),
                                          mbeta[:, :, :].rearrange("p t h -> p (t h)").unsqueeze(2)
                                          .to_broadcast([P, TC * HL, D]), ALU.mult)
                elif name == "minus_alpha_beta":
                    pool.wait_ge(prep_act, prep_at(PREP_ACT, c, "alpha"))
                    ins = g.tensor_tensor(mab[p][:, :, :], alpha[p][:, :, :], mbeta[:, :, :], ALU.mult)
                else:
                    pool.wait_ge(prep_pool, prep_at(PREP_POOL, c, "minus_alpha_beta"))
                    ins = g.tensor_tensor(kabS[p][:, :].rearrange("p (th i) -> p th i", i=D),
                                          kS[p][:, :].rearrange("p (th i) -> p th i", i=D),
                                          mab[p][:, :, :].rearrange("p t h -> p (t h)").unsqueeze(2)
                                          .to_broadcast([P, TC * HL, D]), ALU.mult)
                ins.then_inc(prep_pool, 1)

            def post(name, i, p):
                c = 2 * i + p
                if name == "o_unit":
                    pool.wait_ge(post_act, prep_at(POST_ACT, c, "o_rinv"))
                    ins = nc.gpsimd.tensor_tensor(ounit[:, :], oE[:, :], orinv[:, :], ALU.mult)
                else:
                    pool.wait_ge(post_pool, prep_at(POST_POOL, c, "o_unit"))
                    if not (isinstance(c, int) and c == 0):
                        pool.wait_ge(post_pe, prep_at(POST_PE, c - 1, "out"))
                    ins = nc.gpsimd.tensor_tensor(og[:, :], ounit[:, :], gE[p][:, :], ALU.mult)
                ins.then_inc(post_pool, 1)

            for name in PREP_POOL:
                prep(name, 0, 0)

            def chunk(i, p):
                c = 2 * i + p
                for t in range(TC):
                    pool.wait_ge(state_ready, c * TC + t + 1)
                    if t == 0:
                        pool.wait_ge(prep_dve, prep_at(PREP, c, "q_scan"))
                        if behind(i, p):
                            pool.wait_ge(post_pe, prep_at(POST_PE, c - 1, "o_sum"))
                    qb = qS[p][:, 32 * t:32 * t + 32].rearrange("p (h j) -> p h j", h=HL).unsqueeze(2)
                    nc.gpsimd.tensor_tensor(
                        sq[:, t, :].rearrange("p (h i j) -> p h i j", h=HL, i=D),
                        states[:, t, :].rearrange("p (h i j) -> p h i j", h=HL, i=D),
                        qb.to_broadcast([P, HL, D, D]), ALU.mult).then_inc(sq_ready, 1)
                    if behind(i, p):
                        for name in POST_POOL:
                            if POST_POOL_STEP[name] == t:
                                post(name, *behind(i, p))
                    if ahead(i, p):
                        for name in PREP_POOL:
                            if PREP_POOL_STEP[name] == t:
                                prep(name, *ahead(i, p))

            run_chunks(pool, chunk)
            for name in POST_POOL:
                post(name, NC // 2 - 1, 1)

        @block.tensor
        def _(pe):
            pe.wait_ge(weights, 16 * (5 + H + 2 * HG + 2))

            def prep(i, p):
                c = 2 * i + p
                pe.wait_ge(prep_dve, prep_at(PREP, c, "xn3"))
                for q in range(Q):
                    ins = nc.tensor.transpose(ps_t[:, P * q:P * q + P], xn[:, q, :], ident[:, :])
                ins.then_inc(prep_pe, 1)
                pe.wait_ge(prep_act, prep_at(PREP_ACT, c, "xT"))
                for w, ps in ((wk, ps_k), (wq, ps_q), (wv, ps_v), (wg, ps_g)):
                    nc.tensor.matmul(ps[:, :], w[:, :], xT[:, :], start=True, stop=True).then_inc(prep_pe, 1)

            def norms(i, p):
                c = 2 * i + p
                pe.wait_ge(prep_act, prep_at(PREP_ACT, c, "k_sq"))
                nc.tensor.matmul(ps_n[:, :], head_ones[:, :], ksq[:, :], start=True, stop=True).then_inc(prep_pe, 1)
                pe.wait_ge(prep_act, prep_at(PREP_ACT, c, "q_sq"))
                nc.tensor.matmul(ps_t[:, :], head_ones[:, :], qsq[:, :], start=True, stop=True).then_inc(prep_pe, 1)

            def prep_ab(i, p):
                c = 2 * i + p
                nc.tensor.matmul(ps_a[:, :], wab[:, :], xT[:, :], start=True, stop=True).then_inc(prep_pe, 1)

            def o_sum(i, p):
                c = 2 * i + p
                pe.wait_ge(sq_ready, (c + 1) * TC)
                pe.wait_ge(prep_dve, prep_at(PREP, c, "ab_scan"))
                sv = sq[:, :, :].rearrange("p t (hi j) -> p (t hi) j", j=D)
                for j in range(D):
                    ins = nc.tensor.matmul(ps_a[:, :], ident[:, :], sv[:, :, j], start=(j == 0), stop=(j == D - 1))
                ins.then_inc(post_pe, 1)

            def o_norm(i, p):
                c = 2 * i + p
                pe.wait_ge(post_act, prep_at(POST_ACT, c, "o_sq"))
                nc.tensor.matmul(ps_a[:, :], head_ones[:, :], osq[:, :], start=True, stop=True).then_inc(post_pe, 1)

            def out_proj(i, p):
                c = 2 * i + p
                pe.wait_ge(post_pool, prep_at(POST_POOL, c, "o_gated"))
                pe.wait_ge(x_res[p], 64 * (i + 1))
                if not (isinstance(c, int) and c == 0):
                    pe.wait_ge(post_act, prep_at(POST_ACT, c - 1, "x1"))
                nc.tensor.matmul(ps_o[:, :], ident[:, :], xres[p][:, :, :].rearrange("p q e -> p (q e)"),
                                 start=True, stop=False)
                for q in range(Q):
                    ins = nc.tensor.matmul(ps_o[:, P * q:P * q + P], og[:, P * q:P * q + P], wout_rms[:, :],
                                           start=False, stop=(q == Q - 1))
                ins.then_inc(post_pe, 1)

            pe.wait_ge(wout_ready, 1)
            prep(0, 0)
            norms(0, 0)
            prep_ab(0, 0)

            def chunk(i, p):
                if behind(i, p):
                    o_sum(*behind(i, p))
                if ahead(i, p):
                    prep(*ahead(i, p))
                if behind(i, p):
                    o_norm(*behind(i, p))
                if ahead(i, p):
                    norms(*ahead(i, p))
                if behind(i, p):
                    bi, bp = behind(i, p)
                    pe.wait_ge(post_act, prep_at(POST_ACT, 2 * bi + bp, "o_log"))
                if ahead(i, p):
                    prep_ab(*ahead(i, p))
                if behind(i, p):
                    out_proj(*behind(i, p))

            run_chunks(pe, chunk)
            o_sum(NC // 2 - 1, 1)
            o_norm(NC // 2 - 1, 1)
            out_proj(NC // 2 - 1, 1)

        @block.scalar
        def _(act):
            act.wait_ge(consts, 7)
            act.wait_ge(weights, 16 * (5 + H + 2 * HG + 2))
            nc.scalar.preload_act_table_set("natural_log_exp_and_others")
            nc.scalar.activation(neg_a[:, :], a_log[:, :], ACT.Exp).then_inc(neg_a_exp, 1)

            def prep(name, i, p):
                c = 2 * i + p

                def need(s, names, what):
                    act.wait_ge(s, prep_at(names, c, what))

                if name == "rstd_log":
                    need(prep_dve, PREP, "aggr3")
                    ins = nc.scalar.activation(lnv[:, :], mv[:, :, 1], ACT.Ln, bias=eps_ln[:, :])
                elif name == "rstd":
                    need(prep_act, PREP_ACT, "rstd_log")
                    ins = nc.scalar.activation(rstd[:, :], lnv[:, :], ACT.Exp, scale=-0.5)
                elif name == "xT":
                    need(prep_pe, PREP_PE, "xT")
                    ins = nc.scalar.activation(xT[:, :], ps_t[:, :], ACT.Copy)
                elif name == "k_sq":
                    need(prep_pe, PREP_PE, "k")
                    ins = nc.scalar.activation(ksq[:, :], ps_k[:, :], ACT.Square)
                elif name == "q_sq":
                    need(prep_pe, PREP_PE, "q")
                    ins = nc.scalar.activation(qsq[:, :], ps_q[:, :], ACT.Square)
                elif name == "v_rows":
                    need(prep_pe, PREP_PE, "v")
                    ins = nc.scalar.activation(vE[:, :], ps_v[:, :], ACT.Copy, scale=-1.0)
                elif name == "gate_abs":
                    need(prep_pe, PREP_PE, "g")
                    ins = nc.scalar.activation(gabs[:, :], ps_g[:, :], ACT.Abs)
                elif name == "gate_exp":
                    need(prep_act, PREP_ACT, "gate_abs")
                    ins = nc.scalar.activation(gexp[:, :], gabs[:, :], ACT.Exp, scale=-1.0)
                elif name == "gate_ln":
                    need(prep_act, PREP_ACT, "gate_exp")
                    ins = nc.scalar.activation(gln[:, :], gexp[:, :], ACT.Ln, bias=one[:, :])
                elif name == "gate_sig":
                    need(prep_dve, PREP, "gate_log")
                    ins = nc.scalar.activation(gsig[:, :], glog[:, :], ACT.Exp)
                elif name == "gate_rows":
                    ins = nc.scalar.activation(gR[:, :], ps_g[:, :], ACT.Copy)
                elif name in ("k_log", "q_log"):
                    need(prep_dve, PREP, name[0] + "_clamp")
                    src, dst = (ksq, klog) if name[0] == "k" else (qsq, qlog)
                    ins = nc.scalar.activation(dst[:, :], src[:, :], ACT.Ln, scale=float(2 ** LOG_SHIFT))
                elif name in ("k_rinv", "q_rinv"):
                    need(prep_act, PREP_ACT, name[0] + "_log")
                    src, dst, bias = (klog, krinv, k_bias) if name[0] == "k" else (qlog, qrinv, q_bias)
                    ins = nc.scalar.activation(dst[:, :], src[:, :], ACT.Exp, scale=-0.5, bias=bias[:, :])
                elif name == "u":
                    need(prep_dve, PREP, "minus_abs_z")
                    ins = nc.scalar.activation(u[:, :, :], nab[:, :, :], ACT.Exp)
                elif name == "beta_exp":
                    need(prep_dve, PREP, "ab_scan")
                    zb = aS[:, :].rearrange("p (t r) -> p t r", t=TC)[:, :, HL:2 * HL]
                    ins = nc.scalar.activation(eb[:, :, :], zb, ACT.Exp, scale=-1.0)
                elif name == "alpha":
                    need(prep_dve, PREP, "decay_log")
                    ins = nc.scalar.activation(alpha[p][:, :, :], dlog[:, :, :], ACT.Exp)
                ins.then_inc(prep_act, 1)

            def post(name, i, p):
                c = 2 * i + p
                if name == "o_sq":
                    act.wait_ge(post_dve, prep_at(POST, c, "o_rows"))
                    ins = nc.scalar.activation(osq[:, :], oE[:, :], ACT.Square)
                elif name == "o_log":
                    act.wait_ge(post_pe, prep_at(POST_PE, c, "o_norm"))
                    ins = nc.scalar.activation(olog[:, :], ps_a[:, :], ACT.Ln, scale=1.0 / D, bias=eps_rms[:, :])
                elif name == "x1":
                    act.wait_ge(post_pe, prep_at(POST_PE, c, "out"))
                    if not (isinstance(c, int) and c < 2):
                        act.wait_ge(x1_out[p], 64 * i)
                    ins = nc.scalar.activation(x1[p][:, :, :].rearrange("p q e -> p (q e)"), ps_o[:, :], ACT.Copy)
                else:
                    act.wait_ge(post_act, prep_at(POST_ACT, c, "o_log"))
                    ins = nc.scalar.activation(orinv[:, :], olog[:, :], ACT.Exp, scale=-0.5)
                ins.then_inc(post_act, 1)

            for name in PREP_ACT:
                prep(name, 0, 0)

            def chunk(i, p):
                c = 2 * i + p
                for t in range(TC):
                    wait(act, state_ready, c * TC + t)
                    if t == 0:
                        act.wait_ge(prep_act, prep_at(PREP_ACT, c, "alpha"))
                    for h in range(HL):
                        ins = nc.scalar.activation(decayed[:, 64 * h:64 * h + 64],
                                                   states[:, (t - 1) % TC, 64 * h:64 * h + 64],
                                                   ACT.Copy, scale=alpha[p][:, t, h:h + 1])
                    ins.then_inc(decay_ready, 1)
                    if behind(i, p):
                        for name in POST_ACT:
                            if POST_ACT_STEP[name] == t:
                                post(name, *behind(i, p))
                    if ahead(i, p):
                        for name in PREP_ACT:
                            if PREP_ACT_STEP[name] == t:
                                prep(name, *ahead(i, p))

            run_chunks(act, chunk)
            for name in POST_ACT:
                post(name, NC // 2 - 1, 1)

        @block.vector
        def _(dve):
            dve.wait_ge(consts, 7)
            dve.wait_ge(weights, 16 * (5 + H + 2 * HG + 2))
            dve.wait_ge(neg_a_exp, 1)
            nc.vector.tensor_scalar(neg_a[:, :], neg_a[:, :], -1.0, None, ALU.mult).then_inc(neg_a_ready, 1)
            nc.vector.tensor_scalar(wout_rms[:, :], wout[:, :], rmsw[:, 0:1], None, ALU.mult).then_inc(wout_ready, 1)
            dve.wait_ge(neg_a_ready, 1)

            def prep(name, i, p):
                c = 2 * i + p

                def need(what):
                    dve.wait_ge(prep_dve, prep_at(PREP, c, what))

                def act_did(what):
                    dve.wait_ge(prep_act, prep_at(PREP_ACT, c, what))

                def pe_did(what):
                    dve.wait_ge(prep_pe, prep_at(PREP_PE, c, what))

                aview = aS[:, :].rearrange("p (t r) -> p t r", t=TC)

                def hl(x):
                    return x.unsqueeze(1).to_broadcast([P, TC, HL])

                v = nc.vector
                if name.startswith("stats"):
                    q = int(name[5:])
                    if q == 0:
                        dve.wait_ge(x_in[p], 64 * (i + 1))
                    ins = v.bn_stats(st[:, q, :], xin[p][:, q, :])
                elif name.startswith("aggr"):
                    q = int(name[4:])
                    need(f"stats{q}")
                    dve.sem_inc(stats_seen, 1)
                    ins = v.bn_aggr(mv[:, q, :], st[:, q, :])
                elif name.startswith("xn"):
                    q = int(name[2:])
                    act_did("rstd")
                    ins = v.tensor_scalar(xn[:, q, :], xin[p][:, q, :], mv[:, q, 0:1], rstd[:, q:q + 1],
                                          ALU.subtract, ALU.mult)
                elif name == "v_scan":
                    act_did("v_rows")
                    ins = v.transpose(vS[:, :], vE[:, :])
                elif name == "k_clamp":
                    pe_did("k_norm")
                    ins = v.tensor_scalar(ksq[:, :], ps_n[:, :], 1e-24, None, ALU.max)
                elif name == "q_clamp":
                    pe_did("q_norm")
                    ins = v.tensor_scalar(qsq[:, :], ps_t[:, :], 1e-24, None, ALU.max)
                elif name == "ab_scan":
                    pe_did("ab")
                    ins = v.transpose(aS[:, :], ps_a[:, :])
                elif name == "z":
                    need("ab_scan")
                    ins = v.tensor_tensor(z[:, :, :], aview[:, :, 0:HL], hl(dt_bias[:, :]), ALU.add)
                elif name == "minus_z":
                    need("z")
                    ins = v.tensor_scalar(nz[:, :, :], z[:, :, :], -1.0, None, ALU.mult)
                elif name == "minus_abs_z":
                    need("minus_z")
                    ins = v.tensor_tensor(nab[:, :, :], z[:, :, :], nz[:, :, :], ALU.min)
                elif name == "k_unit":
                    act_did("k_rinv")
                    ins = v.tensor_tensor(kE[:, :], ps_k[:, :], krinv[:, :], ALU.mult)
                elif name == "k_scan":
                    need("k_unit")
                    ins = v.transpose(kS[p][:, :], kE[:, :])
                elif name == "q_unit":
                    act_did("q_rinv")
                    ins = v.tensor_tensor(qE[:, :], ps_q[:, :], qrinv[:, :], ALU.mult)
                elif name == "q_scan":
                    need("q_unit")
                    if not (isinstance(c, int) and c < 2):
                        dve.wait_ge(sq_ready, (c - 1) * TC)
                    ins = v.transpose(qS[p][:, :], qE[:, :])
                elif name == "gate_log":
                    act_did("gate_ln")
                    ins = v.scalar_tensor_tensor(glog[:, :], ps_g[:, :], 0.0, gln[:, :], ALU.min, ALU.subtract)
                elif name == "beta_den":
                    act_did("beta_exp")
                    ins = v.tensor_scalar(eb1[:, :, :], eb[:, :, :], -1.0, -1.0, ALU.mult, ALU.add)
                elif name == "minus_beta":
                    need("beta_den")
                    ins = v.reciprocal(mbeta[:, :, :], eb1[:, :, :])
                elif name == "z_pos":
                    ins = v.tensor_scalar(zp[:, :, :], z[:, :, :], 0.0, None, ALU.max)
                elif name == "u_plus_2":
                    act_did("u")
                    ins = v.tensor_scalar(u2[:, :, :], u[:, :, :], 2.0, None, ALU.add)
                elif name == "u_rec":
                    need("u_plus_2")
                    ins = v.reciprocal(urec[:, :, :], u2[:, :, :])
                elif name == "s":
                    need("u_rec")
                    ins = v.tensor_tensor(s1[:, :, :], u[:, :, :], urec[:, :, :], ALU.mult)
                elif name == "s2":
                    need("s")
                    ins = v.tensor_tensor(s2[:, :, :], s1[:, :, :], s1[:, :, :], ALU.mult)
                elif name == "h15":
                    need("s2")
                    ins = v.tensor_scalar(poly[:, :, :], s2[:, :, :], 1.0 / 15, None, ALU.mult)
                elif name[0] == "h" and name[1:].isdigit():
                    n = int(name[1:])
                    need(f"h{n + 2}")
                    a, b = (poly, polyb) if (n // 2) % 2 == 0 else (polyb, poly)
                    ins = v.scalar_tensor_tensor(b[:, :, :], a[:, :, :], 1.0 / n, s2[:, :, :], ALU.add, ALU.mult)
                elif name == "log1p":
                    need("h3")
                    ins = v.scalar_tensor_tensor(poly[:, :, :], poly[:, :, :], 1.0, s1[:, :, :], ALU.add, ALU.mult)
                elif name == "dt":
                    need("log1p")
                    ins = v.scalar_tensor_tensor(dtt[:, :, :], poly[:, :, :], 2.0, zp[:, :, :], ALU.mult, ALU.add)
                elif name == "decay_log":
                    need("dt")
                    ins = v.tensor_tensor(dlog[:, :, :], dtt[:, :, :], hl(neg_a[:, :]), ALU.mult)
                ins.then_inc(prep_dve, 1)

            def post(name, i, p):
                c = 2 * i + p
                dve.wait_ge(post_pe, prep_at(POST_PE, c, "o_sum"))
                nc.vector.transpose(oE[:, :], ps_a[:, :]).then_inc(post_dve, 1)

            for name in PREP:
                prep(name, 0, 0)

            LINKS = 3

            def chunk(i, p):
                c = 2 * i + p

                def side(slot):
                    if behind(i, p):
                        for name in POST:
                            if POST_SLOT[name] == slot:
                                post(name, *behind(i, p))
                    if ahead(i, p):
                        for name in PREP:
                            if PREP_SLOT[name] == slot:
                                prep(name, *ahead(i, p))

                v = nc.vector
                for t in range(TC):
                    prev = states[:, (t - 1) % TC, :]
                    base = (c * TC + t) * LINKS
                    kt = kS[p][:, 32 * t:32 * t + 32].rearrange("p (h j) -> p h j", h=HL).unsqueeze(2) \
                        .to_broadcast([P, HL, D, D])

                    def hij(x):
                        return x.rearrange("p (h i j) -> p h i j", h=HL, i=D)

                    wait(dve, state_ready, c * TC + t)
                    if t == 0:
                        dve.wait_ge(prep_pool, prep_at(PREP_POOL, c, "k_scaled"))
                    v.tensor_tensor(prod[p][:, t, :, 0:D].rearrange("p (h i) j -> p h i j", h=HL), hij(prev),
                                    kabS[p][:, 32 * t:32 * t + 32].rearrange("p (h j) -> p h j", h=HL).unsqueeze(2)
                                    .to_broadcast([P, HL, D, D]), ALU.mult).then_inc(chain, 1)
                    side(4 * t)
                    dve.wait_ge(chain, base + 1)
                    v.tensor_reduce(delta[:, :], prod[p][:, t, :, :], AX_X, ALU.add).then_inc(chain, 1)
                    side(4 * t + 1)
                    dve.wait_ge(chain, base + 2)
                    v.tensor_tensor(hij(outer[:, :]),
                                    delta[:, :].rearrange("p (h i) -> p h i", h=HL).unsqueeze(3)
                                    .to_broadcast([P, HL, D, D]), kt, ALU.mult).then_inc(chain, 1)
                    side(4 * t + 2)
                    dve.wait_ge(chain, base + 3)
                    dve.wait_ge(decay_ready, c * TC + t + 1)
                    if behind(i, p):
                        dve.wait_ge(sq_ready, (c - 1) * TC + t + 1)
                    v.tensor_tensor(states[:, t, :], decayed[:, :], outer[:, :], ALU.add).then_inc(state_ready, 1)
                    side(4 * t + 3)

            run_chunks(dve, chunk)
            for name in POST:
                post(name, NC // 2 - 1, 1)


NX = 8
F = 512
FC = F // P
NT = B * T // P
BS = 256
BR = BS // P
NB = 2 * NT // BR + NX
NS = NB * BS
G = 8
CB = B * T // BS
SPLIT = 8.0
HSPLIT = 4.0


class Experts:

    def __init__(self, sb, sem):
        self.w1 = [sb(f"w1_{n}", [P, NX, FC, P], F16) for n in "hl"]
        self.w2 = [sb(f"w2_{n}", [P, NX, FC, P], F16) for n in "hl"]
        self.dispatched = sem("dispatched")
        self.got = [sem(f"got{g}") for g in range(G)]
        self.calls = 0
        self.wgate = sb("w_router", [P, NX])
        self.b1 = sb("b1_cols", [P, NX, FC])
        self.b2 = sb("b2_cols", [P, NX])
        self.before = sb("before", [P, P], F16)
        self.all16 = sb("all16", [P, P], F16)
        self.expert_m8 = sb("expert_m8", [P, NX])
        self.block_row = sb("block_row", [P, NB])
        self.slot_row = sb("slot_row", [P, CB])
        self.onesrow = sb("onesrow", [P, NX * NT])


def setup_experts(nc, ctx, A, X, ident, bank):
    with ExitStack() as tmp:
        def sb(name, shape, dt=F32):
            return tmp.enter_context(nc.sbuf_tensor(name, shape, dt))

        def sem(name):
            return ctx.enter_context(nc.semaphore(name))

        raw = sb("raw_w", [P, NX, F])
        iot = sb("iot", [P, NB + CB + NX], mybir.dt.int32)
        zero = sb("zero_rows", [P, NS // P // 8, P])
        raw_in = [sem("w1_in"), sem("w2_in")]
        small_in, high, low, masked, iotas, copied, zeroed, slots_zero = (
            sem(n) for n in ("small_in", "high", "low", "masked", "iotas", "copied", "zeroed", "slots_zero"))
        block = tmp.enter_context(nc.Block())

        @block.sync
        def _(sp):
            sp.dma_start(X.wgate[:, :], A["Wg"]).then_inc(small_in, 16)
            for e in range(NX):
                for c in range(FC):
                    sp.dma_start(X.b1[:, e, c:c + 1], A["b1"][e, P * c:P * c + P].rearrange("(p o) -> p o", o=1)).then_inc(small_in, 16)
                sp.dma_start(X.b2[:, e:e + 1], A["b2"][e, :].rearrange("(p o) -> p o", o=1)).then_inc(small_in, 16)
            sp.dma_start(raw[:, :, :], A["W1"].rearrange("e d f -> d e f")).then_inc(raw_in[0], 16)
            sp.wait_ge(low, 1)
            sp.dma_start(raw[:, :, :].rearrange("p e (c d) -> p e c d", c=FC),
                         A["W2"].rearrange("e (c f) d -> f e c d", c=FC)).then_inc(raw_in[1], 16)
            sp.wait_ge(zeroed, 1)
            for k in range(8):
                sp.dma_start(A["slots_in"].rearrange("(k p r) d -> k p r d", k=8, p=P)[k], zero[:, :, :]).then_inc(slots_zero, 16)
            sp.wait_ge(slots_zero, 8 * 16)

        @block.gpsimd
        def _(pool):
            pool.memset(zero[:, :, :], 0.0).then_inc(zeroed, 1)
            pool.memset(X.before[:, :], 1.0).then_inc(masked, 1)
            pool.memset(X.all16[:, :], 1.0).then_inc(masked, 1)
            pool.memset(X.onesrow[:, :], 1.0).then_inc(masked, 1)
            pool.wait_ge(masked, 3)
            pool.affine_select(out=X.before[:, :], in_=X.before[:, :], compare_op=ALU.is_gt, fill=0.0, base=0,
                               pattern=[[1, P]], channel_multiplier=-1).then_inc(masked, 1)
            pool.iota(iot[:, 0:NB], pattern=[[1, NB]], base=0, channel_multiplier=0).then_inc(iotas, 1)
            pool.iota(iot[:, NB:NB + CB], pattern=[[BS, CB]], base=0, channel_multiplier=0).then_inc(iotas, 1)
            pool.iota(iot[:, NB + CB:], pattern=[[1, NX]], base=-NX, channel_multiplier=0).then_inc(iotas, 1)

        @block.scalar
        def _(act):
            for k, w in enumerate((X.w1, X.w2)):
                act.wait_ge(raw_in[k], 16)
                nc.scalar.activation(w[0][:, :, :, :].rearrange("p e c d -> p (e c d)"),
                                     raw[:, :, :].rearrange("p e f -> p (e f)"), ACT.Copy,
                                     scale=2.0 ** SPLIT).then_inc(high, 1)

        @block.vector
        def _(dve):
            dve.wait_ge(iotas, 3)
            nc.vector.tensor_copy(X.block_row[:, :], iot[:, 0:NB]).then_inc(copied, 1)
            nc.vector.tensor_copy(X.slot_row[:, :], iot[:, NB:NB + CB]).then_inc(copied, 1)
            nc.vector.tensor_copy(X.expert_m8[:, :], iot[:, NB + CB:]).then_inc(copied, 1)
            dve.wait_ge(small_in, 16 * (1 + NX * (FC + 1)))
            nc.vector.tensor_scalar(X.b1[:, :, :], X.b1[:, :, :], 2.0 ** HSPLIT, None, ALU.mult).then_inc(copied, 1)
            for k, w in enumerate((X.w1, X.w2)):
                dve.wait_ge(high, k + 1)
                nc.vector.scalar_tensor_tensor(w[1][:, :, :, :].rearrange("p e c d -> p (e c d)"),
                                               raw[:, :, :].rearrange("p e f -> p (e f)"), 2.0 ** SPLIT,
                                               w[0][:, :, :, :].rearrange("p e c d -> p (e c d)"),
                                               ALU.mult, ALU.subtract).then_inc(low, 1)
            dve.wait_ge(low, 2)


ROUTE = ["m1", "eq1", "cand1", "i1", "O1", "L2", "m2", "eq2", "cand2", "i2", "O2", "d", "mask", "tot", "cum", "excl",
         "base", "cend", "cnt", "over", "nb", "bend", "bstart", "adj", "slot", "p1", "pos1", "p2", "pos2", "posi",
         "past", "blk", "blki", "den", "w1", "w2"]


def ffn(nc, ctx, A, X, ident, bank, name, src, dst):
    with ExitStack() as tmp:
        def sb(n, shape, dt=F32):
            return tmp.enter_context(nc.sbuf_tensor(f"{name}_{n}", shape, dt))

        def sem(n):
            return own.get(f"{name}_{n}")

        own = Semaphores(nc)

        x_all = sb("x_all", [P, NT, E])
        xn_all = sb("xn_all", [P, NT, E])
        xn = [sb(f"xn{p}", [P, Q, E]) for p in range(2)]
        eps = sb("eps", [P, 1])
        st = sb("st", [P, Q, 6])
        mv = sb("mv", [P, Q, 2])
        lnv = sb("lnv", [P, Q])
        rstd = sb("rstd", [P, Q])
        xT = [sb(f"xT{p}", [P, W]) for p in range(2)]
        L, eq, cand, O1, O2, L2, base, prod, cum, tot = (sb(n, [P, NT, NX]) for n in
                                                         ("L", "eq", "cand", "O1", "O2", "L2", "base", "prod", "cum", "tot"))
        m1, m2, i1, i2, d, ex, den, g1, g2, p1, p2 = (sb(n, [P, NT]) for n in
                                                      ("m1", "m2", "i1", "i2", "d", "ex", "den", "g1", "g2", "p1", "p2"))
        mask = sb("mask", [P, NX, NT], F16)
        ce = sb("ce", [P, NX + 1])
        cnt, nb, bend, bstart, adj = (sb(n, [P, NX]) for n in ("cnt", "nb", "bend", "bstart", "adj"))
        over = sb("over", [P, NX, CB])
        past = sb("past", [P, NB, NX])
        blk = sb("blk", [P, NB])
        posi = sb("posi", [P, 2, NT], mybir.dt.int32)
        blki = sb("blki", [P, NB], mybir.dt.int32)
        xs = [sb(f"xs{p}", [P, BR, P]) for p in range(2)]
        xh, xl = ([sb(f"{n}{p}", [P, BS], F16) for p in range(2)] for n in ("xh", "xl"))
        h32 = [sb(f"h32_{p}", [P, FC, BS]) for p in range(2)]
        hh, hl = ([sb(f"{n}{p}", [P, FC, BS], F16) for p in range(2)] for n in ("hh", "hl"))
        yT = [sb(f"yT{p}", [P, BS]) for p in range(2)]
        ys = [sb(f"ys{p}", [P, BR, P]) for p in range(2)]
        yg = sb("yg", [P, G, 2, P])
        half = sb("half", [P, G, P])

        (eps_set, aggr, rstd_s, xnr, xTp, xTr, logits, L_cp, route, ex_s, sums,
         xT_ps, x_high, x_low, h_ps, h_relu, h_high, h_low, y_ps, yT_s, yR_ps, ys_s, halved, added) = (
            sem(n) for n in ("eps_set", "aggregated", "rstd", "normed", "xT_in_psum", "xT_ready", "logits", "logits_kept",
                             "route", "exps", "sums", "block_xT", "x_high", "x_low", "h_in_psum",
                             "h_relu", "h_high", "h_low", "y_in_psum", "yT_ready", "y_rows", "ys_ready", "halved",
                             "added"))
        xn_kept = sem("xn_kept")
        stats = sem("stats")
        stats_seen = sem("stats_seen")
        x_in, xs_in, ys_out = ([sem(f"{n}{p}") for p in range(2)] for n in ("x_in", "xs_in", "ys_out"))
        dispatched, got, calls = X.dispatched, X.got, X.calls
        X.calls += 1
        out_sem = [sem(f"out{g}") for g in range(G)]

        srct = src.rearrange("b t e -> (b t) e").rearrange("(g q p) e -> g p q e", q=Q, p=P)
        dstt = dst.rearrange("b t e -> (b t) e").rearrange("(n p) e -> n p e", p=P)
        slot_in = A["slots_in"].rearrange("(j r p) d -> j p r d", r=BR, p=P)
        slot_out = A["slots_out"].rearrange("(j r p) d -> j p r d", r=BR, p=P)
        NG = NT // Q
        block = tmp.enter_context(nc.Block())
        R = {n: k + 1 for k, n in enumerate(ROUTE)}

        def pairs(eng, count, step):
            for p in range(2):
                step(0, p)
            with eng.Fori(1, count // 2 - 1) as i:
                for p in range(2):
                    step(i, p)
            for p in range(2):
                step(count // 2 - 1, p)

        def early(x):
            return isinstance(x, int) and x < 2

        @block.sync
        def _(sp):
            def load(i, p):
                g = 2 * i + p
                if not early(g):
                    sp.wait_ge(xnr, g - 1)
                sp.dma_start(x_all[:, bass.ds(g * Q, Q), :], srct[g]).then_inc(x_in[p], 16)
            pairs(sp, NG, load)
            sp.wait_ge(dispatched, 2 * NT * 16 * (calls + 1))

            def fetch(i, p):
                j = 2 * i + p
                if not early(j):
                    sp.wait_ge(xT_ps, j - 1)
                sp.dma_start(xs[p][:, :, :], slot_in[j]).then_inc(xs_in[p], 16)

            def keep(i, p):
                j = 2 * i + p
                sp.wait_ge(ys_s, j + 1)
                sp.dma_start(slot_out[j], ys[p][:, :, :]).then_inc(ys_out[p], 16)

            fetch(0, 0)
            fetch(0, 1)

            def step(i, p):
                last = isinstance(i, int) and i == NB // 2 - 1
                if not last:
                    fetch(i + 1, p)
                if not (isinstance(i, int) and i == 0):
                    keep(i - 1, p)
            pairs(sp, NB, step)
            keep(NB // 2 - 1, 0)
            keep(NB // 2 - 1, 1)
            for t in range(NT):
                sp.wait_ge(added, t + 1)
                sp.dma_start(dstt[t], half[:, t % G, :]).then_inc(out_sem[t % G], 16)
            for g in range(G):
                sp.wait_ge(out_sem[g], 16 * (NT // G))

        @block.gpsimd
        def _(pool):
            pool.memset(eps[:, :], LN_EPS).then_inc(eps_set, 1)
            pool.memset(ce[:, 0:1], 0.0).then_inc(eps_set, 1)

            def keep(i, p):
                g = 2 * i + p
                pool.wait_ge(xnr, g + 1)
                nc.gpsimd.tensor_copy(xn_all[:, bass.ds(g * Q, Q), :], xn[p][:, :, :]).then_inc(xn_kept, 1)
            pairs(pool, NG, keep)
            pool.wait_ge(xn_kept, NG)
            pool.wait_ge(route, R["posi"])
            for t in range(NT):
                for k in range(2):
                    pool.indirect_dma_start(A["slots_in"], bass.IndirectOffsetOnAxis(ap=posi[:, k, t:t + 1], axis=0),
                                            xn_all[:, t, :], None).then_inc(dispatched, 16)
            for p in range(2):
                pool.wait_ge(ys_out[p], 16 * (NB // 2))
            for t in range(NT):
                if t >= G:
                    pool.wait_ge(added, t - G + 1)
                for k in range(2):
                    pool.indirect_dma_start(yg[:, t % G, k, :], None, A["slots_out"],
                                            bass.IndirectOffsetOnAxis(ap=posi[:, k, t:t + 1], axis=0)).then_inc(got[t % G], 16)

        @block.tensor
        def _(pe):
            def logits_of(i, p):
                g = 2 * i + p
                pe.wait_ge(xnr, g + 1)
                if not (isinstance(g, int) and g == 0):
                    pe.wait_ge(xTr, g)
                for q in range(Q):
                    ins = nc.tensor.transpose(bank[0][:, P * q:P * q + P], xn[p][:, q, :], ident[:, :])
                ins.then_inc(xTp, 1)
                pe.wait_ge(xTr, g + 1)
                if not early(g):
                    pe.wait_ge(L_cp, g - 1)
                for q in range(Q):
                    ins = nc.tensor.matmul(bank[1 + p][:, NX * q:NX * q + NX], xT[p][:, P * q:P * q + P], X.wgate[:, :],
                                           start=True, stop=True)
                ins.then_inc(logits, 1)
            pairs(pe, NG, logits_of)
            pe.wait_ge(route, R["mask"])
            mk = mask[:, :, :].rearrange("p e t -> p (e t)")
            nc.tensor.matmul(bank[3][:, :], X.before[:, :], mk, start=True, stop=True).then_inc(sums, 1)
            nc.tensor.matmul(bank[4][:, :], X.all16[:, :], mk, start=True, stop=True).then_inc(sums, 1)
            pe.wait_ge(route, R["blki"])
            ps_x, ps_yr = bank[0], bank[1]
            ps_h = [bank[2:4], bank[4:6]]
            ps_y = bank[6:8]

            def expert(j):
                return pe.value_load(blki[0:1, j:j + 1] if isinstance(j, int) else blki[0:1, bass.ds(j, 1)],
                                     min_val=0, max_val=NX - 1)

            def turn(i, p):
                j = 2 * i + p
                pe.wait_ge(xs_in[p], 16 * (i + 1))
                if not (isinstance(j, int) and j == 0):
                    pe.wait_ge(x_low, j)
                for r in range(BR):
                    ins = nc.tensor.transpose(ps_x[:, P * r:P * r + P], xs[p][:, r, :], ident[:, :])
                ins.then_inc(xT_ps, 1)

            def up(i, p):
                j = 2 * i + p
                e = expert(j)
                pe.wait_ge(x_low, j + 1)
                if not early(j):
                    pe.wait_ge(h_relu, FC * (j - 1))
                for c in range(FC):
                    o = ps_h[p][c // 2][:, BS * (c % 2):BS * (c % 2) + BS]
                    for n, (w, x) in enumerate(((0, xh), (0, xl), (1, xh))):
                        ins = nc.tensor.matmul(o, X.w1[w][:, bass.ds(e, 1), c, :].rearrange("p o d -> p (o d)"), x[p][:, :],
                                               start=(n == 0), stop=(n == 2))
                    ins.then_inc(h_ps, 1)

            def down(i, p):
                j = 2 * i + p
                e = expert(j)
                pe.wait_ge(h_low, j + 1)
                if not early(j):
                    pe.wait_ge(yT_s, j - 1)
                for c in range(FC):
                    for n, (w, h) in enumerate(((0, hh), (0, hl), (1, hh))):
                        ins = nc.tensor.matmul(ps_y[p][:, 0:BS], X.w2[w][:, bass.ds(e, 1), c, :].rearrange("p o d -> p (o d)"),
                                               h[p][:, c, :], start=(c == 0 and n == 0), stop=(c == FC - 1 and n == 2))
                ins.then_inc(y_ps, 1)

            def back(i, p):
                j = 2 * i + p
                pe.wait_ge(yT_s, j + 1)
                if not (isinstance(j, int) and j == 0):
                    pe.wait_ge(ys_s, j)
                for r in range(BR):
                    ins = nc.tensor.transpose(ps_yr[:, P * r:P * r + P], yT[p][:, P * r:P * r + P], ident[:, :])
                ins.then_inc(yR_ps, 1)

            turn(0, 0)

            def step(i, p):
                j = 2 * i + p
                up(i, p)
                if not (isinstance(j, int) and j == NB - 1):
                    turn(*((i, 1) if p == 0 else (i + 1, 0)))
                if not (isinstance(j, int) and j == 0):
                    down(*((i - 1, 1) if p == 0 else (i, 0)))
                if not (isinstance(j, int) and j < 2):
                    back(i - 1, p)
            pairs(pe, NB, step)
            back(NB // 2 - 1, 0)
            down(NB // 2 - 1, 1)
            back(NB // 2 - 1, 1)

        @block.scalar
        def _(act):
            nc.scalar.preload_act_table_set("natural_log_exp_and_others")
            act.wait_ge(eps_set, 2)

            def norm(i, p):
                g = 2 * i + p
                act.wait_ge(aggr, g + 1)
                nc.scalar.activation(lnv[:, :], mv[:, :, 1], ACT.Ln, bias=eps[:, :]).then_inc(rstd_s, 1)
                act.wait_ge(rstd_s, 2 * g + 1)
                nc.scalar.activation(rstd[:, :], lnv[:, :], ACT.Exp, scale=-0.5).then_inc(rstd_s, 1)

            def copy(i, p):
                g = 2 * i + p
                act.wait_ge(xTp, g + 1)
                if not early(g):
                    act.wait_ge(logits, g - 1)
                nc.scalar.activation(xT[p][:, :], bank[0][:, :], ACT.Copy).then_inc(xTr, 1)

            def step(i, p):
                norm(i, p)
                copy(i, p)
            pairs(act, NG, step)
            act.wait_ge(route, R["d"])
            nc.scalar.activation(ex[:, :], d[:, :], ACT.Exp).then_inc(ex_s, 1)
            act.wait_ge(route, R["blki"])

            def high(i, p):
                j = 2 * i + p
                act.wait_ge(xT_ps, j + 1)
                if not early(j):
                    act.wait_ge(h_ps, FC * (j - 1))
                nc.scalar.activation(xh[p][:, :], bank[0][:, 0:BS], ACT.Copy).then_inc(x_high, 1)

            def relu(i, p):
                j = 2 * i + p
                e = act.value_load(blki[0:1, j:j + 1] if isinstance(j, int) else blki[0:1, bass.ds(j, 1)],
                                   min_val=0, max_val=NX - 1)
                if not early(j):
                    act.wait_ge(h_low, j - 1)
                for c in range(FC):
                    act.wait_ge(h_ps, FC * j + c // 2 * 2 + 2)
                    nc.scalar.activation(h32[p][:, c, :], bank[2 + 2 * p + c // 2][:, BS * (c % 2):BS * (c % 2) + BS],
                                         ACT.Relu, bias=X.b1[:, bass.ds(e, 1), c],
                                         scale=2.0 ** (HSPLIT - SPLIT)).then_inc(h_relu, 1)

            def y_out(i, p):
                j = 2 * i + p
                e = act.value_load(blki[0:1, j:j + 1] if isinstance(j, int) else blki[0:1, bass.ds(j, 1)],
                                   min_val=0, max_val=NX - 1)
                act.wait_ge(y_ps, j + 1)
                if not early(j):
                    act.wait_ge(yR_ps, j - 1)
                nc.scalar.activation(yT[p][:, :], bank[6 + p][:, 0:BS], ACT.Identity, bias=X.b2[:, bass.ds(e, 1)],
                                     scale=2.0 ** (-HSPLIT - SPLIT)).then_inc(yT_s, 1)

            high(0, 0)

            def step(i, p):
                j = 2 * i + p
                relu(i, p)
                if not (isinstance(j, int) and j == NB - 1):
                    high(*((i, 1) if p == 0 else (i + 1, 0)))
                if not (isinstance(j, int) and j == 0):
                    y_out(*((i - 1, 1) if p == 0 else (i, 0)))
            pairs(act, NB, step)
            y_out(NB // 2 - 1, 1)

        @block.vector
        def _(dve):
            v = nc.vector
            dve.wait_ge(eps_set, 2)

            def norm(i, p):
                g = 2 * i + p
                dve.wait_ge(x_in[p], 16 * (i + 1))
                for q in range(Q):
                    ins = v.bn_stats(st[:, q, :], x_all[:, bass.ds(g * Q + q, 1), :].rearrange("p o e -> p (o e)"))
                    ins.then_inc(stats, 1)
                dve.wait_ge(stats, 2 * Q * g + Q)
                dve.sem_inc(stats_seen, 1)
                for q in range(Q):
                    v.bn_aggr(mv[:, q, :], st[:, q, :]).then_inc(stats, 1)
                dve.wait_ge(stats, 2 * Q * g + 2 * Q)
                dve.sem_inc(aggr, 1)
                dve.wait_ge(rstd_s, 2 * g + 2)
                if not early(g):
                    dve.wait_ge(xTp, g - 1)
                    dve.wait_ge(xn_kept, g - 1)
                for q in range(Q):
                    ins = v.tensor_scalar(xn[p][:, q, :],
                                          x_all[:, bass.ds(g * Q + q, 1), :].rearrange("p o e -> p (o e)"),
                                          mv[:, q, 0:1], rstd[:, q:q + 1], ALU.subtract, ALU.mult)
                ins.then_inc(xnr, 1)

            def keep(i, p):
                g = 2 * i + p
                dve.wait_ge(logits, g + 1)
                v.tensor_copy(L[:, bass.ds(g * Q, Q), :].rearrange("p q e -> p (q e)"), bank[1 + p][:, 0:NX * Q]).then_inc(L_cp, 1)

            def step(i, p):
                norm(i, p)
                g = 2 * i + p
                if not (isinstance(g, int) and g == 0):
                    keep(*((i - 1, 1) if p == 0 else (i, 0)))
            pairs(dve, NG, step)
            keep(NG // 2 - 1, 1)
            dve.wait_ge(L_cp, NG)

            def did(n, ins):
                ins.then_inc(route, 1)
                dve.wait_ge(route, R[n])

            def te(x):
                return x[:, :].unsqueeze(2).to_broadcast([P, NT, NX])

            def et(x):
                return x.rearrange("p t e -> p e t")

            def e_m8():
                return X.expert_m8[:, :].unsqueeze(1).to_broadcast([P, NT, NX])

            for n, (lg, m, i, O) in enumerate(((L, m1, i1, O1), (L2, m2, i2, O2))):
                k = str(n + 1)
                did("m" + k, v.tensor_reduce(m[:, :], lg[:, :, :], AX_X, ALU.max))
                did("eq" + k, v.tensor_tensor(eq[:, :, :], lg[:, :, :], te(m), ALU.is_equal))
                did("cand" + k, v.tensor_tensor(cand[:, :, :], eq[:, :, :], e_m8(), ALU.mult))
                did("i" + k, v.tensor_reduce(i[:, :], cand[:, :, :], AX_X, ALU.min))
                did("O" + k, v.tensor_tensor(O[:, :, :], e_m8(), te(i), ALU.is_equal))
                if n == 0:
                    did("L2", v.scalar_tensor_tensor(L2[:, :, :], O[:, :, :], -3e38, L[:, :, :], ALU.mult, ALU.add))
            did("d", v.tensor_tensor(d[:, :], m2[:, :], m1[:, :], ALU.subtract))
            did("mask", v.tensor_tensor(mask[:, :, :], et(O1[:, :, :]), et(O2[:, :, :]), ALU.add))
            flat = "p a b -> p (a b)"

            def as_et(x):
                return x[:, :, :].rearrange(flat).rearrange("p (e t) -> p e t", e=NX)
            dve.wait_ge(sums, 2)
            did("tot", v.tensor_copy(tot[:, :, :].rearrange(flat), bank[4][:, :]))
            did("cum", v.tensor_tensor_scan(cum[:, :, :].rearrange(flat), X.onesrow[:, :], tot[:, :, :].rearrange(flat),
                                            0.0, ALU.mult, ALU.add))
            did("excl", v.tensor_tensor(prod[:, :, :].rearrange(flat), cum[:, :, :].rearrange(flat),
                                        tot[:, :, :].rearrange(flat), ALU.subtract))
            did("base", v.tensor_tensor(base[:, :, :].rearrange(flat), bank[3][:, :], prod[:, :, :].rearrange(flat), ALU.add))
            did("cend", v.tensor_copy(ce[:, 1:NX + 1], as_et(cum)[:, :, NT - 1]))
            did("cnt", v.tensor_tensor(cnt[:, :], ce[:, 1:NX + 1], ce[:, 0:NX], ALU.subtract))
            did("over", v.tensor_tensor(over[:, :, :], cnt[:, :].unsqueeze(2).to_broadcast([P, NX, CB]),
                                        X.slot_row[:, :].unsqueeze(1).to_broadcast([P, NX, CB]), ALU.is_gt))
            did("nb", v.tensor_reduce(nb[:, :], over[:, :, :], AX_X, ALU.add))
            did("bend", v.tensor_tensor_scan(bend[:, :], X.onesrow[:, 0:NX], nb[:, :], 0.0, ALU.mult, ALU.add))
            did("bstart", v.tensor_tensor(bstart[:, :], bend[:, :], nb[:, :], ALU.subtract))
            did("adj", v.scalar_tensor_tensor(adj[:, :], bstart[:, :], float(BS), ce[:, 0:NX], ALU.mult, ALU.subtract))
            did("slot", v.tensor_tensor(as_et(prod), as_et(base), adj[:, :].unsqueeze(2).to_broadcast([P, NX, NT]), ALU.add))
            for k, (O, q) in enumerate(((O1, p1), (O2, p2))):
                did(f"p{k + 1}", v.tensor_tensor(cand[:, :, :], O[:, :, :], as_et(prod).rearrange("p e t -> p t e"), ALU.mult))
                did(f"pos{k + 1}", v.tensor_reduce(q[:, :], cand[:, :, :], AX_X, ALU.add))
            v.tensor_copy(posi[:, 0, :], p1[:, :]).then_inc(L_cp, 1)
            dve.wait_ge(L_cp, NG + 1)
            did("posi", v.tensor_copy(posi[:, 1, :], p2[:, :]))
            did("past", v.tensor_tensor(past[:, :, :], X.block_row[:, :].unsqueeze(2).to_broadcast([P, NB, NX]),
                                        bend[:, :].unsqueeze(1).to_broadcast([P, NB, NX]), ALU.is_ge))
            did("blk", v.tensor_reduce(blk[:, :], past[:, :, :], AX_X, ALU.add))
            did("blki", v.tensor_scalar(blki[:, :], blk[:, :], NX - 1.0, None, ALU.min))
            dve.wait_ge(ex_s, 1)
            did("den", v.tensor_scalar(den[:, :], ex[:, :], 1.0, None, ALU.add))
            did("w1", v.reciprocal(g1[:, :], den[:, :]))
            did("w2", v.tensor_tensor(g2[:, :], ex[:, :], g1[:, :], ALU.mult))

            def x_lo(i, p):
                j = 2 * i + p
                dve.wait_ge(x_high, j + 1)
                v.tensor_tensor(xl[p][:, :], bank[0][:, 0:BS], xh[p][:, :], ALU.subtract).then_inc(x_low, 1)

            def h_split(i, p):
                j = 2 * i + p
                dve.wait_ge(h_relu, FC * (j + 1))
                if not early(j):
                    dve.wait_ge(y_ps, j - 1)
                v.tensor_copy(hh[p][:, :, :], h32[p][:, :, :]).then_inc(h_high, 1)
                dve.wait_ge(h_high, j + 1)
                v.tensor_tensor(hl[p][:, :, :], h32[p][:, :, :], hh[p][:, :, :], ALU.subtract).then_inc(h_low, 1)

            def rows(i, p):
                j = 2 * i + p
                dve.wait_ge(yR_ps, j + 1)
                if not early(j):
                    dve.wait_ge(ys_out[p], 16 * i)
                v.tensor_copy(ys[p][:, :, :].rearrange("p r d -> p (r d)"), bank[1][:, 0:BS]).then_inc(ys_s, 1)

            x_lo(0, 0)

            def step(i, p):
                j = 2 * i + p
                if not (isinstance(j, int) and j == NB - 1):
                    x_lo(*((i, 1) if p == 0 else (i + 1, 0)))
                h_split(i, p)
                if not early(j):
                    rows(i - 1, p)
            pairs(dve, NB, step)
            rows(NB // 2 - 1, 0)
            rows(NB // 2 - 1, 1)
            for t in range(NT):
                dve.wait_ge(got[t % G], 32 * (calls * NT // G + t // G + 1))
                if t >= G:
                    dve.wait_ge(out_sem[t % G], 16 * (t // G))
                v.scalar_tensor_tensor(half[:, t % G, :], yg[:, t % G, 0, :], g1[:, t:t + 1], x_all[:, t, :],
                                       ALU.mult, ALU.add).then_inc(halved, 1)
                dve.wait_ge(halved, t + 1)
                v.scalar_tensor_tensor(half[:, t % G, :], yg[:, t % G, 1, :], g2[:, t:t + 1], half[:, t % G, :],
                                       ALU.mult, ALU.add).then_inc(added, 1)
    own.release()


DL = 32
TB = T // P
ROW = 32
AS = 4.0
SW = P + 2 * P
NEG = -1e30


class Attention:

    def __init__(self, sb):
        self.wq = [sb(f"wq_{n}", [P, HG, P], F16) for n in "hl"]
        self.wk = [sb(f"wk_{n}", [P, HG, P], F16) for n in "hl"]
        self.wv = [sb(f"wv_{n}", [P, P], F16) for n in "hl"]
        self.wo = sb("wo", [P, P])
        self.q_low = sb("q_low", [P, 1])
        self.k_low = sb("k_low", [P, 1])
        self.k_bias = sb("k_const", [P, 1])
        self.ident16 = sb("ident16", [P, P], F16)
        self.identb = sb("identb", [P, P], BF16)
        self.mask_ts = sb("mask_ts", [P, P], BF16)
        self.mask_st = sb("mask_st", [P, P], BF16)


def setup_attention(nc, ctx, A, X, ident, head_ones, bank):
    with ExitStack() as tmp:
        def sb(name, shape, dt=F32):
            return tmp.enter_context(nc.sbuf_tensor(name, shape, dt))

        def sem(name):
            return ctx.enter_context(nc.semaphore(name))

        wqkv = sb("wqkv", [P, 3 * P])
        lq = sb("lq", [P, DL])
        lk = sb("lk", [P, DL])
        core = sb("core", [P, DL])
        lqT = sb("lqT", [DL, P])
        lkT = sb("lkT", [DL, P])
        wqT = sb("wqT", [P, P])
        fold = sb("fold", [P, P])
        wqf = sb("wqf", [P, P])
        rowi = sb("rowi", [P, P], mybir.dt.int32)
        rows = sb("rows", [P, P])
        cls = sb("cls", [P, 3])
        loaded, made, chosen, steps, pe_steps, act_steps = (sem("att_" + n) for n in
                                                            ("loaded", "made", "chosen", "steps", "pe_steps", "act_steps"))
        block = tmp.enter_context(nc.Block())

        @block.sync
        def _(sp):
            sp.dma_start(wqkv[:, :], A["W_qkv"]).then_inc(loaded, 16)
            sp.dma_start(X.wo[:, :], A["W_o"]).then_inc(loaded, 16)
            sp.dma_start(lq[:, :], A["W_q_lsr"].rearrange("h d r -> (h d) r")).then_inc(loaded, 16)
            sp.dma_start(lk[:, :], A["W_k_lsr"].rearrange("h d r -> (h d) r")).then_inc(loaded, 16)
            for h in range(H):
                sp.dma_start(core[D * h:D * h + D, :], A["core"][h, :].partition_broadcast(D)).then_inc(loaded, 16)

        @block.gpsimd
        def _(pool):
            for t in (X.wq[0], X.wq[1], X.wk[0], X.wk[1]):
                pool.memset(t[:, :, :], 0.0).then_inc(made, 1)
            pool.memset(X.mask_ts[:, :], 0.0).then_inc(made, 1)
            pool.memset(X.mask_st[:, :], 0.0).then_inc(made, 1)
            pool.wait_ge(made, 6)
            pool.affine_select(out=X.mask_ts[:, :], in_=X.mask_ts[:, :], compare_op=ALU.is_ge, fill=NEG, base=0,
                               pattern=[[-1, P]], channel_multiplier=1).then_inc(made, 1)
            pool.affine_select(out=X.mask_st[:, :], in_=X.mask_st[:, :], compare_op=ALU.is_ge, fill=NEG, base=0,
                               pattern=[[1, P]], channel_multiplier=-1).then_inc(made, 1)
            pool.iota(rowi[:, 0:1], pattern=[[0, 1]], base=0, channel_multiplier=1).then_inc(made, 1)

        @block.tensor
        def _(pe):
            pe.wait_ge(steps, 1)
            nc.tensor.transpose(bank[0][0:DL, 0:P], lq[:, :], ident[:, :])
            nc.tensor.transpose(bank[1][0:DL, 0:P], lk[:, :], ident[:, :])
            nc.tensor.transpose(bank[2][:, 0:P], wqkv[:, 0:P], ident[:, :]).then_inc(pe_steps, 1)
            pe.wait_ge(steps, 4)
            nc.tensor.matmul(bank[3][:, 0:P], lqT[:, :], lkT[:, :], start=True, stop=True).then_inc(pe_steps, 1)
            pe.wait_ge(steps, 5)
            nc.tensor.matmul(bank[4][:, 0:P], wqT[:, :], fold[:, :], start=True, stop=True).then_inc(pe_steps, 1)

        @block.vector
        def _(dve):
            v = nc.vector
            dve.wait_ge(loaded, 16 * (4 + H))
            n = [0]

            def did(ins):
                ins.then_inc(steps, 1)
                n[0] += 1
                dve.wait_ge(steps, n[0])
            did(v.scalar_tensor_tensor(lq[:, :], lq[:, :], DL ** -0.5, core[:, :], ALU.mult, ALU.mult))
            dve.wait_ge(pe_steps, 1)
            did(v.tensor_copy(lqT[:, :], bank[0][0:DL, 0:P]))
            did(v.tensor_copy(lkT[:, :], bank[1][0:DL, 0:P]))
            did(v.tensor_copy(wqT[:, :], bank[2][:, 0:P]))
            dve.wait_ge(pe_steps, 2)
            did(v.tensor_tensor(fold[:, :], bank[3][:, 0:P], head_ones[:, :], ALU.mult))
            dve.wait_ge(pe_steps, 3)
            did(v.tensor_scalar(wqf[:, :], bank[4][:, 0:P], 2.0 ** AS, None, ALU.mult))
            did(v.tensor_scalar(wqkv[:, :], wqkv[:, :], 2.0 ** AS, None, ALU.mult))
            dve.wait_ge(made, 9)

            def hd(x):
                return x.rearrange("p (h d) -> p h d", d=D)

            for w, src in ((X.wq, wqf[:, :]), (X.wk, wqkv[:, P:2 * P])):
                for part in range(3):
                    o = [t[:, :, :].rearrange("p g (h r) -> p (g h) r", r=ROW)[:, :, D * part:D * part + D] for t in w]
                    did(v.tensor_copy(o[0], hd(src)))
                    did(v.tensor_tensor(o[1], hd(src), o[0], ALU.subtract))
            did(v.tensor_copy(X.wv[0][:, :], wqkv[:, 2 * P:]))
            did(v.tensor_tensor(X.wv[1][:, :], wqkv[:, 2 * P:], X.wv[0][:, :], ALU.subtract))
            did(v.tensor_copy(X.ident16[:, :], ident[:, :]))
            did(v.tensor_copy(X.identb[:, :], ident[:, :]))
            did(v.tensor_copy(rows[:, 0:1], rowi[:, 0:1]))
            for k in range(P // ROW - 1):
                did(v.tensor_scalar(rows[:, 1:2], rows[:, 0:1], float(ROW), -float(ROW), ALU.is_ge, ALU.mult))
                did(v.tensor_tensor(rows[:, 0:1], rows[:, 0:1], rows[:, 1:2], ALU.add))
            for k in range(1, 4):
                did(v.tensor_scalar(cls[:, k - 1:k], rows[:, 0:1], float(D * k), None, ALU.is_ge))
            did(v.tensor_scalar(rows[:, 2:3], rows[:, 0:1], float(3 * D + 2), None, ALU.is_ge))
            did(v.tensor_tensor(X.q_low[:, :], cls[:, 2:3], cls[:, 1:2], ALU.subtract))
            did(v.tensor_tensor(X.k_low[:, :], cls[:, 1:2], cls[:, 0:1], ALU.subtract))
            did(v.tensor_tensor(rows[:, 3:4], cls[:, 2:3], rows[:, 2:3], ALU.subtract))
            did(v.tensor_tensor(X.k_low[:, :], X.k_low[:, :], rows[:, 3:4], ALU.add))
            did(v.tensor_scalar(X.k_bias[:, :], rows[:, 3:4], 2.0 ** (2 * AS), None, ALU.mult))


FRONT_DVE_AT = dict(stats0=9, stats1=9, aggr0=10, aggr1=10, xn0=12, xn1=12, x_low=15)
FRONT_ACT_AT = dict(rstd_log=11, rstd=11, x_high=14)
PROJ_AT = dict(q01=0, q23=2, k01=4, k23=6, v=8)
FRONT_DVE, FRONT_ACT, PROJ = list(FRONT_DVE_AT), list(FRONT_ACT_AT), list(PROJ_AT)
MAXI = ["m", "high", "low", "add0", "add1"]
TAIL_DVE = ["sum0", "rec0", "yn0", "sum1", "rec1", "yn1", "out"]


def attention(nc, ctx, A, X, ident, bank, src, dst):
    with ExitStack() as tmp:
        def sb(n, shape, dt=F32):
            return tmp.enter_context(nc.sbuf_tensor(f"att_{n}", shape, dt))

        def sem(n):
            return own.get(f"att_{n}")

        own = Semaphores(nc)

        RP = 4
        xin, xres, xout = ([sb(f"{n}{p}", [P, TB, E]) for p in range(2)] for n in ("xin", "xres", "xout"))
        eps = sb("eps", [P, 1])
        st = sb("st", [P, TB, 6])
        mv = sb("mv", [P, TB, 2])
        lnv, rstd = (sb(n, [P, TB]) for n in ("lnv", "rstd"))
        xn = sb("xn", [P, TB, E])
        xh, xl = ([sb(f"{n}{p}", [P, T], F16) for p in range(2)] for n in ("xh", "xl"))
        raw = sb("raw", [P, 2 * T], F16)
        qp, kp = ([sb(f"{n}{p}", [P, HG, T], F16) for p in range(2)] for n in ("qp", "kp"))
        vx = [sb(f"vx{p}", [P, TB, H, 2, D + 1], F16) for p in range(2)]
        mx = [sb(f"mx{p}", [P, TB, H]) for p in range(2)]
        mneg = sb("mneg", [P, TB, H])
        mrow = sb("mrow", [P, TB, H, ROW], F16)
        p32 = sb("p32", [P, RP, SW])
        ph, pl = (sb(n, [P, RP, SW], F16) for n in ("ph", "pl"))
        ysum = sb("ysum", [P, TB, E])
        yrec = sb("yrec", [P, TB, H])
        yn = sb("yn", [P, TB, E])
        yT = sb("yT", [P, T])

        x_in, x_res, x_out = ([sem(f"{n}{p}") for p in range(2)] for n in ("x_in", "x_res", "x_out"))
        stats_seen = sem("stats_seen")
        (ready, front_dve, front_act, front_pe, proj_pe, proj_act, proj_dve, maxi_dve, maxi_pe, tail_dve, tail_pe,
         tail_act, s_ps, max_done, st_ps, exp_done, high_done, low_done, pv_done) = (
            sem(n) for n in ("ready", "front_dve", "front_act", "front_pe", "proj_pe", "proj_act", "proj_dve",
                             "maxi_dve", "maxi_pe", "tail_dve", "tail_pe", "tail_act", "s_in_psum", "max_done",
                             "st_in_psum", "exp_done", "high_done", "low_done", "pv_done"))

        ps_s, ps_st, ps_y, ps_x = bank[0:2], bank[2:4], bank[4:6], bank[6:8]
        srcb = src.rearrange("b (k p) e -> b p k e", p=P)
        dstb = dst.rearrange("b (k p) e -> b p k e", p=P)
        block = tmp.enter_context(nc.Block())

        def at(names, b, name):
            return b * len(names) + names.index(name) + 1

        def pairs(eng, count, step):
            for p in range(2):
                step(0, p)
            with eng.Fori(1, count // 2 - 1) as i:
                for p in range(2):
                    step(i, p)
            for p in range(2):
                step(count // 2 - 1, p)

        def first(i, p):
            return isinstance(i, int) and i == 0 and p == 0

        def last(i, p):
            return isinstance(i, int) and i == B // 2 - 1 and p == 1

        def nxt(i, p):
            return None if last(i, p) else (i, 1) if p == 0 else (i + 1, 0)

        def nxt2(i, p):
            return None if isinstance(i, int) and i == B // 2 - 1 else (i + 1, p)

        def prv(i, p):
            return None if first(i, p) else (i - 1, 1) if p == 0 else (i, 0)

        def segs(k):
            return (0, P) if k == 0 else (P, 2 * P)

        @block.sync
        def _(sp):
            def load(i, p):
                b = 2 * i + p
                if not (isinstance(i, int) and i == 0):
                    sp.wait_ge(front_dve, at(FRONT_DVE, b - 2, "xn1"))
                sp.dma_start(xin[p][:, :, :], srcb[b]).then_inc(x_in[p], 16)

            def load_res(i, p):
                b = 2 * i + p
                if not (isinstance(i, int) and i == 0):
                    sp.wait_ge(tail_pe, 2 * (b - 1))
                sp.dma_start(xres[p][:, :, :], srcb[b]).then_inc(x_res[p], 16)

            def store(i, p):
                b = 2 * i + p
                sp.wait_ge(tail_dve, at(TAIL_DVE, b, "out"))
                sp.dma_start(dstb[b], xout[p][:, :, :]).then_inc(x_out[p], 16)
            load(0, 0)
            load(0, 1)

            def step(i, p):
                if nxt2(i, p):
                    load(*nxt2(i, p))
                load_res(i, p)
                if prv(i, p):
                    store(*prv(i, p))
            pairs(sp, B, step)
            store(B // 2 - 1, 1)
            for p in range(2):
                sp.wait_ge(x_out[p], 16 * (B // 2))

        @block.gpsimd
        def _(pool):
            pool.memset(eps[:, :], LN_EPS).then_inc(ready, 1)
            pool.memset(mrow[:, :, :, :], 0.0).then_inc(ready, 1)
            for p in range(2):
                pool.memset(vx[p][:, :, :, 0, D], 2.0 ** AS).then_inc(ready, 1)
                pool.memset(vx[p][:, :, :, 1, D], 0.0).then_inc(ready, 1)

            def step(i, p):
                b = 2 * i + p
                for h in range(H):
                    pool.wait_ge(high_done, b * H + h + 1)
                    nc.gpsimd.tensor_tensor(pl[:, h % RP, :], p32[:, h % RP, :], ph[:, h % RP, :],
                                            ALU.subtract).then_inc(low_done, 1)
            pairs(pool, B, step)

        @block.tensor
        def _(pe):
            pe.wait_ge(ready, 6)
            mm = nc.tensor.matmul

            def front(i, p):
                b = 2 * i + p
                pe.wait_ge(front_dve, at(FRONT_DVE, b, "xn1"))
                if not (isinstance(i, int) and i == 0):
                    bb = b - 3
                    if not (isinstance(b, int) and b < 3):
                        pe.wait_ge(tail_act, bb + 1)
                    pe.wait_ge(proj_dve, at(PROJ, b - 1, "k23"))
                elif p == 1:
                    pe.wait_ge(front_dve, at(FRONT_DVE, 0, "x_low"))
                for k in range(TB):
                    ins = nc.tensor.transpose(ps_x[1][:, P * k:P * k + P], xn[:, k, :], ident[:, :])
                ins.then_inc(front_pe, 1)

            def proj(name, i, p):
                b = 2 * i + p
                three = ((0, xh), (0, xl), (1, xh))
                ps = ps_x[0 if name in ("q01", "k01", "v") else 1]
                if name == "q01":
                    pe.wait_ge(front_dve, at(FRONT_DVE, b, "x_low"))
                    if not first(i, p):
                        pe.wait_ge(maxi_dve, at(MAXI, b - 1, "add0"))
                elif name == "q23":
                    if first(i, p):
                        pe.wait_ge(front_dve, at(FRONT_DVE, 1, "x_low"))
                    else:
                        pe.wait_ge(maxi_dve, at(MAXI, b - 1, "add1"))
                else:
                    pe.wait_ge(proj_dve, at(PROJ, b, {"k01": "q01", "k23": "q23", "v": "k01"}[name]))
                if name == "v":
                    for k in range(TB):
                        for n, (w, x) in enumerate(three):
                            ins = mm(ps[:, P * k:P * k + P], x[p][:, P * k:P * k + P], X.wv[w][:, :],
                                     start=(n == 0), stop=(n == 2))
                else:
                    w = X.wq if name[0] == "q" else X.wk
                    for s in range(2):
                        g = int(name[1]) + s
                        for n, (wn, x) in enumerate(three):
                            ins = mm(ps[:, T * s:T * s + T], w[wn][:, g, :], x[p][:, :], start=(n == 0), stop=(n == 2))
                ins.then_inc(proj_pe, 1)

            def s_pass(i, p, h):
                b = 2 * i + p
                g, r = h // HL, ROW * (h % HL)
                if h == 0:
                    pe.wait_ge(proj_dve, at(PROJ, b, "k23"))
                if not (first(i, p) and h < 2):
                    pe.wait_ge(max_done, b * H + h - 1)
                ps = ps_s[h % 2]
                for k in range(TB):
                    o, n = segs(k)
                    mm(ps[:, o:o + n], qp[p][r:r + ROW, g, P * k:P * k + P], kp[p][r:r + ROW, g, 0:n],
                       start=True, stop=False)
                    ins = mm(ps[:, o + n - P:o + n], X.identb[:, :], X.mask_ts[:, :], start=False, stop=True)
                ins.then_inc(s_ps, 1)

            def turn_max(i, p):
                b = 2 * i + p
                pe.wait_ge(maxi_dve, at(MAXI, b, "low"))
                for n in range(2):
                    if n == 0:
                        if first(i, p):
                            pe.wait_ge(proj_dve, at(PROJ, 0, "v"))
                        else:
                            pe.wait_ge(proj_dve, at(PROJ, b, "v"))
                            if not (isinstance(b, int) and b < 2):
                                pe.wait_ge(tail_dve, at(TAIL_DVE, b - 2, "out"))
                    else:
                        pe.wait_ge(proj_dve, at(PROJ, b, "k23"))
                        if not last(i, p):
                            pe.wait_ge(front_dve, at(FRONT_DVE, b + 1, "x_low"))
                        if not (isinstance(b, int) and b < 2):
                            pe.wait_ge(tail_act, b - 1)
                    for s in range(2):
                        for k in range(TB):
                            g = 2 * n + s
                            ins = mm(ps_x[n][:, T * s + P * k:T * s + P * k + P],
                                     mrow[:, k, HL * g:HL * g + HL, :].rearrange("p h r -> p (h r)"), X.ident16[:, :],
                                     start=True, stop=True)
                    ins.then_inc(maxi_pe, 1)

            def st_pass(i, p, h):
                b = 2 * i + p
                g, r = h // HL, ROW * (h % HL)
                if h == 0:
                    pe.wait_ge(maxi_dve, at(MAXI, b, "add1"))
                if not (first(i, p) and h < 2):
                    pe.wait_ge(exp_done, b * H + h - 1)
                ps = ps_st[h % 2]
                for o, n, k in ((0, 2 * P, 0), (2 * P, P, 1)):
                    mm(ps[:, o:o + n], kp[p][r:r + ROW, g, P * k:P * k + P], qp[p][r:r + ROW, g, T - n:T],
                       start=True, stop=False)
                    ins = mm(ps[:, o:o + P], X.identb[:, :], X.mask_st[:, :], start=False, stop=True)
                ins.then_inc(st_ps, 1)

            def pv(i, p, h):
                b = 2 * i + p
                pe.wait_ge(low_done, b * H + h + 1)
                if h == 0:
                    pe.wait_ge(proj_dve, at(PROJ, b, "v"))
                    if not first(i, p):
                        pe.wait_ge(tail_dve, at(TAIL_DVE, b - 1, "yn1"))
                W2 = 2 * (D + 1)
                vv = [vx[p][:, k, h, :, :].rearrange("p a d -> p (a d)") for k in range(TB)]
                for k, blocks in ((0, ((0, 0),)), (1, ((P, 0), (2 * P, 1)))):
                    todo = [(pt, o, s) for o, s in blocks for pt in (ph, pl)]
                    for n, (pt, o, s) in enumerate(todo):
                        ins = mm(ps_y[k][:, W2 * h:W2 * h + W2], pt[:, h % RP, o:o + P], vv[s],
                                 start=(n == 0), stop=(n == len(todo) - 1))
                ins.then_inc(pv_done, 1)

            def tail_turn(i, p):
                b = 2 * i + p
                pe.wait_ge(tail_dve, at(TAIL_DVE, b, "yn1"))
                if not last(i, p):
                    pe.wait_ge(maxi_dve, at(MAXI, b + 1, "add1"))
                    if nxt2(i, p):
                        pe.wait_ge(proj_dve, at(PROJ, b + 2, "k23"))
                for k in range(TB):
                    ins = nc.tensor.transpose(ps_x[1][:, P * k:P * k + P], yn[:, k, :], ident[:, :])
                ins.then_inc(tail_pe, 1)

            def tail_out(i, p):
                b = 2 * i + p
                pe.wait_ge(tail_act, b + 1)
                pe.wait_ge(x_res[p], 16 * (i + 1))
                if not last(i, p):
                    pe.wait_ge(maxi_dve, at(MAXI, b + 1, "add0"))
                    if nxt2(i, p):
                        pe.wait_ge(proj_dve, at(PROJ, b + 2, "v"))
                if last(i, p):
                    pe.wait_ge(tail_dve, at(TAIL_DVE, b - 1, "out"))
                mm(ps_x[0][:, 0:T], ident[:, :], xres[p][:, :, :].rearrange("p k e -> p (k e)"), start=True, stop=False)
                for k in range(TB):
                    ins = mm(ps_x[0][:, P * k:P * k + P], yT[:, P * k:P * k + P], X.wo[:, :], start=False,
                             stop=(k == TB - 1))
                ins.then_inc(tail_pe, 1)

            front(0, 0)
            front(0, 1)
            for name in PROJ:
                proj(name, 0, 0)
            for h in range(H):
                s_pass(0, 0, h)

            def step(i, p):
                turn_max(i, p)
                for h in range(H):
                    st_pass(i, p, h)
                    if nxt(i, p):
                        for name in PROJ:
                            if PROJ_AT[name] == h:
                                proj(name, *nxt(i, p))
                        if h >= 8:
                            s_pass(*nxt(i, p), 2 * h - 16)
                            s_pass(*nxt(i, p), 2 * h - 15)
                    if h >= 2:
                        pv(i, p, h - 2)
                    if prv(i, p):
                        if h == 9:
                            tail_turn(*prv(i, p))
                        if h == 11:
                            tail_out(*prv(i, p))
                    if nxt2(i, p) and h == 13:
                        front(*nxt2(i, p))
                pv(i, p, H - 2)
                pv(i, p, H - 1)
            pairs(pe, B, step)
            tail_turn(B // 2 - 1, 1)
            tail_out(B // 2 - 1, 1)

        @block.scalar
        def _(act):
            nc.scalar.preload_act_table_set("natural_log_exp_and_others")
            act.wait_ge(ready, 6)
            a = nc.scalar.activation

            def front(name, i, p):
                b = 2 * i + p
                if name == "rstd_log":
                    act.wait_ge(front_dve, at(FRONT_DVE, b, "aggr1"))
                    ins = a(lnv[:, :], mv[:, :, 1], ACT.Ln, bias=eps[:, :])
                elif name == "rstd":
                    act.wait_ge(front_act, at(FRONT_ACT, b, "rstd_log"))
                    ins = a(rstd[:, :], lnv[:, :], ACT.Exp, scale=-0.5)
                else:
                    act.wait_ge(front_pe, b + 1)
                    if not (isinstance(i, int) and i == 0):
                        act.wait_ge(proj_pe, at(PROJ, b - 2, "v"))
                    ins = a(xh[p][:, :], ps_x[1][:, 0:T], ACT.Copy)
                ins.then_inc(front_act, 1)

            def proj(name, i, p):
                b = 2 * i + p
                act.wait_ge(proj_pe, at(PROJ, b, name))
                if name != "q01":
                    act.wait_ge(proj_dve, at(PROJ, b, PROJ[PROJ.index(name) - 1]))
                ps = ps_x[0 if name in ("q01", "k01", "v") else 1]
                if name == "v":
                    if not (isinstance(i, int) and i == 0):
                        act.wait_ge(pv_done, (b - 1) * H)
                    ins = a(vx[p][:, :, :, 0, 0:D], ps[:, 0:T].rearrange("p (k h d) -> p k h d", k=TB, d=D), ACT.Copy)
                elif name[0] == "q":
                    ins = a(raw[:, :], ps[:, :], ACT.Copy)
                else:
                    ins = a(raw[:, :], ps[:, :], ACT.Identity, bias=X.k_bias[:, :])
                ins.then_inc(proj_act, 1)

            def exps(i, p, h):
                b = 2 * i + p
                act.wait_ge(st_ps, b * H + h + 1)
                if not (first(i, p) and h < RP):
                    act.wait_ge(low_done, b * H + h - RP + 1)
                a(p32[:, h % RP, :], ps_st[h % 2][:, 0:SW], ACT.Exp, scale=2.0 ** (-2 * AS)).then_inc(exp_done, 1)

            def tail(i, p):
                b = 2 * i + p
                act.wait_ge(tail_pe, 2 * b + 1)
                a(yT[:, :], ps_x[1][:, 0:T], ACT.Copy).then_inc(tail_act, 1)

            for p in range(2):
                for name in FRONT_ACT:
                    front(name, 0, p)
            for name in PROJ:
                proj(name, 0, 0)

            def step(i, p):
                for h in range(H):
                    exps(i, p, h)
                    if nxt(i, p):
                        for name in PROJ:
                            if PROJ_AT[name] == h:
                                proj(name, *nxt(i, p))
                    if prv(i, p) and h == 9:
                        tail(*prv(i, p))
                    if nxt2(i, p):
                        for name in FRONT_ACT:
                            if FRONT_ACT_AT[name] == h:
                                front(name, *nxt2(i, p))
            pairs(act, B, step)
            tail(B // 2 - 1, 1)

        @block.vector
        def _(dve):
            v = nc.vector
            dve.wait_ge(ready, 6)

            def front(name, i, p):
                b = 2 * i + p
                k = int(name[-1]) if name[-1].isdigit() else 0
                if name.startswith("stats"):
                    dve.wait_ge(x_in[p], 16 * (i + 1))
                    ins = v.bn_stats(st[:, k, :], xin[p][:, k, :])
                elif name.startswith("aggr"):
                    dve.wait_ge(front_dve, at(FRONT_DVE, b, f"stats{k}"))
                    dve.sem_inc(stats_seen, 1)
                    ins = v.bn_aggr(mv[:, k, :], st[:, k, :])
                elif name.startswith("xn"):
                    dve.wait_ge(front_act, at(FRONT_ACT, b, "rstd"))
                    ins = v.tensor_scalar(xn[:, k, :], xin[p][:, k, :], mv[:, k, 0:1], rstd[:, k:k + 1],
                                          ALU.subtract, ALU.mult)
                else:
                    dve.wait_ge(front_act, at(FRONT_ACT, b, "x_high"))
                    ins = v.tensor_tensor(xl[p][:, :], ps_x[1][:, 0:T], xh[p][:, :], ALU.subtract)
                ins.then_inc(front_dve, 1)

            def proj(name, i, p):
                b = 2 * i + p
                dve.wait_ge(proj_act, at(PROJ, b, name))
                ps = ps_x[0 if name in ("q01", "k01", "v") else 1]
                if name == "v":
                    ins = v.tensor_tensor(vx[p][:, :, :, 1, 0:D].rearrange("p k h d -> p (k h) d"),
                                          ps[:, 0:T].rearrange("p (k h d) -> p (k h) d", k=TB, d=D),
                                          vx[p][:, :, :, 0, 0:D].rearrange("p k h d -> p (k h) d"), ALU.subtract)
                else:
                    q = name[0] == "q"
                    g = int(name[1])
                    ins = v.scalar_tensor_tensor((qp if q else kp)[p][:, g:g + 2, :].rearrange("p g t -> p (g t)"),
                                                 raw[:, :], (X.q_low if q else X.k_low)[:, :], ps[:, :],
                                                 ALU.mult, ALU.add)
                ins.then_inc(proj_dve, 1)

            def maxima(i, p, h):
                b = 2 * i + p
                dve.wait_ge(s_ps, b * H + h + 1)
                ps = ps_s[h % 2]
                v.tensor_reduce(mx[p][:, 0, h:h + 1], ps[:, 0:P], AX_X, ALU.max)
                v.tensor_reduce(mx[p][:, 1, h:h + 1], ps[:, P:3 * P], AX_X, ALU.max).then_inc(max_done, 1)

            def maxi(name, i, p):
                b = 2 * i + p
                if name == "m":
                    dve.wait_ge(max_done, (b + 1) * H)
                    ins = v.tensor_scalar(mneg[:, :, :], mx[p][:, :, :], -(2.0 ** (-2 * AS)), None, ALU.mult)
                elif name == "high":
                    dve.wait_ge(maxi_dve, at(MAXI, b, "m"))
                    if not first(i, p):
                        dve.wait_ge(maxi_pe, 2 * b)
                    ins = v.tensor_copy(mrow[:, :, :, 3 * D], mneg[:, :, :])
                elif name == "low":
                    dve.wait_ge(maxi_dve, at(MAXI, b, "high"))
                    ins = v.tensor_tensor(mrow[:, :, :, 3 * D + 1], mneg[:, :, :], mrow[:, :, :, 3 * D], ALU.subtract)
                else:
                    n = int(name[3])
                    dve.wait_ge(maxi_pe, 2 * b + n + 1)
                    o = qp[p][:, 2 * n:2 * n + 2, :].rearrange("p g t -> p (g t)")
                    ins = v.tensor_tensor(o, ps_x[n][:, :], o, ALU.add)
                ins.then_inc(maxi_dve, 1)

            def high(i, p, h):
                b = 2 * i + p
                dve.wait_ge(exp_done, b * H + h + 1)
                if not (first(i, p) and h < RP):
                    dve.wait_ge(pv_done, b * H + h - RP + 1)
                v.tensor_copy(ph[:, h % RP, :], p32[:, h % RP, :]).then_inc(high_done, 1)

            def tail(name, i, p):
                b = 2 * i + p
                k = int(name[-1]) if name[-1].isdigit() else 0
                yv = ps_y[k][:, 0:H * 2 * (D + 1)].rearrange("p (h a d) -> p h a d", h=H, a=2)
                if name.startswith("sum"):
                    dve.wait_ge(pv_done, (b + 1) * H)
                    ins = v.tensor_reduce(ysum[:, k, :].rearrange("p (h d) -> p h d", d=D),
                                          yv[:, :, :, 0:D].rearrange("p h a d -> p h d a"), AX_X, ALU.add)
                elif name.startswith("rec"):
                    ins = v.reciprocal(yrec[:, k, :], yv[:, :, 0, D])
                elif name.startswith("yn"):
                    dve.wait_ge(tail_dve, at(TAIL_DVE, b, f"rec{k}"))
                    if not first(i, p):
                        dve.wait_ge(tail_pe, 2 * (b - 1) + 1)
                    ins = v.tensor_tensor(yn[:, k, :].rearrange("p (h d) -> p h d", d=D),
                                          ysum[:, k, :].rearrange("p (h d) -> p h d", d=D),
                                          yrec[:, k, :].unsqueeze(2).to_broadcast([P, H, D]), ALU.mult)
                else:
                    dve.wait_ge(tail_pe, 2 * b + 2)
                    if not (isinstance(i, int) and i == 0):
                        dve.wait_ge(x_out[p], 16 * i)
                    ins = v.tensor_copy(xout[p][:, :, :].rearrange("p k e -> p (k e)"), ps_x[0][:, 0:T])
                ins.then_inc(tail_dve, 1)

            for p in range(2):
                for name in FRONT_DVE:
                    front(name, 0, p)
            for name in PROJ:
                proj(name, 0, 0)
            for h in range(H):
                maxima(0, 0, h)

            def step(i, p):
                for name in ("m", "high", "low"):
                    maxi(name, i, p)
                if prv(i, p):
                    for name in TAIL_DVE[:-1]:
                        tail(name, *prv(i, p))
                for name in ("add0", "add1"):
                    maxi(name, i, p)
                for h in range(H):
                    high(i, p, h)
                    if nxt(i, p):
                        for name in PROJ:
                            if PROJ_AT[name] == h:
                                proj(name, *nxt(i, p))
                        if h >= 8:
                            maxima(*nxt(i, p), 2 * h - 16)
                            maxima(*nxt(i, p), 2 * h - 15)
                    if prv(i, p) and h == 12:
                        tail("out", *prv(i, p))
                    if nxt2(i, p):
                        for name in FRONT_DVE:
                            if FRONT_DVE_AT[name] == h:
                                front(name, *nxt2(i, p))
            pairs(dve, B, step)
            for name in TAIL_DVE:
                tail(name, B // 2 - 1, 1)
    own.release()


def build(nc, A):
    with ExitStack() as ctx:
        def sb(name, shape, dt=F32):
            return ctx.enter_context(nc.sbuf_tensor(name, shape, dt))

        def sem(name):
            return ctx.enter_context(nc.semaphore(name))

        bank = [ctx.enter_context(nc.psum_tensor(f"bank{k}", [P, 512], F32)) for k in range(8)]
        ident = sb("ident", [P, P])
        head_ones = sb("head_ones", [P, P])
        setup_masks(nc, ctx, ident, head_ones)
        scan(nc, ctx, A, ident, head_ones, bank)
        experts = Experts(sb, sem)
        setup_experts(nc, ctx, A, experts, ident, bank)
        ffn(nc, ctx, A, experts, ident, bank, "ffn1", A["x1"], A["x2"])
        heads = Attention(sb)
        setup_attention(nc, ctx, A, heads, ident, head_ones, bank)
        attention(nc, ctx, A, heads, ident, bank, A["x2"], A["x3"])
        ffn(nc, ctx, A, experts, ident, bank, "ffn2", A["x3"], A["out"])


INPUTS = dict(x="L0_attn_a_x", Wq="L0_attn_a_Wq", Wk="L0_attn_a_Wk", Wv="L0_attn_a_Wv", Walpha="L0_attn_a_Walpha",
              Wbeta="L0_attn_a_Wbeta", A_log="L0_attn_a_A_log", dt_bias="L0_attn_a_dt_bias",
              Wgate="L0_attn_a_Wgate", Wout="L0_attn_a_Wout", rms_w="L0_attn_a_rms_w",
              W_qkv="L0_attn_b_W_qkv", W_q_lsr="L0_attn_b_W_q_lsr", W_k_lsr="L0_attn_b_W_k_lsr",
              core="L0_attn_b_lsr_core", W_o="L0_attn_b_W_o",
              Wg="L0_ffn_Wg", W1="L0_ffn_W1", b1="L0_ffn_b1", W2="L0_ffn_W2", b2="L0_ffn_b2")


def kernel(**inputs):
    import numpy as np
    import concourse.bacc as bacc
    from concourse.bass_utils import run_bass_kernel_spmd

    nc = bacc.Bacc("TRN2", target_bir_lowering=False, num_devices=1)
    arrays, A = {}, {}
    for name, long_name in INPUTS.items():
        a = np.ascontiguousarray(inputs[long_name])
        arrays[f"in_{name}"] = a
        A[name] = nc.dram_tensor(f"in_{name}", a.shape, mybir.dt.from_np(a.dtype), kind="ExternalInput").ap()
    for name in ("x1", "x2", "x3"):
        A[name] = nc.dram_tensor(name, (B, T, E), F32).ap()
    for name in ("slots_in", "slots_out"):
        A[name] = nc.dram_tensor(name, (NS, E), F32).ap()
    A["out"] = nc.dram_tensor("out", (B, T, E), F32, kind="ExternalOutput").ap()
    build(nc, A)
    r = run_bass_kernel_spmd(nc, [arrays], core_ids=[0])
    return r.results[0]["out"]
```

```python
import math
from contextlib import ExitStack

import concourse.bass as bass
from concourse import mybir

F32 = mybir.dt.float32
F16 = mybir.dt.float16
BF16 = mybir.dt.bfloat16
ALU = mybir.AluOpType
ACT = mybir.ActivationFunctionType
AX_X = mybir.AxisListType.X

P = 128
E = 128
H = 16
D = E // H
B = 32
T = 256
HG = 4
HL = H // HG
TC = 16
NC = T // TC
Q = 4
W = TC * B
SD = HL * D * D
LN_EPS = 1e-5
RMS_EPS = 1e-6
LOG_SHIFT = 20

PREP_SLOT = dict(
    stats0=0, stats1=1, stats2=2, stats3=3, aggr0=4, aggr1=5, aggr2=6, aggr3=7, xn0=12, xn1=13, xn2=14, xn3=15,
    v_scan=27, gate_log=31, k_clamp=29, q_clamp=33, ab_scan=37, z=38, minus_z=39, minus_abs_z=40, k_unit=36,
    k_scan=42, q_unit=43, q_scan=44, beta_den=45, minus_beta=46, z_pos=41, u_plus_2=47,
    u_rec=48, s=49, s2=50, h15=51, h13=52, h11=53, h9=54, h7=55, h5=56, h3=57, log1p=58, dt=59, decay_log=60)
PREP = sorted(PREP_SLOT, key=PREP_SLOT.get)
POST = ["o_rows"]
POST_SLOT = dict(o_rows=17)
PREP_ACT_STEP = dict(rstd_log=1, rstd=2, xT=3, k_sq=4, q_sq=5, v_rows=5, gate_abs=6, gate_exp=6, gate_ln=7,
                     k_log=8, k_rinv=8, gate_sig=9, gate_rows=9, q_log=10, q_rinv=10, beta_exp=11, u=11, alpha=15)
PREP_ACT = list(PREP_ACT_STEP)
POST_ACT_STEP = dict(o_sq=5, o_log=7, o_rinv=7, x1=13)
POST_ACT = list(POST_ACT_STEP)
PREP_POOL_STEP = dict(gate=10, beta_v=12, minus_alpha_beta=15, k_scaled=15)
PREP_POOL = list(PREP_POOL_STEP)
POST_POOL_STEP = dict(o_unit=8, o_gated=9)
POST_POOL = list(POST_POOL_STEP)
PREP_PE = ["xT", "k", "q", "v", "g", "k_norm", "q_norm", "ab"]
POST_PE = ["o_sum", "o_norm", "out"]


class Semaphores:

    def __init__(self, nc):
        self.nc, self.stack, self.all = nc, ExitStack(), []

    def get(self, name):
        self.all.append(self.stack.enter_context(self.nc.semaphore(name)))
        return self.all[-1]

    def release(self):
        with self.nc.Block() as block:
            @block.gpsimd
            def _(pool):
                for s in self.all:
                    pool.sem_clear(s)
        self.stack.close()


def setup_masks(nc, ctx, ident, head_ones):
    masks = ctx.enter_context(nc.semaphore("masks"))
    with nc.Block() as block:
        @block.gpsimd
        def _(pool):
            pool.memset(ident[:, :], 0.0).then_inc(masks, 1)
            pool.memset(head_ones[:, :], 1.0).then_inc(masks, 1)
            pool.wait_ge(masks, 2)
            pool.affine_select(out=ident[:, :], in_=ident[:, :], compare_op=ALU.not_equal, fill=1.0, base=0,
                               pattern=[[-1, P]], channel_multiplier=1).then_inc(masks, 1)
            ho = head_ones[:, :].rearrange("p (h d) -> p h d", d=D)
            pool.affine_select(out=ho, in_=ho, compare_op=ALU.is_ge, fill=0.0, base=0,
                               pattern=[[-D, H], [0, D]], channel_multiplier=1).then_inc(masks, 1)
            pool.wait_ge(masks, 4)
            pool.affine_select(out=ho, in_=ho, compare_op=ALU.is_ge, fill=0.0, base=D - 1,
                               pattern=[[D, H], [0, D]], channel_multiplier=-1).then_inc(masks, 1)


def scan(nc, ctx, A, ident, head_ones, bank):
    with ExitStack() as tmp:
        def sb(name, shape, dt=F32):
            return tmp.enter_context(nc.sbuf_tensor(name, shape, dt))

        def sem(name):
            return ctx.enter_context(nc.semaphore(name))

        ps_t, ps_k, ps_q, ps_v, ps_a, ps_g, ps_n, ps_o = bank

        eps_ln = sb("eps_ln", [P, 1])
        eps_rms = sb("eps_rms", [P, 1])
        one = sb("one", [P, 1])
        wout_rms = sb("wout_rms", [P, E])
        k_bias = sb("k_bias", [P, 1])
        q_bias = sb("q_bias", [P, 1])
        wk, wq, wv, wg, wab, wout = (sb(n, [P, E]) for n in ("wk", "wq", "wv", "wg", "wab", "wout"))
        rmsw = sb("rmsw", [P, 1])
        dt_bias = sb("dt_bias", [P, HL])
        a_log = sb("a_log", [P, HL])
        neg_a = sb("neg_a", [P, HL])

        xin = [sb(f"xin{p}", [P, Q, E]) for p in range(2)]
        xres = [sb(f"xres{p}", [P, Q, E]) for p in range(2)]
        x1 = [sb(f"x1_{p}", [P, Q, E]) for p in range(2)]
        st = sb("st", [P, Q, 6])
        mv = sb("mv", [P, Q, 2])
        lnv = sb("lnv", [P, Q])
        rstd = sb("rstd", [P, Q])
        xn = sb("xn", [P, Q, E])
        xT = sb("xT", [P, W])
        ksq, qsq, klog, qlog, krinv, qrinv, kE, qE, vE, aS = (
            sb(n, [P, W]) for n in ("ksq", "qsq", "klog", "qlog", "krinv", "qrinv", "kE", "qE", "vE", "aS"))
        vS = sb("vS", [P, W])
        kS, qS, gE = ([sb(f"{n}{p}", [P, W]) for p in range(2)] for n in ("kS", "qS", "gE"))
        gabs, gexp, gln, glog, gsig, gR = (sb(n, [P, W]) for n in ("gabs", "gexp", "gln", "glog", "gsig", "gR"))
        kabS = [sb(f"kabS{p}", [P, W]) for p in range(2)]
        (z, nz, nab, u, u2, urec, s1, s2, poly, zp, dtt, dlog, eb, eb1, mbeta) = (
            sb(n, [P, TC, HL]) for n in ("z", "nz", "nab", "u", "u2", "urec", "s1", "s2", "poly", "zp", "dtt",
                                         "dlog", "eb", "eb1", "mbeta"))
        polyb = sb("polyb", [P, TC, HL])
        alpha, mab = ([sb(f"{n}{p}", [P, TC, HL]) for p in range(2)] for n in ("alpha", "mab"))
        states = sb("states", [P, TC, SD])
        prod = [sb(f"prod{p}", [P, TC, HL * D, D + 1]) for p in range(2)]
        delta = sb("delta", [P, HL * D])
        outer = sb("outer", [P, SD])
        decayed = sb("decayed", [P, SD])
        sq = sb("sq", [P, TC, SD])
        osq = sb("osq", [P, W])
        olog, orinv, ounit, oE, og = (sb(n, [P, W]) for n in ("olog", "orinv", "ounit", "oE", "og"))

        consts = sem("consts")
        weights = sem("weights")
        neg_a_exp = sem("neg_a_exp")
        neg_a_ready = sem("neg_a_ready")
        wout_ready = sem("wout_ready")
        x_in = [sem(f"x_in{p}") for p in range(2)]
        x_res = [sem(f"x_res{p}") for p in range(2)]
        x1_out = [sem(f"x1_out{p}") for p in range(2)]
        stats_seen = sem("stats_seen")
        prep_dve, post_dve, prep_act, post_act, prep_pe, post_pe, prep_pool, post_pool = (
            sem(n) for n in ("prep_dve", "post_dve", "prep_act", "post_act", "prep_pe", "post_pe",
                             "prep_pool", "post_pool"))
        chain = sem("chain")
        state_ready = sem("state_ready")
        decay_ready = sem("decay_ready")
        sq_ready = sem("sq_ready")

        def prep_at(names, c, name):
            return c * len(names) + names.index(name) + 1

        def wait(eng, s, value):
            if not (isinstance(value, int) and value <= 0):
                eng.wait_ge(s, value)

        def run_chunks(eng, chunk):
            for p in range(2):
                chunk(0, p)
            with eng.Fori(1, NC // 2 - 1) as i:
                for p in range(2):
                    chunk(i, p)
            for p in range(2):
                chunk(NC // 2 - 1, p)

        def ahead(i, p):
            if isinstance(i, int) and i == NC // 2 - 1 and p:
                return None
            return (i, 1) if p == 0 else (i + 1, 0)

        def behind(i, p):
            if isinstance(i, int) and i == 0 and p == 0:
                return None
            return (i - 1, 1) if p == 0 else (i, 0)

        xc = A["x"].rearrange("b (c q l) e -> c l b q e", q=Q, l=4)
        x1c = A["x1"].rearrange("b (c q l) e -> c l b q e", q=Q, l=4)

        block = tmp.enter_context(nc.Block())

        @block.sync
        def _(sp):
            for dst, src in ((wk, "Wk"), (wq, "Wq"), (wv, "Wv"), (wg, "Wgate"), (wout, "Wout")):
                sp.dma_start(dst[:, :], A[src]).then_inc(weights, 16)
            for hh in range(H):
                sp.dma_start(rmsw[D * hh:D * hh + D, :], A["rms_w"].rearrange("(p o) -> p o", o=1)).then_inc(weights, 16)
            for g in range(HG):
                sp.dma_start(dt_bias[32 * g:32 * g + 32, :],
                             A["dt_bias"][HL * g:HL * g + HL].partition_broadcast(32)).then_inc(weights, 16)
                sp.dma_start(a_log[32 * g:32 * g + 32, :],
                             A["A_log"][HL * g:HL * g + HL].partition_broadcast(32)).then_inc(weights, 16)
            sp.wait_ge(consts, 1)
            wabv = wab[:, :].rearrange("p (g r) -> p g r", g=HG)
            sp.dma_start(wabv[:, :, 0:HL], A["Walpha"].rearrange("e (g r) -> e g r", g=HG)).then_inc(weights, 16)
            sp.dma_start(wabv[:, :, HL:2 * HL], A["Wbeta"].rearrange("e (g r) -> e g r", g=HG)).then_inc(weights, 16)

            def load(i, p):
                c = 2 * i + p
                wait(sp, prep_dve, prep_at(PREP, c - 2, "xn3") if not (isinstance(c, int) and c < 2) else 0)
                for l in range(4):
                    sp.dma_start(xin[p][32 * l:32 * l + 32, :, :], xc[c, l]).then_inc(x_in[p], 16)

            def load_res(i, p):
                c = 2 * i + p
                wait(sp, post_pe, prep_at(POST_PE, c - 2, "out") if not (isinstance(c, int) and c < 2) else 0)
                for l in range(4):
                    sp.dma_start(xres[p][32 * l:32 * l + 32, :, :], xc[c, l]).then_inc(x_res[p], 16)

            def store(i, p):
                c = 2 * i + p
                sp.wait_ge(post_act, prep_at(POST_ACT, c, "x1"))
                for l in range(4):
                    sp.dma_start(x1c[c, l], x1[p][32 * l:32 * l + 32, :, :]).then_inc(x1_out[p], 16)

            load(0, 0)

            def chunk(i, p):
                if ahead(i, p):
                    load(*ahead(i, p))
                load_res(i, p)
                if behind(i, p):
                    store(*behind(i, p))

            run_chunks(sp, chunk)
            store(NC // 2 - 1, 1)
            for p in range(2):
                sp.wait_ge(x1_out[p], 64 * (NC // 2))

        @block.gpsimd
        def _(pool):
            pool.memset(wab[:, :], 0.0).then_inc(consts, 1)
            pool.memset(eps_ln[:, :], LN_EPS).then_inc(consts, 1)
            pool.memset(eps_rms[:, :], RMS_EPS).then_inc(consts, 1)
            pool.memset(one[:, :], 1.0).then_inc(consts, 1)
            pool.memset(k_bias[:, :], 0.5 * LOG_SHIFT * math.log(2.0)).then_inc(consts, 1)
            pool.memset(q_bias[:, :], 0.5 * LOG_SHIFT * math.log(2.0) - 0.5 * math.log(D)).then_inc(consts, 1)
            pool.memset(states[:, TC - 1, :], 0.0).then_inc(consts, 1)
            def prep(name, i, p):
                c = 2 * i + p
                g = nc.gpsimd
                if name == "gate":
                    pool.wait_ge(prep_act, prep_at(PREP_ACT, c, "gate_rows"))
                    if not (isinstance(c, int) and c < 2):
                        pool.wait_ge(post_pool, prep_at(POST_POOL, c - 2, "o_gated"))
                    ins = g.tensor_tensor(gE[p][:, :], gR[:, :], gsig[:, :], ALU.mult)
                elif name == "beta_v":
                    pool.wait_ge(prep_dve, prep_at(PREP, c, "minus_beta"))
                    ins = g.tensor_tensor(prod[p][:, :, :, D].rearrange("p t (h i) -> p (t h) i", i=D),
                                          vS[:, :].rearrange("p (th i) -> p th i", i=D),
                                          mbeta[:, :, :].rearrange("p t h -> p (t h)").unsqueeze(2)
                                          .to_broadcast([P, TC * HL, D]), ALU.mult)
                elif name == "minus_alpha_beta":
                    pool.wait_ge(prep_act, prep_at(PREP_ACT, c, "alpha"))
                    ins = g.tensor_tensor(mab[p][:, :, :], alpha[p][:, :, :], mbeta[:, :, :], ALU.mult)
                else:
                    pool.wait_ge(prep_pool, prep_at(PREP_POOL, c, "minus_alpha_beta"))
                    ins = g.tensor_tensor(kabS[p][:, :].rearrange("p (th i) -> p th i", i=D),
                                          kS[p][:, :].rearrange("p (th i) -> p th i", i=D),
                                          mab[p][:, :, :].rearrange("p t h -> p (t h)").unsqueeze(2)
                                          .to_broadcast([P, TC * HL, D]), ALU.mult)
                ins.then_inc(prep_pool, 1)

            def post(name, i, p):
                c = 2 * i + p
                if name == "o_unit":
                    pool.wait_ge(post_act, prep_at(POST_ACT, c, "o_rinv"))
                    ins = nc.gpsimd.tensor_tensor(ounit[:, :], oE[:, :], orinv[:, :], ALU.mult)
                else:
                    pool.wait_ge(post_pool, prep_at(POST_POOL, c, "o_unit"))
                    if not (isinstance(c, int) and c == 0):
                        pool.wait_ge(post_pe, prep_at(POST_PE, c - 1, "out"))
                    ins = nc.gpsimd.tensor_tensor(og[:, :], ounit[:, :], gE[p][:, :], ALU.mult)
                ins.then_inc(post_pool, 1)

            for name in PREP_POOL:
                prep(name, 0, 0)

            def chunk(i, p):
                c = 2 * i + p
                for t in range(TC):
                    pool.wait_ge(state_ready, c * TC + t + 1)
                    if t == 0:
                        pool.wait_ge(prep_dve, prep_at(PREP, c, "q_scan"))
                        if behind(i, p):
                            pool.wait_ge(post_pe, prep_at(POST_PE, c - 1, "o_sum"))
                    qb = qS[p][:, 32 * t:32 * t + 32].rearrange("p (h j) -> p h j", h=HL).unsqueeze(2)
                    nc.gpsimd.tensor_tensor(
                        sq[:, t, :].rearrange("p (h i j) -> p h i j", h=HL, i=D),
                        states[:, t, :].rearrange("p (h i j) -> p h i j", h=HL, i=D),
                        qb.to_broadcast([P, HL, D, D]), ALU.mult).then_inc(sq_ready, 1)
                    if behind(i, p):
                        for name in POST_POOL:
                            if POST_POOL_STEP[name] == t:
                                post(name, *behind(i, p))
                    if ahead(i, p):
                        for name in PREP_POOL:
                            if PREP_POOL_STEP[name] == t:
                                prep(name, *ahead(i, p))

            run_chunks(pool, chunk)
            for name in POST_POOL:
                post(name, NC // 2 - 1, 1)

        @block.tensor
        def _(pe):
            pe.wait_ge(weights, 16 * (5 + H + 2 * HG + 2))

            def prep(i, p):
                c = 2 * i + p
                pe.wait_ge(prep_dve, prep_at(PREP, c, "xn3"))
                for q in range(Q):
                    ins = nc.tensor.transpose(ps_t[:, P * q:P * q + P], xn[:, q, :], ident[:, :])
                ins.then_inc(prep_pe, 1)
                pe.wait_ge(prep_act, prep_at(PREP_ACT, c, "xT"))
                for w, ps in ((wk, ps_k), (wq, ps_q), (wv, ps_v), (wg, ps_g)):
                    nc.tensor.matmul(ps[:, :], w[:, :], xT[:, :], start=True, stop=True).then_inc(prep_pe, 1)

            def norms(i, p):
                c = 2 * i + p
                pe.wait_ge(prep_act, prep_at(PREP_ACT, c, "k_sq"))
                nc.tensor.matmul(ps_n[:, :], head_ones[:, :], ksq[:, :], start=True, stop=True).then_inc(prep_pe, 1)
                pe.wait_ge(prep_act, prep_at(PREP_ACT, c, "q_sq"))
                nc.tensor.matmul(ps_t[:, :], head_ones[:, :], qsq[:, :], start=True, stop=True).then_inc(prep_pe, 1)

            def prep_ab(i, p):
                c = 2 * i + p
                nc.tensor.matmul(ps_a[:, :], wab[:, :], xT[:, :], start=True, stop=True).then_inc(prep_pe, 1)

            def o_sum(i, p):
                c = 2 * i + p
                pe.wait_ge(sq_ready, (c + 1) * TC)
                pe.wait_ge(prep_dve, prep_at(PREP, c, "ab_scan"))
                sv = sq[:, :, :].rearrange("p t (hi j) -> p (t hi) j", j=D)
                for j in range(D):
                    ins = nc.tensor.matmul(ps_a[:, :], ident[:, :], sv[:, :, j], start=(j == 0), stop=(j == D - 1))
                ins.then_inc(post_pe, 1)

            def o_norm(i, p):
                c = 2 * i + p
                pe.wait_ge(post_act, prep_at(POST_ACT, c, "o_sq"))
                nc.tensor.matmul(ps_a[:, :], head_ones[:, :], osq[:, :], start=True, stop=True).then_inc(post_pe, 1)

            def out_proj(i, p):
                c = 2 * i + p
                pe.wait_ge(post_pool, prep_at(POST_POOL, c, "o_gated"))
                pe.wait_ge(x_res[p], 64 * (i + 1))
                if not (isinstance(c, int) and c == 0):
                    pe.wait_ge(post_act, prep_at(POST_ACT, c - 1, "x1"))
                nc.tensor.matmul(ps_o[:, :], ident[:, :], xres[p][:, :, :].rearrange("p q e -> p (q e)"),
                                 start=True, stop=False)
                for q in range(Q):
                    ins = nc.tensor.matmul(ps_o[:, P * q:P * q + P], og[:, P * q:P * q + P], wout_rms[:, :],
                                           start=False, stop=(q == Q - 1))
                ins.then_inc(post_pe, 1)

            pe.wait_ge(wout_ready, 1)
            prep(0, 0)
            norms(0, 0)
            prep_ab(0, 0)

            def chunk(i, p):
                if behind(i, p):
                    o_sum(*behind(i, p))
                if ahead(i, p):
                    prep(*ahead(i, p))
                if behind(i, p):
                    o_norm(*behind(i, p))
                if ahead(i, p):
                    norms(*ahead(i, p))
                if behind(i, p):
                    bi, bp = behind(i, p)
                    pe.wait_ge(post_act, prep_at(POST_ACT, 2 * bi + bp, "o_log"))
                if ahead(i, p):
                    prep_ab(*ahead(i, p))
                if behind(i, p):
                    out_proj(*behind(i, p))

            run_chunks(pe, chunk)
            o_sum(NC // 2 - 1, 1)
            o_norm(NC // 2 - 1, 1)
            out_proj(NC // 2 - 1, 1)

        @block.scalar
        def _(act):
            act.wait_ge(consts, 7)
            act.wait_ge(weights, 16 * (5 + H + 2 * HG + 2))
            nc.scalar.preload_act_table_set("natural_log_exp_and_others")
            nc.scalar.activation(neg_a[:, :], a_log[:, :], ACT.Exp).then_inc(neg_a_exp, 1)

            def prep(name, i, p):
                c = 2 * i + p

                def need(s, names, what):
                    act.wait_ge(s, prep_at(names, c, what))

                if name == "rstd_log":
                    need(prep_dve, PREP, "aggr3")
                    ins = nc.scalar.activation(lnv[:, :], mv[:, :, 1], ACT.Ln, bias=eps_ln[:, :])
                elif name == "rstd":
                    need(prep_act, PREP_ACT, "rstd_log")
                    ins = nc.scalar.activation(rstd[:, :], lnv[:, :], ACT.Exp, scale=-0.5)
                elif name == "xT":
                    need(prep_pe, PREP_PE, "xT")
                    ins = nc.scalar.activation(xT[:, :], ps_t[:, :], ACT.Copy)
                elif name == "k_sq":
                    need(prep_pe, PREP_PE, "k")
                    ins = nc.scalar.activation(ksq[:, :], ps_k[:, :], ACT.Square)
                elif name == "q_sq":
                    need(prep_pe, PREP_PE, "q")
                    ins = nc.scalar.activation(qsq[:, :], ps_q[:, :], ACT.Square)
                elif name == "v_rows":
                    need(prep_pe, PREP_PE, "v")
                    ins = nc.scalar.activation(vE[:, :], ps_v[:, :], ACT.Copy, scale=-1.0)
                elif name == "gate_abs":
                    need(prep_pe, PREP_PE, "g")
                    ins = nc.scalar.activation(gabs[:, :], ps_g[:, :], ACT.Abs)
                elif name == "gate_exp":
                    need(prep_act, PREP_ACT, "gate_abs")
                    ins = nc.scalar.activation(gexp[:, :], gabs[:, :], ACT.Exp, scale=-1.0)
                elif name == "gate_ln":
                    need(prep_act, PREP_ACT, "gate_exp")
                    ins = nc.scalar.activation(gln[:, :], gexp[:, :], ACT.Ln, bias=one[:, :])
                elif name == "gate_sig":
                    need(prep_dve, PREP, "gate_log")
                    ins = nc.scalar.activation(gsig[:, :], glog[:, :], ACT.Exp)
                elif name == "gate_rows":
                    ins = nc.scalar.activation(gR[:, :], ps_g[:, :], ACT.Copy)
                elif name in ("k_log", "q_log"):
                    need(prep_dve, PREP, name[0] + "_clamp")
                    src, dst = (ksq, klog) if name[0] == "k" else (qsq, qlog)
                    ins = nc.scalar.activation(dst[:, :], src[:, :], ACT.Ln, scale=float(2 ** LOG_SHIFT))
                elif name in ("k_rinv", "q_rinv"):
                    need(prep_act, PREP_ACT, name[0] + "_log")
                    src, dst, bias = (klog, krinv, k_bias) if name[0] == "k" else (qlog, qrinv, q_bias)
                    ins = nc.scalar.activation(dst[:, :], src[:, :], ACT.Exp, scale=-0.5, bias=bias[:, :])
                elif name == "u":
                    need(prep_dve, PREP, "minus_abs_z")
                    ins = nc.scalar.activation(u[:, :, :], nab[:, :, :], ACT.Exp)
                elif name == "beta_exp":
                    need(prep_dve, PREP, "ab_scan")
                    zb = aS[:, :].rearrange("p (t r) -> p t r", t=TC)[:, :, HL:2 * HL]
                    ins = nc.scalar.activation(eb[:, :, :], zb, ACT.Exp, scale=-1.0)
                elif name == "alpha":
                    need(prep_dve, PREP, "decay_log")
                    ins = nc.scalar.activation(alpha[p][:, :, :], dlog[:, :, :], ACT.Exp)
                ins.then_inc(prep_act, 1)

            def post(name, i, p):
                c = 2 * i + p
                if name == "o_sq":
                    act.wait_ge(post_dve, prep_at(POST, c, "o_rows"))
                    ins = nc.scalar.activation(osq[:, :], oE[:, :], ACT.Square)
                elif name == "o_log":
                    act.wait_ge(post_pe, prep_at(POST_PE, c, "o_norm"))
                    ins = nc.scalar.activation(olog[:, :], ps_a[:, :], ACT.Ln, scale=1.0 / D, bias=eps_rms[:, :])
                elif name == "x1":
                    act.wait_ge(post_pe, prep_at(POST_PE, c, "out"))
                    if not (isinstance(c, int) and c < 2):
                        act.wait_ge(x1_out[p], 64 * i)
                    ins = nc.scalar.activation(x1[p][:, :, :].rearrange("p q e -> p (q e)"), ps_o[:, :], ACT.Copy)
                else:
                    act.wait_ge(post_act, prep_at(POST_ACT, c, "o_log"))
                    ins = nc.scalar.activation(orinv[:, :], olog[:, :], ACT.Exp, scale=-0.5)
                ins.then_inc(post_act, 1)

            for name in PREP_ACT:
                prep(name, 0, 0)

            def chunk(i, p):
                c = 2 * i + p
                for t in range(TC):
                    wait(act, state_ready, c * TC + t)
                    if t == 0:
                        act.wait_ge(prep_act, prep_at(PREP_ACT, c, "alpha"))
                    for h in range(HL):
                        ins = nc.scalar.activation(decayed[:, 64 * h:64 * h + 64],
                                                   states[:, (t - 1) % TC, 64 * h:64 * h + 64],
                                                   ACT.Copy, scale=alpha[p][:, t, h:h + 1])
                    ins.then_inc(decay_ready, 1)
                    if behind(i, p):
                        for name in POST_ACT:
                            if POST_ACT_STEP[name] == t:
                                post(name, *behind(i, p))
                    if ahead(i, p):
                        for name in PREP_ACT:
                            if PREP_ACT_STEP[name] == t:
                                prep(name, *ahead(i, p))

            run_chunks(act, chunk)
            for name in POST_ACT:
                post(name, NC // 2 - 1, 1)

        @block.vector
        def _(dve):
            dve.wait_ge(consts, 7)
            dve.wait_ge(weights, 16 * (5 + H + 2 * HG + 2))
            dve.wait_ge(neg_a_exp, 1)
            nc.vector.tensor_scalar(neg_a[:, :], neg_a[:, :], -1.0, None, ALU.mult).then_inc(neg_a_ready, 1)
            nc.vector.tensor_scalar(wout_rms[:, :], wout[:, :], rmsw[:, 0:1], None, ALU.mult).then_inc(wout_ready, 1)
            dve.wait_ge(neg_a_ready, 1)

            def prep(name, i, p):
                c = 2 * i + p

                def need(what):
                    dve.wait_ge(prep_dve, prep_at(PREP, c, what))

                def act_did(what):
                    dve.wait_ge(prep_act, prep_at(PREP_ACT, c, what))

                def pe_did(what):
                    dve.wait_ge(prep_pe, prep_at(PREP_PE, c, what))

                aview = aS[:, :].rearrange("p (t r) -> p t r", t=TC)

                def hl(x):
                    return x.unsqueeze(1).to_broadcast([P, TC, HL])

                v = nc.vector
                if name.startswith("stats"):
                    q = int(name[5:])
                    if q == 0:
                        dve.wait_ge(x_in[p], 64 * (i + 1))
                    ins = v.bn_stats(st[:, q, :], xin[p][:, q, :])
                elif name.startswith("aggr"):
                    q = int(name[4:])
                    need(f"stats{q}")
                    dve.sem_inc(stats_seen, 1)
                    ins = v.bn_aggr(mv[:, q, :], st[:, q, :])
                elif name.startswith("xn"):
                    q = int(name[2:])
                    act_did("rstd")
                    ins = v.tensor_scalar(xn[:, q, :], xin[p][:, q, :], mv[:, q, 0:1], rstd[:, q:q + 1],
                                          ALU.subtract, ALU.mult)
                elif name == "v_scan":
                    act_did("v_rows")
                    ins = v.transpose(vS[:, :], vE[:, :])
                elif name == "k_clamp":
                    pe_did("k_norm")
                    ins = v.tensor_scalar(ksq[:, :], ps_n[:, :], 1e-24, None, ALU.max)
                elif name == "q_clamp":
                    pe_did("q_norm")
                    ins = v.tensor_scalar(qsq[:, :], ps_t[:, :], 1e-24, None, ALU.max)
                elif name == "ab_scan":
                    pe_did("ab")
                    ins = v.transpose(aS[:, :], ps_a[:, :])
                elif name == "z":
                    need("ab_scan")
                    ins = v.tensor_tensor(z[:, :, :], aview[:, :, 0:HL], hl(dt_bias[:, :]), ALU.add)
                elif name == "minus_z":
                    need("z")
                    ins = v.tensor_scalar(nz[:, :, :], z[:, :, :], -1.0, None, ALU.mult)
                elif name == "minus_abs_z":
                    need("minus_z")
                    ins = v.tensor_tensor(nab[:, :, :], z[:, :, :], nz[:, :, :], ALU.min)
                elif name == "k_unit":
                    act_did("k_rinv")
                    ins = v.tensor_tensor(kE[:, :], ps_k[:, :], krinv[:, :], ALU.mult)
                elif name == "k_scan":
                    need("k_unit")
                    ins = v.transpose(kS[p][:, :], kE[:, :])
                elif name == "q_unit":
                    act_did("q_rinv")
                    ins = v.tensor_tensor(qE[:, :], ps_q[:, :], qrinv[:, :], ALU.mult)
                elif name == "q_scan":
                    need("q_unit")
                    if not (isinstance(c, int) and c < 2):
                        dve.wait_ge(sq_ready, (c - 1) * TC)
                    ins = v.transpose(qS[p][:, :], qE[:, :])
                elif name == "gate_log":
                    act_did("gate_ln")
                    ins = v.scalar_tensor_tensor(glog[:, :], ps_g[:, :], 0.0, gln[:, :], ALU.min, ALU.subtract)
                elif name == "beta_den":
                    act_did("beta_exp")
                    ins = v.tensor_scalar(eb1[:, :, :], eb[:, :, :], -1.0, -1.0, ALU.mult, ALU.add)
                elif name == "minus_beta":
                    need("beta_den")
                    ins = v.reciprocal(mbeta[:, :, :], eb1[:, :, :])
                elif name == "z_pos":
                    ins = v.tensor_scalar(zp[:, :, :], z[:, :, :], 0.0, None, ALU.max)
                elif name == "u_plus_2":
                    act_did("u")
                    ins = v.tensor_scalar(u2[:, :, :], u[:, :, :], 2.0, None, ALU.add)
                elif name == "u_rec":
                    need("u_plus_2")
                    ins = v.reciprocal(urec[:, :, :], u2[:, :, :])
                elif name == "s":
                    need("u_rec")
                    ins = v.tensor_tensor(s1[:, :, :], u[:, :, :], urec[:, :, :], ALU.mult)
                elif name == "s2":
                    need("s")
                    ins = v.tensor_tensor(s2[:, :, :], s1[:, :, :], s1[:, :, :], ALU.mult)
                elif name == "h15":
                    need("s2")
                    ins = v.tensor_scalar(poly[:, :, :], s2[:, :, :], 1.0 / 15, None, ALU.mult)
                elif name[0] == "h" and name[1:].isdigit():
                    n = int(name[1:])
                    need(f"h{n + 2}")
                    a, b = (poly, polyb) if (n // 2) % 2 == 0 else (polyb, poly)
                    ins = v.scalar_tensor_tensor(b[:, :, :], a[:, :, :], 1.0 / n, s2[:, :, :], ALU.add, ALU.mult)
                elif name == "log1p":
                    need("h3")
                    ins = v.scalar_tensor_tensor(poly[:, :, :], poly[:, :, :], 1.0, s1[:, :, :], ALU.add, ALU.mult)
                elif name == "dt":
                    need("log1p")
                    ins = v.scalar_tensor_tensor(dtt[:, :, :], poly[:, :, :], 2.0, zp[:, :, :], ALU.mult, ALU.add)
                elif name == "decay_log":
                    need("dt")
                    ins = v.tensor_tensor(dlog[:, :, :], dtt[:, :, :], hl(neg_a[:, :]), ALU.mult)
                ins.then_inc(prep_dve, 1)

            def post(name, i, p):
                c = 2 * i + p
                dve.wait_ge(post_pe, prep_at(POST_PE, c, "o_sum"))
                nc.vector.transpose(oE[:, :], ps_a[:, :]).then_inc(post_dve, 1)

            for name in PREP:
                prep(name, 0, 0)

            LINKS = 3

            def chunk(i, p):
                c = 2 * i + p

                def side(slot):
                    if behind(i, p):
                        for name in POST:
                            if POST_SLOT[name] == slot:
                                post(name, *behind(i, p))
                    if ahead(i, p):
                        for name in PREP:
                            if PREP_SLOT[name] == slot:
                                prep(name, *ahead(i, p))

                v = nc.vector
                for t in range(TC):
                    prev = states[:, (t - 1) % TC, :]
                    base = (c * TC + t) * LINKS
                    kt = kS[p][:, 32 * t:32 * t + 32].rearrange("p (h j) -> p h j", h=HL).unsqueeze(2) \
                        .to_broadcast([P, HL, D, D])

                    def hij(x):
                        return x.rearrange("p (h i j) -> p h i j", h=HL, i=D)

                    wait(dve, state_ready, c * TC + t)
                    if t == 0:
                        dve.wait_ge(prep_pool, prep_at(PREP_POOL, c, "k_scaled"))
                    v.tensor_tensor(prod[p][:, t, :, 0:D].rearrange("p (h i) j -> p h i j", h=HL), hij(prev),
                                    kabS[p][:, 32 * t:32 * t + 32].rearrange("p (h j) -> p h j", h=HL).unsqueeze(2)
                                    .to_broadcast([P, HL, D, D]), ALU.mult).then_inc(chain, 1)
                    side(4 * t)
                    dve.wait_ge(chain, base + 1)
                    v.tensor_reduce(delta[:, :], prod[p][:, t, :, :], AX_X, ALU.add).then_inc(chain, 1)
                    side(4 * t + 1)
                    dve.wait_ge(chain, base + 2)
                    v.tensor_tensor(hij(outer[:, :]),
                                    delta[:, :].rearrange("p (h i) -> p h i", h=HL).unsqueeze(3)
                                    .to_broadcast([P, HL, D, D]), kt, ALU.mult).then_inc(chain, 1)
                    side(4 * t + 2)
                    dve.wait_ge(chain, base + 3)
                    dve.wait_ge(decay_ready, c * TC + t + 1)
                    if behind(i, p):
                        dve.wait_ge(sq_ready, (c - 1) * TC + t + 1)
                    v.tensor_tensor(states[:, t, :], decayed[:, :], outer[:, :], ALU.add).then_inc(state_ready, 1)
                    side(4 * t + 3)

            run_chunks(dve, chunk)
            for name in POST:
                post(name, NC // 2 - 1, 1)


NX = 8
F = 512
FC = F // P
NT = B * T // P
BS = 256
BR = BS // P
NB = 2 * NT // BR + NX
NS = NB * BS
NA = NS // P
TQ = 8
AHEAD = 4
LAG = 3
ROUND = 1.5 * 2.0 ** 23
CB = B * T // BS
SPLIT = 8.0
HSPLIT = 4.0


class Experts:

    def __init__(self, sb, sem):
        self.w1 = [sb(f"w1_{n}", [P, NX, FC, P], F16) for n in "hl"]
        self.w2 = [sb(f"w2_{n}", [P, NX, FC, P], F16) for n in "hl"]
        self.fetched = [sem(f"fetched{g}") for g in range(AHEAD)]
        self.scattered = [sem(f"scattered{g}") for g in range(AHEAD)]
        self.calls = 0
        self.wgate = sb("w_router", [P, NX])
        self.b1 = sb("b1_cols", [P, NX, FC])
        self.b2 = sb("b2_cols", [P, NX])
        self.before = sb("before", [P, P], F16)
        self.all16 = sb("all16", [P, P], F16)
        self.expert_m8 = sb("expert_m8", [P, NX])
        self.block_row = sb("block_row", [P, NB])
        self.slot_row = sb("slot_row", [P, CB])
        self.onesrow = sb("onesrow", [P, NX * NT])
        self.slot_col = sb("slot_col", [P, P], F16)
        self.slot_tile = sb("slot_tile", [P, NA], F16)
        self.nth = sb("nth", [P, 2 * NT])
        self.row = sb("row", [P, 1])
        self.spare = sb("spare", [P, NA])


def setup_experts(nc, ctx, tmp, block, A, X, ident, bank):
    def sb(name, shape, dt=F32):
        return tmp.enter_context(nc.sbuf_tensor(name, shape, dt))

    def sem(name):
        return ctx.enter_context(nc.semaphore(name))

    raw = [sb(f"raw_w{k}", [P, NX, F]) for k in range(2)]
    biases = sb("biases", [NX * (FC + 1), P])
    iot = sb("iot", [P, NB + CB + NX], mybir.dt.int32)
    iot2 = sb("iot2", [P, P + NA + 2 * NT + 1 + NA], mybir.dt.int32)
    raw_in = [sem("w1_in"), sem("w2_in")]
    small_in, high, low, masked, iotas, copied, turned = (
        sem(n) for n in ("small_in", "high", "low", "masked", "iotas", "copied", "turned"))

    @block.sync
    def _(sp):
        sp.dma_start(X.wgate[:, :], A["Wg"]).then_inc(small_in, 16)
        sp.dma_start(biases[0:NX * FC, :], A["b1"].rearrange("e (c p) -> (e c) p", c=FC)).then_inc(small_in, 16)
        sp.dma_start(biases[NX * FC:, :], A["b2"]).then_inc(small_in, 16)

    @block.tensor
    def _(pe):
        pe.wait_ge(small_in, 16 * 3)
        n = NX * (FC + 1)
        nc.tensor.transpose(bank[5][:, 0:n], biases[:, :], ident[0:n, 0:n]).then_inc(turned, 1)

    @block.gpsimd
    def _(pool):
        pool.memset(X.before[:, :], 1.0).then_inc(masked, 1)
        pool.memset(X.all16[:, :], 1.0).then_inc(masked, 1)
        pool.memset(X.onesrow[:, :], 1.0).then_inc(masked, 1)
        pool.wait_ge(masked, 3)
        pool.affine_select(out=X.before[:, :], in_=X.before[:, :], compare_op=ALU.is_gt, fill=0.0, base=0,
                           pattern=[[1, P]], channel_multiplier=-1).then_inc(masked, 1)
        pool.iota(iot[:, 0:NB], pattern=[[1, NB]], base=0, channel_multiplier=0).then_inc(iotas, 1)
        pool.iota(iot[:, NB:NB + CB], pattern=[[BS, CB]], base=0, channel_multiplier=0).then_inc(iotas, 1)
        pool.iota(iot[:, NB + CB:], pattern=[[1, NX]], base=-NX, channel_multiplier=0).then_inc(iotas, 1)
        pool.iota(iot2[:, 0:P], pattern=[[1, P]], base=0, channel_multiplier=0).then_inc(iotas, 1)
        pool.iota(iot2[:, P:P + NA], pattern=[[1, NA]], base=0, channel_multiplier=0).then_inc(iotas, 1)
        pool.iota(iot2[:, P + NA:P + NA + 2 * NT], pattern=[[1, 2 * NT]], base=1, channel_multiplier=0).then_inc(iotas, 1)
        pool.iota(iot2[:, P + NA + 2 * NT:P + NA + 2 * NT + 1], pattern=[[1, 1]], base=0,
                  channel_multiplier=1).then_inc(iotas, 1)
        pool.iota(iot2[:, P + NA + 2 * NT + 1:], pattern=[[P, NA]], base=2 * B * T, channel_multiplier=1).then_inc(iotas, 1)

    @block.scalar
    def _(act):
        nc.scalar.dma_start(raw[0][:, :, :], A["W1"].rearrange("e d f -> d e f")).then_inc(raw_in[0], 16)
        nc.scalar.dma_start(raw[1][:, :, :].rearrange("p e (c d) -> p e c d", c=FC),
                     A["W2"].rearrange("e (c f) d -> f e c d", c=FC)).then_inc(raw_in[1], 16)
        for k, w in enumerate((X.w1, X.w2)):
            act.wait_ge(raw_in[k], 16)
            nc.scalar.activation(w[0][:, :, :, :].rearrange("p e c d -> p (e c d)"),
                                 raw[k][:, :, :].rearrange("p e f -> p (e f)"), ACT.Copy,
                                 scale=2.0 ** SPLIT).then_inc(high, 1)

    @block.vector
    def _(dve):
        dve.wait_ge(iotas, 8)
        nc.vector.tensor_copy(X.block_row[:, :], iot[:, 0:NB]).then_inc(copied, 1)
        nc.vector.tensor_copy(X.slot_row[:, :], iot[:, NB:NB + CB]).then_inc(copied, 1)
        nc.vector.tensor_copy(X.expert_m8[:, :], iot[:, NB + CB:]).then_inc(copied, 1)
        nc.vector.tensor_copy(X.slot_col[:, :], iot2[:, 0:P]).then_inc(copied, 1)
        nc.vector.tensor_copy(X.slot_tile[:, :], iot2[:, P:P + NA]).then_inc(copied, 1)
        nc.vector.tensor_copy(X.nth[:, :], iot2[:, P + NA:P + NA + 2 * NT]).then_inc(copied, 1)
        nc.vector.tensor_copy(X.row[:, :], iot2[:, P + NA + 2 * NT:P + NA + 2 * NT + 1]).then_inc(copied, 1)
        nc.vector.tensor_copy(X.spare[:, :], iot2[:, P + NA + 2 * NT + 1:]).then_inc(copied, 1)
        dve.wait_ge(turned, 1)
        nc.vector.tensor_scalar(X.b1[:, :, :].rearrange("p e c -> p (e c)"), bank[5][:, 0:NX * FC], 2.0 ** HSPLIT, None,
                                ALU.mult).then_inc(copied, 1)
        nc.vector.tensor_copy(X.b2[:, :], bank[5][:, NX * FC:NX * (FC + 1)]).then_inc(copied, 1)
        for k, w in enumerate((X.w1, X.w2)):
            dve.wait_ge(high, k + 1)
            nc.vector.scalar_tensor_tensor(w[1][:, :, :, :].rearrange("p e c d -> p (e c d)"),
                                           raw[k][:, :, :].rearrange("p e f -> p (e f)"), 2.0 ** SPLIT,
                                           w[0][:, :, :, :].rearrange("p e c d -> p (e c d)"),
                                           ALU.mult, ALU.subtract).then_inc(low, 1)
        dve.wait_ge(low, 2)


ROUTE = ["m1", "eq1", "cand1", "i1", "O1", "L2", "m2", "eq2", "cand2", "i2", "O2", "d", "mask", "tot", "cum", "excl",
         "base", "cend", "cnt", "over", "nb", "bend", "bstart", "adj", "slot", "p1", "pos1", "p2", "pos2",
         "tile0", "tile1", "tile", "col", "past", "blk", "blki", "den", "w1", "w2",
         "sums_kept", "one", "inverse", "row0", "row1", "row", "held", "id0", "id", "id_held", "second", "token0", "token",
         "empty", "spare", "target", "targeti"]


def ffn(nc, ctx, A, X, ident, bank, name, src, dst):
    with ExitStack() as tmp:
        def sb(n, shape, dt=F32):
            return tmp.enter_context(nc.sbuf_tensor(f"{name}_{n}", shape, dt))

        def sem(n):
            return own.get(f"{name}_{n}")

        own = Semaphores(nc)

        x_all = sb("x_all", [P, NT, E])
        xn = [sb(f"xn{p}", [P, Q, E]) for p in range(2)]
        eps = sb("eps", [P, 1])
        st = [sb(f"st{p}", [P, Q, 6]) for p in range(2)]
        mv = [sb(f"mv{p}", [P, Q, 2]) for p in range(2)]
        lnv, rstd = ([sb(f"{n}{p}", [P, Q]) for p in range(2)] for n in ("lnv", "rstd"))
        xT = [sb(f"xT{p}", [P, W]) for p in range(2)]
        L, eq, cand, O1, O2, L2, base, prod, cum, tot = (sb(n, [P, NT, NX]) for n in
                                                         ("L", "eq", "cand", "O1", "O2", "L2", "base", "prod", "cum", "tot"))
        m1, m2, i1, i2, d, ex, den, g1, g2 = (sb(n, [P, NT]) for n in
                                                      ("m1", "m2", "i1", "i2", "d", "ex", "den", "g1", "g2"))
        mask = sb("mask", [P, NX, NT], F16)
        ce = sb("ce", [P, NX + 1])
        cnt, nb, bend, bstart, adj = (sb(n, [P, NX]) for n in ("cnt", "nb", "bend", "bstart", "adj"))
        over = sb("over", [P, NX, CB])
        past = sb("past", [P, NB, NX])
        blk = sb("blk", [P, NB])
        pos, tile, col = (sb(n, [P, 2, NT]) for n in ("pos", "tile", "col"))
        isb = [sb(f"isb{p}", [P, TQ, P], F16) for p in range(2)]
        isa = [sb(f"isa{p}", [P, TQ, 2, NA], F16) for p in range(2)]
        found = sb("found", [P, 2, NA])
        one, inverse, trow, held, tid, second, token, empty, target = (sb(n, [P, NA]) for n in (
            "one", "inverse", "trow", "held", "tid", "second", "token", "empty", "target"))
        tokeni, targeti = (sb(n, [P, NA], mybir.dt.int32) for n in ("tokeni", "targeti"))
        blki = sb("blki", [P, NB], mybir.dt.int32)
        xs = [sb(f"xs{p}", [P, BR, P]) for p in range(AHEAD)]
        xh, xl = ([sb(f"{n}{p}", [P, BS], F16) for p in range(2)] for n in ("xh", "xl"))
        h32 = [sb(f"h32_{p}", [P, FC, BS]) for p in range(2)]
        hh, hl = ([sb(f"{n}{p}", [P, FC, BS], F16) for p in range(2)] for n in ("hh", "hl"))
        yT = [sb(f"yT{p}", [P, BS]) for p in range(2)]
        ys = [sb(f"ys{p}", [P, BR, P]) for p in range(AHEAD)]
        yg = [sb(f"yg{k}", [P, 2, Q, E]) for k in range(AHEAD)]

        (eps_set, aggr, rstd_s, xnr, xTp, xTr, logits, L_cp, route, ex_s, sums,
         xT_ps, x_high, x_low, h_ps, h_relu, h_high, h_low, y_ps, yT_s, yR_ps, ys_s, halved, added) = (
            sem(n) for n in ("eps_set", "aggregated", "rstd", "normed", "xT_in_psum", "xT_ready", "logits", "logits_kept",
                             "route", "exps", "sums", "block_xT", "x_high", "x_low", "h_in_psum",
                             "h_relu", "h_high", "h_low", "y_in_psum", "yT_ready", "y_rows", "ys_ready", "halved",
                             "added"))
        onehots, rowed, counted = (sem(n) for n in ("onehots", "rowed", "counted"))
        stats = sem("stats")
        stats_seen = sem("stats_seen")
        x_part = [sem(f"x_part{k}") for k in range(8)]
        x_in = sem("x_in")
        xn_kept = [sem(f"xn_kept{p}") for p in range(2)]
        fetched, scattered, before = X.fetched, X.scattered, 32 * (NB // AHEAD) * X.calls
        X.calls += 1
        got = [sem(f"got{g}") for g in range(AHEAD)]
        stored = sem("stored")

        dstt = dst.rearrange("b t e -> (b t) e").rearrange("(g q p) e -> g p q e", q=Q, p=P)
        normt = A["normed"].rearrange("(g q p) e -> g p q e", q=Q, p=P)
        pickt = A["picked"][0:2 * B * T, :].rearrange("(k g q p) e -> k g p q e", k=2, q=Q, p=P)
        NG = NT // Q
        block = tmp.enter_context(nc.Block())
        R = {n: k + 1 for k, n in enumerate(ROUTE)}

        def pairs(eng, count, step):
            for p in range(2):
                step(0, p)
            with eng.Fori(1, count // 2 - 1) as i:
                for p in range(2):
                    step(i, p)
            for p in range(2):
                step(count // 2 - 1, p)

        def quads(eng, step):
            for p in range(AHEAD):
                step(0, p)
            with eng.Fori(1, NB // AHEAD - 1) as i:
                for p in range(AHEAD):
                    step(i, p)
            for p in range(AHEAD):
                step(NB // AHEAD - 1, p)

        def back_by(i, p, n):
            return (i, p - n) if p >= n else (i - 1, p - n + AHEAD)

        def last_group(i, p):
            return isinstance(i, int) and i == NG // 2 - 1 and p == 1

        def early(x):
            return isinstance(x, int) and x < 2

        @block.sync
        def _(sp):
            parts = len(x_part)
            for k in range(parts):
                sp.dma_start(x_all[:, NT // parts * k:NT // parts * (k + 1), :],
                             src.rearrange("b t e -> (b t) e").rearrange("(k n p) e -> k p n e", k=parts, p=P)[k]
                             ).then_inc(x_part[k], 16)
            for k in range(parts):
                sp.wait_ge(x_part[k], 16)
                sp.sem_inc(x_in, NG // parts)
            for k in range(AHEAD):
                sp.wait_ge(scattered[k], before + 32 * (NB // AHEAD))
            for g in range(NG + AHEAD):
                if g < NG:
                    if g >= AHEAD:
                        sp.wait_ge(added, g - AHEAD + 1)
                    for k in range(2):
                        sp.dma_start(yg[g % AHEAD][:, k, :, :], pickt[k, g]).then_inc(got[g % AHEAD], 16)
                if g >= AHEAD:
                    sp.wait_ge(added, g - AHEAD + 1)
                    sp.dma_start(dstt[g - AHEAD], x_all[:, Q * (g - AHEAD):Q * (g - AHEAD + 1), :]).then_inc(stored, 16)
            sp.wait_ge(stored, 16 * NG)

        @block.gpsimd
        def _(pool):
            pool.memset(eps[:, :], LN_EPS).then_inc(eps_set, 1)
            pool.memset(ce[:, 0:1], 0.0).then_inc(eps_set, 1)

            def fetch(j):
                for r in range(BR):
                    pool.indirect_dma_start(xs[j % AHEAD][:, r, :], None, A["normed"], bass.IndirectOffsetOnAxis(
                        ap=tokeni[:, BR * j + r:BR * j + r + 1], axis=0)).then_inc(fetched[j % AHEAD], 16)

            def put(j):
                pool.wait_ge(ys_s, j + 1)
                for r in range(BR):
                    pool.indirect_dma_start(A["picked"], bass.IndirectOffsetOnAxis(
                        ap=targeti[:, BR * j + r:BR * j + r + 1], axis=0),
                        ys[j % AHEAD][:, r, :], None).then_inc(scattered[j % AHEAD], 16)

            for p in range(2):
                pool.wait_ge(xn_kept[p], 16 * (NG // 2))
            pool.wait_ge(route, R["token"])
            for j in range(AHEAD):
                fetch(j)
            pool.wait_ge(route, R["targeti"])
            for j in range(NB + LAG):
                if j + AHEAD < NB:
                    pool.wait_ge(xT_ps, j + 1)
                    fetch(j + AHEAD)
                if j >= LAG:
                    put(j - LAG)

        @block.tensor
        def _(pe):
            def turn_tokens(i, p):
                g = 2 * i + p
                pe.wait_ge(xnr, g + 1)
                if not early(g):
                    pe.wait_ge(xTr, g - 1)
                for q in range(Q):
                    ins = nc.tensor.transpose(bank[6 * p][:, P * q:P * q + P], xn[p][:, q, :], ident[:, :])
                ins.then_inc(xTp, 1)

            def logits_of(i, p):
                g = 2 * i + p
                pe.wait_ge(xTr, g + 1)
                if not early(g):
                    pe.wait_ge(L_cp, g - 1)
                for q in range(Q):
                    ins = nc.tensor.matmul(bank[1 + p][:, NX * q:NX * q + NX], xT[p][:, P * q:P * q + P], X.wgate[:, :],
                                           start=True, stop=True)
                ins.then_inc(logits, 1)

            turn_tokens(0, 0)

            def step(i, p):
                if not last_group(i, p):
                    turn_tokens(*((i, 1) if p == 0 else (i + 1, 0)))
                logits_of(i, p)
            pairs(pe, NG, step)
            pe.wait_ge(route, R["mask"])
            mk = mask[:, :, :].rearrange("p e t -> p (e t)")
            nc.tensor.matmul(bank[3][:, :], X.before[:, :], mk, start=True, stop=True).then_inc(sums, 1)
            nc.tensor.matmul(bank[4][:, :], X.all16[:, :], mk, start=True, stop=True).then_inc(sums, 1)

            def find(i, p):
                u = 2 * i + p
                pe.wait_ge(rowed, u + 1)
                for q in range(TQ):
                    ins = nc.tensor.matmul(bank[5][:, 0:2 * NA], isb[p][:, q, :], isa[p][:, q, :, :].rearrange("p a n -> p (a n)"),
                                           start=(isinstance(u, int) and u == 0 and q == 0),
                                           stop=(isinstance(u, int) and u == 2 * NT // TQ - 1 and q == TQ - 1))
                ins.then_inc(counted, 1)
            pairs(pe, 2 * NT // TQ, find)
            pe.wait_ge(route, R["sums_kept"])
            ps_x, ps_yr = bank[0], bank[1]
            ps_h = [bank[2:4], bank[4:6]]
            ps_y = bank[6:8]

            def expert(j):
                return pe.value_load(blki[0:1, j:j + 1] if isinstance(j, int) else blki[0:1, bass.ds(j, 1)],
                                     min_val=0, max_val=NX - 1)

            def turn(i, p):
                j, b = AHEAD * i + p, p % 2
                pe.wait_ge(fetched[p], before + 32 * (i + 1))
                if not (isinstance(j, int) and j == 0):
                    pe.wait_ge(x_low, j)
                for r in range(BR):
                    ins = nc.tensor.transpose(ps_x[:, P * r:P * r + P], xs[p][:, r, :], ident[:, :])
                ins.then_inc(xT_ps, 1)

            def up(i, p):
                j, b = AHEAD * i + p, p % 2
                e = expert(j)
                pe.wait_ge(x_low, j + 1)
                if not early(j):
                    pe.wait_ge(h_relu, FC * (j - 1))
                for c in range(FC):
                    o = ps_h[b][c // 2][:, BS * (c % 2):BS * (c % 2) + BS]
                    for n, (w, x) in enumerate(((0, xh), (0, xl), (1, xh))):
                        ins = nc.tensor.matmul(o, X.w1[w][:, bass.ds(e, 1), c, :].rearrange("p o d -> p (o d)"), x[b][:, :],
                                               start=(n == 0), stop=(n == 2))
                    ins.then_inc(h_ps, 1)

            def down(i, p):
                j, b = AHEAD * i + p, p % 2
                e = expert(j)
                if not early(j):
                    pe.wait_ge(yT_s, j - 1)
                for c in range(FC):
                    if c % 2 == 0:
                        pe.wait_ge(h_low, 2 * j + c // 2 + 1)
                    for n, (w, h) in enumerate(((0, hh), (0, hl), (1, hh))):
                        ins = nc.tensor.matmul(ps_y[b][:, 0:BS], X.w2[w][:, bass.ds(e, 1), c, :].rearrange("p o d -> p (o d)"),
                                               h[b][:, c, :], start=(c == 0 and n == 0), stop=(c == FC - 1 and n == 2))
                ins.then_inc(y_ps, 1)

            def back(i, p):
                j, b = AHEAD * i + p, p % 2
                pe.wait_ge(yT_s, j + 1)
                if not (isinstance(j, int) and j == 0):
                    pe.wait_ge(ys_s, j)
                for r in range(BR):
                    ins = nc.tensor.transpose(ps_yr[:, P * r:P * r + P], yT[b][:, P * r:P * r + P], ident[:, :])
                ins.then_inc(yR_ps, 1)

            turn(0, 0)

            def step(i, p):
                j = AHEAD * i + p
                up(i, p)
                if not (isinstance(j, int) and j == NB - 1):
                    turn(*((i, p + 1) if p + 1 < AHEAD else (i + 1, 0)))
                if not (isinstance(j, int) and j < 1):
                    down(*back_by(i, p, 1))
                if not (isinstance(j, int) and j < 2):
                    back(*back_by(i, p, 2))
            quads(pe, step)
            back(NB // AHEAD - 1, AHEAD - 2)
            down(NB // AHEAD - 1, AHEAD - 1)
            back(NB // AHEAD - 1, AHEAD - 1)

        @block.scalar
        def _(act):
            nc.scalar.preload_act_table_set("natural_log_exp_and_others")
            act.wait_ge(eps_set, 2)

            def norm(i, p):
                g = 2 * i + p
                act.wait_ge(aggr, g + 1)
                nc.scalar.activation(lnv[p][:, :], mv[p][:, :, 1], ACT.Ln, bias=eps[:, :]).then_inc(rstd_s, 1)
                act.wait_ge(rstd_s, 2 * g + 1)
                nc.scalar.activation(rstd[p][:, :], lnv[p][:, :], ACT.Exp, scale=-0.5).then_inc(rstd_s, 1)

            def copy(i, p):
                g = 2 * i + p
                act.wait_ge(xTp, g + 1)
                if not early(g):
                    act.wait_ge(logits, g - 1)
                nc.scalar.activation(xT[p][:, :], bank[6 * p][:, :], ACT.Copy).then_inc(xTr, 1)
                act.wait_ge(xnr, g + 1)
                nc.scalar.dma_start(normt[g], xn[p][:, :, :]).then_inc(xn_kept[p], 16)

            norm(0, 0)

            def step(i, p):
                if not last_group(i, p):
                    norm(*((i, 1) if p == 0 else (i + 1, 0)))
                copy(i, p)
            pairs(act, NG, step)
            act.wait_ge(route, R["d"])
            nc.scalar.activation(ex[:, :], d[:, :], ACT.Exp).then_inc(ex_s, 1)

            def rows(i, p):
                act.wait_ge(onehots, 2 * i + p + 1)
                nc.scalar.activation(isa[p][:, :, 1, :], isa[p][:, :, 0, :], ACT.Copy, scale=X.row[:, :]).then_inc(rowed, 1)
            pairs(act, 2 * NT // TQ, rows)
            act.wait_ge(route, R["blki"])

            def high(i, p):
                j, b = AHEAD * i + p, p % 2
                act.wait_ge(xT_ps, j + 1)
                if not early(j):
                    act.wait_ge(h_ps, FC * (j - 1))
                nc.scalar.activation(xh[b][:, :], bank[0][:, 0:BS], ACT.Copy).then_inc(x_high, 1)

            def relu(i, p):
                j, b = AHEAD * i + p, p % 2
                e = act.value_load(blki[0:1, j:j + 1] if isinstance(j, int) else blki[0:1, bass.ds(j, 1)],
                                   min_val=0, max_val=NX - 1)
                if not early(j):
                    act.wait_ge(h_low, 2 * (j - 1))
                for c in range(FC):
                    act.wait_ge(h_ps, FC * j + c // 2 * 2 + 2)
                    nc.scalar.activation(h32[b][:, c, :], bank[2 + 2 * b + c // 2][:, BS * (c % 2):BS * (c % 2) + BS],
                                         ACT.Relu, bias=X.b1[:, bass.ds(e, 1), c],
                                         scale=2.0 ** (HSPLIT - SPLIT)).then_inc(h_relu, 1)

            def y_out(i, p):
                j, b = AHEAD * i + p, p % 2
                e = act.value_load(blki[0:1, j:j + 1] if isinstance(j, int) else blki[0:1, bass.ds(j, 1)],
                                   min_val=0, max_val=NX - 1)
                act.wait_ge(y_ps, j + 1)
                if not early(j):
                    act.wait_ge(yR_ps, j - 1)
                nc.scalar.activation(yT[b][:, :], bank[6 + b][:, 0:BS], ACT.Identity, bias=X.b2[:, bass.ds(e, 1)],
                                     scale=2.0 ** (-HSPLIT - SPLIT)).then_inc(yT_s, 1)

            high(0, 0)

            def step(i, p):
                j = AHEAD * i + p
                relu(i, p)
                if not (isinstance(j, int) and j == NB - 1):
                    high(*((i, p + 1) if p + 1 < AHEAD else (i + 1, 0)))
                if not (isinstance(j, int) and j == 0):
                    y_out(*back_by(i, p, 1))
            quads(act, step)
            y_out(NB // AHEAD - 1, AHEAD - 1)

        @block.vector
        def _(dve):
            v = nc.vector
            dve.wait_ge(eps_set, 2)

            def measure(i, p):
                g = 2 * i + p
                dve.wait_ge(x_in, g + 1)
                for q in range(Q):
                    ins = v.bn_stats(st[p][:, q, :], x_all[:, bass.ds(g * Q + q, 1), :].rearrange("p o e -> p (o e)"))
                ins.then_inc(stats, 1)
                dve.wait_ge(stats, g + 1)
                dve.sem_inc(stats_seen, 1)
                for q in range(Q):
                    ins = v.bn_aggr(mv[p][:, q, :], st[p][:, q, :])
                ins.then_inc(aggr, 1)

            def normalise(i, p):
                g = 2 * i + p
                dve.wait_ge(rstd_s, 2 * g + 2)
                if not early(g):
                    dve.wait_ge(xTp, g - 1)
                    dve.wait_ge(xn_kept[p], 16 * i)
                for q in range(Q):
                    ins = v.tensor_scalar(xn[p][:, q, :],
                                          x_all[:, bass.ds(g * Q + q, 1), :].rearrange("p o e -> p (o e)"),
                                          mv[p][:, q, 0:1], rstd[p][:, q:q + 1], ALU.subtract, ALU.mult)
                ins.then_inc(xnr, 1)

            def keep(i, p):
                g = 2 * i + p
                dve.wait_ge(logits, g + 1)
                v.tensor_copy(L[:, bass.ds(g * Q, Q), :].rearrange("p q e -> p (q e)"), bank[1 + p][:, 0:NX * Q]).then_inc(L_cp, 1)

            measure(0, 0)

            def step(i, p):
                if not last_group(i, p):
                    measure(*((i, 1) if p == 0 else (i + 1, 0)))
                normalise(i, p)
                if not early(2 * i + p):
                    keep(i - 1, p)
            pairs(dve, NG, step)
            keep(NG // 2 - 1, 0)
            keep(NG // 2 - 1, 1)
            dve.wait_ge(L_cp, NG)

            def did(n, ins):
                ins.then_inc(route, 1)
                dve.wait_ge(route, R[n])

            def te(x):
                return x[:, :].unsqueeze(2).to_broadcast([P, NT, NX])

            def et(x):
                return x.rearrange("p t e -> p e t")

            def e_m8():
                return X.expert_m8[:, :].unsqueeze(1).to_broadcast([P, NT, NX])

            for n, (lg, m, i, O) in enumerate(((L, m1, i1, O1), (L2, m2, i2, O2))):
                k = str(n + 1)
                did("m" + k, v.tensor_reduce(m[:, :], lg[:, :, :], AX_X, ALU.max))
                did("eq" + k, v.tensor_tensor(eq[:, :, :], lg[:, :, :], te(m), ALU.is_equal))
                did("cand" + k, v.tensor_tensor(cand[:, :, :], eq[:, :, :], e_m8(), ALU.mult))
                did("i" + k, v.tensor_reduce(i[:, :], cand[:, :, :], AX_X, ALU.min))
                did("O" + k, v.tensor_tensor(O[:, :, :], e_m8(), te(i), ALU.is_equal))
                if n == 0:
                    did("L2", v.scalar_tensor_tensor(L2[:, :, :], O[:, :, :], -3e38, L[:, :, :], ALU.mult, ALU.add))
            did("d", v.tensor_tensor(d[:, :], m2[:, :], m1[:, :], ALU.subtract))
            did("mask", v.tensor_tensor(mask[:, :, :], et(O1[:, :, :]), et(O2[:, :, :]), ALU.add))
            flat = "p a b -> p (a b)"

            def as_et(x):
                return x[:, :, :].rearrange(flat).rearrange("p (e t) -> p e t", e=NX)
            dve.wait_ge(sums, 2)
            did("tot", v.tensor_copy(tot[:, :, :].rearrange(flat), bank[4][:, :]))
            did("cum", v.tensor_tensor_scan(cum[:, :, :].rearrange(flat), X.onesrow[:, :], tot[:, :, :].rearrange(flat),
                                            0.0, ALU.mult, ALU.add))
            did("excl", v.tensor_tensor(prod[:, :, :].rearrange(flat), cum[:, :, :].rearrange(flat),
                                        tot[:, :, :].rearrange(flat), ALU.subtract))
            did("base", v.tensor_tensor(base[:, :, :].rearrange(flat), bank[3][:, :], prod[:, :, :].rearrange(flat), ALU.add))
            did("cend", v.tensor_copy(ce[:, 1:NX + 1], as_et(cum)[:, :, NT - 1]))
            did("cnt", v.tensor_tensor(cnt[:, :], ce[:, 1:NX + 1], ce[:, 0:NX], ALU.subtract))
            did("over", v.tensor_tensor(over[:, :, :], cnt[:, :].unsqueeze(2).to_broadcast([P, NX, CB]),
                                        X.slot_row[:, :].unsqueeze(1).to_broadcast([P, NX, CB]), ALU.is_gt))
            did("nb", v.tensor_reduce(nb[:, :], over[:, :, :], AX_X, ALU.add))
            did("bend", v.tensor_tensor_scan(bend[:, :], X.onesrow[:, 0:NX], nb[:, :], 0.0, ALU.mult, ALU.add))
            did("bstart", v.tensor_tensor(bstart[:, :], bend[:, :], nb[:, :], ALU.subtract))
            did("adj", v.scalar_tensor_tensor(adj[:, :], bstart[:, :], float(BS), ce[:, 0:NX], ALU.mult, ALU.subtract))
            did("slot", v.tensor_tensor(as_et(prod), as_et(base), adj[:, :].unsqueeze(2).to_broadcast([P, NX, NT]), ALU.add))
            for k, O in enumerate((O1, O2)):
                did(f"p{k + 1}", v.tensor_tensor(cand[:, :, :], O[:, :, :], as_et(prod).rearrange("p e t -> p t e"), ALU.mult))
                did(f"pos{k + 1}", v.tensor_reduce(pos[:, k, :], cand[:, :, :], AX_X, ALU.add))
            did("tile0", v.tensor_scalar(tile[:, :, :], pos[:, :, :], 1.0 / P, -(P - 1) / (2.0 * P), ALU.mult, ALU.add))
            did("tile1", v.tensor_scalar(tile[:, :, :], tile[:, :, :], ROUND, None, ALU.add))
            did("tile", v.tensor_scalar(tile[:, :, :], tile[:, :, :], -ROUND, None, ALU.add))
            did("col", v.scalar_tensor_tensor(col[:, :, :], tile[:, :, :], -float(P), pos[:, :, :], ALU.mult, ALU.add))
            tile_of, col_of = (x[:, :, :].rearrange("p k t -> p (k t)") for x in (tile, col))

            def onehot(i, p):
                u = 2 * i + p
                if not early(u):
                    dve.wait_ge(counted, u - 1)
                for q in range(TQ):
                    at = bass.ds(u * TQ + q, 1)
                    v.tensor_scalar(isb[p][:, q, :], X.slot_col[:, :], col_of[:, at], None, ALU.is_equal)
                    ins = v.tensor_scalar(isa[p][:, q, 0, :], X.slot_tile[:, :], tile_of[:, at], X.nth[:, at],
                                          ALU.is_equal, ALU.mult)
                ins.then_inc(onehots, 1)
            pairs(dve, 2 * NT // TQ, onehot)
            did("past", v.tensor_tensor(past[:, :, :], X.block_row[:, :].unsqueeze(2).to_broadcast([P, NB, NX]),
                                        bend[:, :].unsqueeze(1).to_broadcast([P, NB, NX]), ALU.is_ge))
            did("blk", v.tensor_reduce(blk[:, :], past[:, :, :], AX_X, ALU.add))
            did("blki", v.tensor_scalar(blki[:, :], blk[:, :], NX - 1.0, None, ALU.min))
            dve.wait_ge(ex_s, 1)
            did("den", v.tensor_scalar(den[:, :], ex[:, :], 1.0, None, ALU.add))
            did("w1", v.reciprocal(g1[:, :], den[:, :]))
            did("w2", v.tensor_tensor(g2[:, :], ex[:, :], g1[:, :], ALU.mult))
            dve.wait_ge(counted, 2 * NT // TQ)
            did("sums_kept", v.tensor_copy(found[:, :, :].rearrange("p a n -> p (a n)"), bank[5][:, 0:2 * NA]))
            n = found[:, 0, :]
            did("one", v.tensor_scalar(one[:, :], n, 1.0, None, ALU.max))
            did("inverse", v.reciprocal(inverse[:, :], one[:, :]))
            did("row0", v.tensor_tensor(trow[:, :], found[:, 1, :], inverse[:, :], ALU.mult))
            did("row1", v.tensor_scalar(trow[:, :], trow[:, :], ROUND, None, ALU.add))
            did("row", v.tensor_scalar(trow[:, :], trow[:, :], -ROUND, None, ALU.add))
            did("held", v.tensor_scalar(held[:, :], n, 0.5, None, ALU.is_gt))
            did("id0", v.tensor_scalar(tid[:, :], n, float(P), -float(P), ALU.mult, ALU.add))
            did("id", v.tensor_tensor(tid[:, :], tid[:, :], trow[:, :], ALU.add))
            did("id_held", v.tensor_tensor(tid[:, :], tid[:, :], held[:, :], ALU.mult))
            did("second", v.tensor_scalar(second[:, :], tid[:, :], B * T - 0.5, -float(B * T), ALU.is_gt, ALU.mult))
            did("token0", v.tensor_tensor(token[:, :], tid[:, :], second[:, :], ALU.add))
            did("token", v.tensor_copy(tokeni[:, :], token[:, :]))
            did("empty", v.tensor_scalar(empty[:, :], n, 0.5, None, ALU.is_lt))
            did("spare", v.tensor_tensor(empty[:, :], empty[:, :], X.spare[:, :], ALU.mult))
            did("target", v.tensor_tensor(target[:, :], tid[:, :], empty[:, :], ALU.add))
            did("targeti", v.tensor_copy(targeti[:, :], target[:, :]))

            def x_lo(i, p):
                j, b = AHEAD * i + p, p % 2
                dve.wait_ge(x_high, j + 1)
                v.tensor_tensor(xl[b][:, :], bank[0][:, 0:BS], xh[b][:, :], ALU.subtract).then_inc(x_low, 1)

            def h_split(i, p, c):
                j, b = AHEAD * i + p, p % 2
                dve.wait_ge(h_relu, FC * j + 2 * c + 2)
                if not early(j):
                    dve.wait_ge(y_ps, j - 1)
                v.tensor_copy(hh[b][:, 2 * c:2 * c + 2, :], h32[b][:, 2 * c:2 * c + 2, :]).then_inc(h_high, 1)
                dve.wait_ge(h_high, 2 * j + c + 1)
                v.tensor_tensor(hl[b][:, 2 * c:2 * c + 2, :], h32[b][:, 2 * c:2 * c + 2, :], hh[b][:, 2 * c:2 * c + 2, :],
                                ALU.subtract).then_inc(h_low, 1)

            def rows(i, p):
                j = AHEAD * i + p
                dve.wait_ge(yR_ps, j + 1)
                if not (isinstance(j, int) and j < AHEAD):
                    dve.wait_ge(scattered[p], before + 32 * i)
                v.tensor_copy(ys[p][:, :, :].rearrange("p r d -> p (r d)"), bank[1][:, 0:BS]).then_inc(ys_s, 1)

            x_lo(0, 0)

            def step(i, p):
                j = AHEAD * i + p
                h_split(i, p, 0)
                if not (isinstance(j, int) and j == NB - 1):
                    x_lo(*((i, p + 1) if p + 1 < AHEAD else (i + 1, 0)))
                h_split(i, p, 1)
                if not early(j):
                    rows(*back_by(i, p, 2))
            quads(dve, step)
            rows(NB // AHEAD - 1, AHEAD - 2)
            rows(NB // AHEAD - 1, AHEAD - 1)
            for g in range(NG):
                dve.wait_ge(got[g % AHEAD], 32 * (g // AHEAD + 1))
                for k, w in enumerate((g1, g2)):
                    if k == 1:
                        dve.wait_ge(halved, g + 1)
                    for q in range(Q):
                        t = Q * g + q
                        ins = v.scalar_tensor_tensor(x_all[:, t, :], yg[g % AHEAD][:, k, q, :], w[:, t:t + 1],
                                                     x_all[:, t, :], ALU.mult, ALU.add)
                    ins.then_inc((halved, added)[k], 1)
    own.release()


DL = 32
TB = T // P
ROW = 32
AS = 4.0
SW = P + 2 * P
NEG = -1e30


class Attention:

    def __init__(self, sb):
        self.wq = [sb(f"wq_{n}", [P, HG, P], F16) for n in "hl"]
        self.wk = [sb(f"wk_{n}", [P, HG, P], F16) for n in "hl"]
        self.wv = [sb(f"wv_{n}", [P, P], F16) for n in "hl"]
        self.wo = sb("wo", [P, P])
        self.q_low = sb("q_low", [P, 1])
        self.k_low = sb("k_low", [P, 1])
        self.k_bias = sb("k_const", [P, 1])
        self.ident16 = sb("ident16", [P, P], F16)
        self.identb = sb("identb", [P, P], BF16)
        self.mask_ts = sb("mask_ts", [P, P], BF16)
        self.mask_st = sb("mask_st", [P, P], BF16)


def setup_attention(nc, ctx, tmp, block, A, X, ident, head_ones, bank):
    def sb(name, shape, dt=F32):
        return tmp.enter_context(nc.sbuf_tensor(name, shape, dt))

    def sem(name):
        return ctx.enter_context(nc.semaphore(name))

    wqkv = sb("wqkv", [P, 3 * P])
    lq = sb("lq", [P, DL])
    lk = sb("lk", [P, DL])
    core = sb("core", [P, DL])
    lqT = sb("lqT", [DL, P])
    lkT = sb("lkT", [DL, P])
    wqT = sb("wqT", [P, P])
    fold = sb("fold", [P, P])
    wqf = sb("wqf", [P, P])
    rowi = sb("rowi", [P, P], mybir.dt.int32)
    rows = sb("rows", [P, P])
    cls = sb("cls", [P, 3])
    loaded, made, chosen, steps, pe_steps, act_steps = (sem("att_" + n) for n in
                                                        ("loaded", "made", "chosen", "steps", "pe_steps", "act_steps"))

    @block.sync
    def _(sp):
        sp.dma_start(wqkv[:, :], A["W_qkv"]).then_inc(loaded, 16)
        sp.dma_start(X.wo[:, :], A["W_o"]).then_inc(loaded, 16)
        sp.dma_start(lq[:, :], A["W_q_lsr"].rearrange("h d r -> (h d) r")).then_inc(loaded, 16)
        sp.dma_start(lk[:, :], A["W_k_lsr"].rearrange("h d r -> (h d) r")).then_inc(loaded, 16)
        for h in range(H):
            sp.dma_start(core[D * h:D * h + D, :], A["core"][h, :].partition_broadcast(D)).then_inc(loaded, 16)

    @block.gpsimd
    def _(pool):
        for t in (X.wq[0], X.wq[1], X.wk[0], X.wk[1]):
            pool.memset(t[:, :, :], 0.0).then_inc(made, 1)
        pool.memset(X.mask_ts[:, :], 0.0).then_inc(made, 1)
        pool.memset(X.mask_st[:, :], 0.0).then_inc(made, 1)
        pool.wait_ge(made, 6)
        pool.affine_select(out=X.mask_ts[:, :], in_=X.mask_ts[:, :], compare_op=ALU.is_ge, fill=NEG, base=0,
                           pattern=[[-1, P]], channel_multiplier=1).then_inc(made, 1)
        pool.affine_select(out=X.mask_st[:, :], in_=X.mask_st[:, :], compare_op=ALU.is_ge, fill=NEG, base=0,
                           pattern=[[1, P]], channel_multiplier=-1).then_inc(made, 1)
        pool.iota(rowi[:, 0:1], pattern=[[0, 1]], base=0, channel_multiplier=1).then_inc(made, 1)

    @block.tensor
    def _(pe):
        pe.wait_ge(steps, 1)
        nc.tensor.transpose(bank[0][0:DL, 0:P], lq[:, :], ident[:, :])
        nc.tensor.transpose(bank[1][0:DL, 0:P], lk[:, :], ident[:, :])
        nc.tensor.transpose(bank[2][:, 0:P], wqkv[:, 0:P], ident[:, :]).then_inc(pe_steps, 1)
        pe.wait_ge(steps, 4)
        nc.tensor.matmul(bank[3][:, 0:P], lqT[:, :], lkT[:, :], start=True, stop=True).then_inc(pe_steps, 1)
        pe.wait_ge(steps, 5)
        nc.tensor.matmul(bank[4][:, 0:P], wqT[:, :], fold[:, :], start=True, stop=True).then_inc(pe_steps, 1)

    @block.vector
    def _(dve):
        v = nc.vector
        dve.wait_ge(loaded, 16 * (4 + H))
        n = [0]

        def did(ins):
            ins.then_inc(steps, 1)
            n[0] += 1
            dve.wait_ge(steps, n[0])
        did(v.scalar_tensor_tensor(lq[:, :], lq[:, :], DL ** -0.5, core[:, :], ALU.mult, ALU.mult))
        dve.wait_ge(pe_steps, 1)
        did(v.tensor_copy(lqT[:, :], bank[0][0:DL, 0:P]))
        did(v.tensor_copy(lkT[:, :], bank[1][0:DL, 0:P]))
        did(v.tensor_copy(wqT[:, :], bank[2][:, 0:P]))
        dve.wait_ge(pe_steps, 2)
        did(v.tensor_tensor(fold[:, :], bank[3][:, 0:P], head_ones[:, :], ALU.mult))
        dve.wait_ge(pe_steps, 3)
        did(v.tensor_scalar(wqf[:, :], bank[4][:, 0:P], 2.0 ** AS, None, ALU.mult))
        did(v.tensor_scalar(wqkv[:, :], wqkv[:, :], 2.0 ** AS, None, ALU.mult))
        dve.wait_ge(made, 9)

        def hd(x):
            return x.rearrange("p (h d) -> p h d", d=D)

        for w, src in ((X.wq, wqf[:, :]), (X.wk, wqkv[:, P:2 * P])):
            for part in range(3):
                o = [t[:, :, :].rearrange("p g (h r) -> p (g h) r", r=ROW)[:, :, D * part:D * part + D] for t in w]
                did(v.tensor_copy(o[0], hd(src)))
                did(v.tensor_tensor(o[1], hd(src), o[0], ALU.subtract))
        did(v.tensor_copy(X.wv[0][:, :], wqkv[:, 2 * P:]))
        did(v.tensor_tensor(X.wv[1][:, :], wqkv[:, 2 * P:], X.wv[0][:, :], ALU.subtract))
        did(v.tensor_copy(X.ident16[:, :], ident[:, :]))
        did(v.tensor_copy(X.identb[:, :], ident[:, :]))
        did(v.tensor_copy(rows[:, 0:1], rowi[:, 0:1]))
        for k in range(P // ROW - 1):
            did(v.tensor_scalar(rows[:, 1:2], rows[:, 0:1], float(ROW), -float(ROW), ALU.is_ge, ALU.mult))
            did(v.tensor_tensor(rows[:, 0:1], rows[:, 0:1], rows[:, 1:2], ALU.add))
        for k in range(1, 4):
            did(v.tensor_scalar(cls[:, k - 1:k], rows[:, 0:1], float(D * k), None, ALU.is_ge))
        did(v.tensor_scalar(rows[:, 2:3], rows[:, 0:1], float(3 * D + 2), None, ALU.is_ge))
        did(v.tensor_tensor(X.q_low[:, :], cls[:, 2:3], cls[:, 1:2], ALU.subtract))
        did(v.tensor_tensor(X.k_low[:, :], cls[:, 1:2], cls[:, 0:1], ALU.subtract))
        did(v.tensor_tensor(rows[:, 3:4], cls[:, 2:3], rows[:, 2:3], ALU.subtract))
        did(v.tensor_tensor(X.k_low[:, :], X.k_low[:, :], rows[:, 3:4], ALU.add))
        did(v.tensor_scalar(X.k_bias[:, :], rows[:, 3:4], 2.0 ** (2 * AS), None, ALU.mult))


FRONT_DVE_AT = dict(stats0=5, stats1=5, aggr0=6, aggr1=6, xn0=7, xn1=7, x_low=13)
FRONT_PE_AT = 8
FRONT_ACT_AT = dict(rstd_log=7, rstd=7, x_high=11)
PROJ_AT = dict(q01=0, q23=1, k01=2, k23=3, v=3)
SCORES_AT = [5, 5, 6, 6, 7, 7, 8, 8, 9, 9, 10, 10, 11, 11, 12, 12]
MAX_UNTIL = SCORES_AT[-1]
TURN_AT = 14
MAXI_AT = dict(larger=12, m=12, high=12, low=12, add0=13, add1=13)
TAIL_DVE_AT = dict(rec=2, yn=2, out=8)
TAIL_TURN_AT, TAIL_ACT_AT, TAIL_OUT_AT = 5, 5, 8
PV_LAG = 3
FRONT_DVE, FRONT_ACT, PROJ, MAXI, TAIL_DVE = (list(x) for x in (FRONT_DVE_AT, FRONT_ACT_AT, PROJ_AT, MAXI_AT, TAIL_DVE_AT))


def attention(nc, ctx, A, X, ident, bank, src, dst):
    with ExitStack() as tmp:
        def sb(n, shape, dt=F32):
            return tmp.enter_context(nc.sbuf_tensor(f"att_{n}", shape, dt))

        def sem(n):
            return own.get(f"att_{n}")

        own = Semaphores(nc)

        RP = 8
        xin, xres, xout = ([sb(f"{n}{p}", [P, TB, E]) for p in range(2)] for n in ("xin", "xres", "xout"))
        eps = sb("eps", [P, 1])
        st = sb("st", [P, TB, 6])
        mv = sb("mv", [P, TB, 2])
        lnv, rstd = (sb(n, [P, TB]) for n in ("lnv", "rstd"))
        xn = sb("xn", [P, TB, E])
        xh, xl = ([sb(f"{n}{p}", [P, T], F16) for p in range(2)] for n in ("xh", "xl"))
        raw = sb("raw", [P, 2 * T], F16)
        qp, kp = ([sb(f"{n}{p}", [P, HG, T], F16) for p in range(2)] for n in ("qp", "kp"))
        vx = [sb(f"vx{p}", [P, TB, H, 2, D + 1], F16) for p in range(2)]
        mx = [sb(f"mx{p}", [P, H, 3]) for p in range(2)]
        mneg = sb("mneg", [P, TB, H])
        mrow = sb("mrow", [P, TB, H, ROW], F16)
        p32 = sb("p32", [P, RP, SW])
        ph, pl = (sb(n, [P, RP, SW], F16) for n in ("ph", "pl"))
        yrec = sb("yrec", [P, TB, H])
        yn = sb("yn", [P, TB, E])
        yT = sb("yT", [P, T])

        x_in, x_res, x_out = ([sem(f"{n}{p}") for p in range(2)] for n in ("x_in", "x_res", "x_out"))
        stats_seen = sem("stats_seen")
        (ready, front_dve, front_act, front_pe, proj_pe, proj_act, proj_dve, maxi_dve, maxi_pe, tail_dve, tail_pe,
         tail_act, s_ps, max_done, st_ps, exp_done, high_done, low_done, pv_done) = (
            sem(n) for n in ("ready", "front_dve", "front_act", "front_pe", "proj_pe", "proj_act", "proj_dve",
                             "maxi_dve", "maxi_pe", "tail_dve", "tail_pe", "tail_act", "s_in_psum", "max_done",
                             "st_in_psum", "exp_done", "high_done", "low_done", "pv_done"))

        ps_s, ps_st, ps_y, ps_x = bank[0:2], bank[2:4], bank[4:6], bank[6:8]
        srcb = src.rearrange("b (k p) e -> b p k e", p=P)
        dstb = dst.rearrange("b (k p) e -> b p k e", p=P)
        block = tmp.enter_context(nc.Block())

        def at(names, b, name):
            return b * len(names) + names.index(name) + 1

        def pairs(eng, count, step):
            for p in range(2):
                step(0, p)
            with eng.Fori(1, count // 2 - 1) as i:
                for p in range(2):
                    step(i, p)
            for p in range(2):
                step(count // 2 - 1, p)

        def first(i, p):
            return isinstance(i, int) and i == 0 and p == 0

        def last(i, p):
            return isinstance(i, int) and i == B // 2 - 1 and p == 1

        def nxt(i, p):
            return None if last(i, p) else (i, 1) if p == 0 else (i + 1, 0)

        def nxt2(i, p):
            return None if isinstance(i, int) and i == B // 2 - 1 else (i + 1, p)

        def prv(i, p):
            return None if first(i, p) else (i - 1, 1) if p == 0 else (i, 0)

        @block.sync
        def _(sp):
            def load(i, p):
                b = 2 * i + p
                if not (isinstance(i, int) and i == 0):
                    sp.wait_ge(front_dve, at(FRONT_DVE, b - 2, "xn1"))
                sp.dma_start(xin[p][:, :, :], srcb[b]).then_inc(x_in[p], 16)

            def load_res(i, p):
                b = 2 * i + p
                if not (isinstance(i, int) and i == 0):
                    sp.wait_ge(tail_pe, 2 * (b - 1))
                sp.dma_start(xres[p][:, :, :], srcb[b]).then_inc(x_res[p], 16)

            def store(i, p):
                b = 2 * i + p
                sp.wait_ge(tail_dve, at(TAIL_DVE, b, "out"))
                sp.dma_start(dstb[b], xout[p][:, :, :]).then_inc(x_out[p], 16)
            load(0, 0)
            load(0, 1)

            def step(i, p):
                if nxt2(i, p):
                    load(*nxt2(i, p))
                load_res(i, p)
                if prv(i, p):
                    store(*prv(i, p))
            pairs(sp, B, step)
            store(B // 2 - 1, 1)
            for p in range(2):
                sp.wait_ge(x_out[p], 16 * (B // 2))

        @block.gpsimd
        def _(pool):
            pool.memset(eps[:, :], LN_EPS).then_inc(ready, 1)
            pool.memset(mrow[:, :, :, :], 0.0).then_inc(ready, 1)
            for p in range(2):
                pool.memset(vx[p][:, :, :, 0, D], 2.0 ** AS).then_inc(ready, 1)
                pool.memset(vx[p][:, :, :, 1, D], 0.0).then_inc(ready, 1)

            def step(i, p):
                b = 2 * i + p
                for h in range(H):
                    pool.wait_ge(high_done, b * H + h + 1)
                    nc.gpsimd.tensor_tensor(pl[:, h % RP, :], p32[:, h % RP, :], ph[:, h % RP, :],
                                            ALU.subtract).then_inc(low_done, 1)
            pairs(pool, B, step)

        @block.tensor
        def _(pe):
            pe.wait_ge(ready, 6)
            mm = nc.tensor.matmul

            def front(i, p):
                b = 2 * i + p
                pe.wait_ge(front_dve, at(FRONT_DVE, b, "xn1"))
                if not (isinstance(i, int) and i == 0):
                    bb = b - 3
                    if not (isinstance(b, int) and b < 3):
                        pe.wait_ge(tail_act, bb + 1)
                    pe.wait_ge(proj_dve, at(PROJ, b - 1, "k23"))
                elif p == 1:
                    pe.wait_ge(front_dve, at(FRONT_DVE, 0, "x_low"))
                for k in range(TB):
                    ins = nc.tensor.transpose(ps_x[1][:, P * k:P * k + P], xn[:, k, :], ident[:, :])
                ins.then_inc(front_pe, 1)

            def proj(name, i, p):
                b = 2 * i + p
                three = ((0, xh), (0, xl), (1, xh))
                ps = ps_x[0 if name in ("q01", "k01", "v") else 1]
                if name == "q01":
                    pe.wait_ge(front_dve, at(FRONT_DVE, b, "x_low"))
                    if not first(i, p):
                        pe.wait_ge(maxi_dve, at(MAXI, b - 1, "add0"))
                elif name == "q23":
                    if first(i, p):
                        pe.wait_ge(front_dve, at(FRONT_DVE, 1, "x_low"))
                    else:
                        pe.wait_ge(maxi_dve, at(MAXI, b - 1, "add1"))
                else:
                    pe.wait_ge(proj_dve, at(PROJ, b, {"k01": "q01", "k23": "q23", "v": "k01"}[name]))
                if name == "v":
                    for k in range(TB):
                        for n, (w, x) in enumerate(three):
                            ins = mm(ps[:, P * k:P * k + P], x[p][:, P * k:P * k + P], X.wv[w][:, :],
                                     start=(n == 0), stop=(n == 2))
                else:
                    w = X.wq if name[0] == "q" else X.wk
                    for s in range(2):
                        g = int(name[1]) + s
                        for n, (wn, x) in enumerate(three):
                            ins = mm(ps[:, T * s:T * s + T], w[wn][:, g, :], x[p][:, :], start=(n == 0), stop=(n == 2))
                ins.then_inc(proj_pe, 1)

            def s_pass(i, p, h):
                b = 2 * i + p
                g, r = h // HL, ROW * (h % HL)
                if h == 0:
                    pe.wait_ge(proj_dve, at(PROJ, b, "k23"))
                if not (first(i, p) and h < 2):
                    pe.wait_ge(max_done, b * H + h - 1)
                ps = ps_s[h % 2]
                mm(ps[:, 0:P], X.identb[:, :], X.mask_ts[:, :], start=True, stop=True)
                for k, o, n in ((1, 0, 2 * P), (0, 2 * P, P)):
                    mm(ps[:, o:o + n], qp[p][r:r + ROW, g, P * k:P * k + P], kp[p][r:r + ROW, g, 0:n],
                       start=(k == 1), stop=False)
                ins = mm(ps[:, P:3 * P].rearrange("p (a n) -> p a n", a=2), X.identb[:, :],
                         X.mask_ts[:, :].unsqueeze(1).to_broadcast([P, 2, P]), start=False, stop=True)
                ins.then_inc(s_ps, 1)

            def turn_max(i, p):
                b = 2 * i + p
                pe.wait_ge(maxi_dve, at(MAXI, b, "low"))
                for n in range(2):
                    if n == 0:
                        if first(i, p):
                            pe.wait_ge(proj_dve, at(PROJ, 0, "v"))
                        else:
                            pe.wait_ge(proj_dve, at(PROJ, b, "v"))
                            if not (isinstance(b, int) and b < 2):
                                pe.wait_ge(tail_dve, at(TAIL_DVE, b - 2, "out"))
                    else:
                        pe.wait_ge(proj_dve, at(PROJ, b, "k23"))
                        if not last(i, p):
                            pe.wait_ge(front_dve, at(FRONT_DVE, b + 1, "x_low"))
                        if not (isinstance(b, int) and b < 2):
                            pe.wait_ge(tail_act, b - 1)
                    for s in range(2):
                        for k in range(TB):
                            g = 2 * n + s
                            ins = mm(ps_x[n][:, T * s + P * k:T * s + P * k + P],
                                     mrow[:, TB - 1 - k, HL * g:HL * g + HL, :].rearrange("p h r -> p (h r)"), X.ident16[:, :],
                                     start=True, stop=True)
                    ins.then_inc(maxi_pe, 1)

            def st_pass(i, p, h):
                b = 2 * i + p
                g, r = h // HL, ROW * (h % HL)
                if h == 0:
                    pe.wait_ge(maxi_dve, at(MAXI, b, "add1"))
                if not (first(i, p) and h < 2):
                    pe.wait_ge(high_done, b * H + h - 1)
                ps = ps_st[h % 2]
                cols = ps[:, :].rearrange("p (a n) -> p a n", n=P)
                mm(cols[:, 0:3:2, :], kp[p][r:r + ROW, g, 0:P],
                   qp[p][r:r + ROW, g, :].rearrange("p (a n) -> p a n", n=P), start=True, stop=False)
                mm(cols[:, 1, :], kp[p][r:r + ROW, g, P:T], qp[p][r:r + ROW, g, P:T], start=False, stop=False)
                ins = mm(cols[:, 0:2, :], X.identb[:, :], X.mask_st[:, :].unsqueeze(1).to_broadcast([P, 2, P]),
                         start=False, stop=True)
                ins.then_inc(st_ps, 1)

            def pv(i, p, h):
                b = 2 * i + p
                pe.wait_ge(low_done, b * H + h + 1)
                if h == 0:
                    pe.wait_ge(proj_dve, at(PROJ, b, "v"))
                    if not (isinstance(i, int) and i == 0):
                        pe.wait_ge(tail_dve, at(TAIL_DVE, b - 2, "yn"))
                for k, blocks in ((0, ((0, 0),)), (1, ((2 * P, 0), (P, 1)))):
                    todo = [(pt, o, s, a) for o, s in blocks for pt, a in ((ph, 0), (ph, 1), (pl, 0))]
                    at_y = (k * H + h) * (D + 1)
                    for n, (pt, o, s, a) in enumerate(todo):
                        ins = mm(ps_y[p][:, at_y:at_y + D + 1], pt[:, h % RP, o:o + P], vx[p][:, s, h, a, :],
                                 start=(n == 0), stop=(n == len(todo) - 1))
                ins.then_inc(pv_done, 1)

            def tail_turn(i, p):
                b = 2 * i + p
                pe.wait_ge(tail_dve, at(TAIL_DVE, b, "yn"))
                if not last(i, p):
                    pe.wait_ge(maxi_dve, at(MAXI, b + 1, "add1"))
                    if nxt2(i, p):
                        pe.wait_ge(proj_dve, at(PROJ, b + 2, "k23"))
                for k in range(TB):
                    ins = nc.tensor.transpose(ps_x[1][:, P * k:P * k + P], yn[:, k, :], ident[:, :])
                ins.then_inc(tail_pe, 1)

            def tail_out(i, p):
                b = 2 * i + p
                pe.wait_ge(tail_act, b + 1)
                pe.wait_ge(x_res[p], 16 * (i + 1))
                if not last(i, p):
                    pe.wait_ge(maxi_dve, at(MAXI, b + 1, "add0"))
                    if nxt2(i, p):
                        pe.wait_ge(proj_dve, at(PROJ, b + 2, "v"))
                if last(i, p):
                    pe.wait_ge(tail_dve, at(TAIL_DVE, b - 1, "out"))
                mm(ps_x[0][:, 0:T], ident[:, :], xres[p][:, :, :].rearrange("p k e -> p (k e)"), start=True, stop=False)
                for k in range(TB):
                    ins = mm(ps_x[0][:, P * k:P * k + P], yT[:, P * k:P * k + P], X.wo[:, :], start=False,
                             stop=(k == TB - 1))
                ins.then_inc(tail_pe, 1)

            front(0, 0)
            front(0, 1)
            for name in PROJ:
                proj(name, 0, 0)
            for h in range(H):
                s_pass(0, 0, h)
            turn_max(0, 0)

            def step(i, p):
                for h in range(H):
                    st_pass(i, p, h)
                    if nxt(i, p):
                        for name in PROJ:
                            if PROJ_AT[name] == h:
                                proj(name, *nxt(i, p))
                        for g in range(H):
                            if SCORES_AT[g] == h:
                                s_pass(*nxt(i, p), g)
                    if h >= PV_LAG:
                        pv(i, p, h - PV_LAG)
                    elif prv(i, p):
                        pv(*prv(i, p), h - PV_LAG + H)
                    if prv(i, p):
                        if h == TAIL_TURN_AT:
                            tail_turn(*prv(i, p))
                        if h == TAIL_OUT_AT:
                            tail_out(*prv(i, p))
                    if nxt2(i, p) and h == FRONT_PE_AT:
                        front(*nxt2(i, p))
                    if nxt(i, p) and h == TURN_AT:
                        turn_max(*nxt(i, p))
            pairs(pe, B, step)
            for h in range(H - PV_LAG, H):
                pv(B // 2 - 1, 1, h)
            tail_turn(B // 2 - 1, 1)
            tail_out(B // 2 - 1, 1)

        @block.scalar
        def _(act):
            nc.scalar.preload_act_table_set("natural_log_exp_and_others")
            act.wait_ge(ready, 6)
            a = nc.scalar.activation

            def front(name, i, p):
                b = 2 * i + p
                if name == "rstd_log":
                    act.wait_ge(front_dve, at(FRONT_DVE, b, "aggr1"))
                    ins = a(lnv[:, :], mv[:, :, 1], ACT.Ln, bias=eps[:, :])
                elif name == "rstd":
                    act.wait_ge(front_act, at(FRONT_ACT, b, "rstd_log"))
                    ins = a(rstd[:, :], lnv[:, :], ACT.Exp, scale=-0.5)
                else:
                    act.wait_ge(front_pe, b + 1)
                    if not (isinstance(i, int) and i == 0):
                        act.wait_ge(proj_pe, at(PROJ, b - 2, "v"))
                    ins = a(xh[p][:, :], ps_x[1][:, 0:T], ACT.Copy)
                ins.then_inc(front_act, 1)

            def proj(name, i, p):
                b = 2 * i + p
                act.wait_ge(proj_pe, at(PROJ, b, name))
                if name != "q01":
                    act.wait_ge(proj_dve, at(PROJ, b, PROJ[PROJ.index(name) - 1]))
                ps = ps_x[0 if name in ("q01", "k01", "v") else 1]
                if name == "v":
                    if not (isinstance(i, int) and i == 0):
                        act.wait_ge(pv_done, (b - 1) * H)
                    ins = a(vx[p][:, :, :, 0, 0:D], ps[:, 0:T].rearrange("p (k h d) -> p k h d", k=TB, d=D), ACT.Copy)
                elif name[0] == "q":
                    ins = a(raw[:, :], ps[:, :], ACT.Copy)
                else:
                    ins = a(raw[:, :], ps[:, :], ACT.Identity, bias=X.k_bias[:, :])
                ins.then_inc(proj_act, 1)

            def exps(i, p, h):
                b = 2 * i + p
                act.wait_ge(st_ps, b * H + h + 1)
                if not (first(i, p) and h < RP):
                    act.wait_ge(low_done, b * H + h - RP + 1)
                a(p32[:, h % RP, :], ps_st[h % 2][:, 0:SW], ACT.Exp, scale=2.0 ** (-2 * AS)).then_inc(exp_done, 1)
                if not (first(i, p) and h < RP):
                    act.wait_ge(pv_done, b * H + h - RP + 1)
                a(ph[:, h % RP, :], ps_st[h % 2][:, 0:SW], ACT.Exp, scale=2.0 ** (-2 * AS)).then_inc(high_done, 1)

            def tail(i, p):
                b = 2 * i + p
                act.wait_ge(tail_pe, 2 * b + 1)
                a(yT[:, :], ps_x[1][:, 0:T], ACT.Copy).then_inc(tail_act, 1)

            for p in range(2):
                for name in FRONT_ACT:
                    front(name, 0, p)
            for name in PROJ:
                proj(name, 0, 0)

            def step(i, p):
                for h in range(H):
                    exps(i, p, h)
                    if nxt(i, p):
                        for name in PROJ:
                            if PROJ_AT[name] == h:
                                proj(name, *nxt(i, p))
                    if prv(i, p) and h == TAIL_ACT_AT:
                        tail(*prv(i, p))
                    if nxt2(i, p):
                        for name in FRONT_ACT:
                            if FRONT_ACT_AT[name] == h:
                                front(name, *nxt2(i, p))
            pairs(act, B, step)
            tail(B // 2 - 1, 1)

        @block.vector
        def _(dve):
            v = nc.vector
            dve.wait_ge(ready, 6)

            def front(name, i, p):
                b = 2 * i + p
                k = int(name[-1]) if name[-1].isdigit() else 0
                if name.startswith("stats"):
                    dve.wait_ge(x_in[p], 16 * (i + 1))
                    ins = v.bn_stats(st[:, k, :], xin[p][:, k, :])
                elif name.startswith("aggr"):
                    dve.wait_ge(front_dve, at(FRONT_DVE, b, f"stats{k}"))
                    dve.sem_inc(stats_seen, 1)
                    ins = v.bn_aggr(mv[:, k, :], st[:, k, :])
                elif name.startswith("xn"):
                    dve.wait_ge(front_act, at(FRONT_ACT, b, "rstd"))
                    ins = v.tensor_scalar(xn[:, k, :], xin[p][:, k, :], mv[:, k, 0:1], rstd[:, k:k + 1],
                                          ALU.subtract, ALU.mult)
                else:
                    dve.wait_ge(front_act, at(FRONT_ACT, b, "x_high"))
                    ins = v.tensor_tensor(xl[p][:, :], ps_x[1][:, 0:T], xh[p][:, :], ALU.subtract)
                ins.then_inc(front_dve, 1)

            def proj(name, i, p):
                b = 2 * i + p
                dve.wait_ge(proj_act, at(PROJ, b, name))
                ps = ps_x[0 if name in ("q01", "k01", "v") else 1]
                if name == "v":
                    ins = v.tensor_tensor(vx[p][:, :, :, 1, 0:D].rearrange("p k h d -> p (k h) d"),
                                          ps[:, 0:T].rearrange("p (k h d) -> p (k h) d", k=TB, d=D),
                                          vx[p][:, :, :, 0, 0:D].rearrange("p k h d -> p (k h) d"), ALU.subtract)
                else:
                    q = name[0] == "q"
                    g = int(name[1])
                    ins = v.scalar_tensor_tensor((qp if q else kp)[p][:, g:g + 2, :].rearrange("p g t -> p (g t)"),
                                                 raw[:, :], (X.q_low if q else X.k_low)[:, :], ps[:, :],
                                                 ALU.mult, ALU.add)
                ins.then_inc(proj_dve, 1)

            def maxima(i, p, h):
                b = 2 * i + p
                dve.wait_ge(s_ps, b * H + h + 1)
                ps = ps_s[h % 2]
                v.tensor_reduce(mx[p][:, h, :], ps[:, 0:SW].rearrange("p (a n) -> p a n", n=P), AX_X,
                                ALU.max).then_inc(max_done, 1)

            def maxi(name, i, p):
                b = 2 * i + p
                if name == "larger":
                    dve.wait_ge(max_done, (b + 1) * H)
                    ins = v.tensor_tensor(mx[p][:, :, 0], mx[p][:, :, 0], mx[p][:, :, 1], ALU.max)
                elif name == "m":
                    dve.wait_ge(maxi_dve, at(MAXI, b, "larger"))
                    ins = v.tensor_scalar(mneg[:, :, :], mx[p][:, :, 0:3:2].rearrange("p h k -> p k h"),
                                          -(2.0 ** (-2 * AS)), None, ALU.mult)
                elif name == "high":
                    dve.wait_ge(maxi_dve, at(MAXI, b, "m"))
                    if not first(i, p):
                        dve.wait_ge(maxi_pe, 2 * b)
                    ins = v.tensor_copy(mrow[:, :, :, 3 * D], mneg[:, :, :])
                elif name == "low":
                    dve.wait_ge(maxi_dve, at(MAXI, b, "high"))
                    ins = v.tensor_tensor(mrow[:, :, :, 3 * D + 1], mneg[:, :, :], mrow[:, :, :, 3 * D], ALU.subtract)
                else:
                    n = int(name[3])
                    dve.wait_ge(maxi_pe, 2 * b + n + 1)
                    o = qp[p][:, 2 * n:2 * n + 2, :].rearrange("p g t -> p (g t)")
                    ins = v.tensor_tensor(o, ps_x[n][:, :], o, ALU.add)
                ins.then_inc(maxi_dve, 1)

            def tail(name, i, p):
                b = 2 * i + p
                yv = ps_y[p][:, 0:TB * H * (D + 1)].rearrange("p (r d) -> p r d", d=D + 1)
                if name == "rec":
                    dve.wait_ge(pv_done, (b + 1) * H)
                    ins = v.reciprocal(yrec[:, :, :].rearrange("p k h -> p (k h)"), yv[:, :, D])
                elif name == "yn":
                    dve.wait_ge(tail_dve, at(TAIL_DVE, b, "rec"))
                    if not first(i, p):
                        dve.wait_ge(tail_pe, 2 * (b - 1) + 1)
                    ins = v.tensor_tensor(yn[:, :, :].rearrange("p k (h d) -> p (k h) d", d=D), yv[:, :, 0:D],
                                          yrec[:, :, :].rearrange("p k h -> p (k h)").unsqueeze(2).to_broadcast([P, TB * H, D]),
                                          ALU.mult)
                else:
                    dve.wait_ge(tail_pe, 2 * b + 2)
                    if not (isinstance(i, int) and i == 0):
                        dve.wait_ge(x_out[p], 16 * i)
                    ins = v.tensor_copy(xout[p][:, :, :].rearrange("p k e -> p (k e)"), ps_x[0][:, 0:T])
                ins.then_inc(tail_dve, 1)

            for p in range(2):
                for name in FRONT_DVE:
                    front(name, 0, p)
            for name in PROJ:
                proj(name, 0, 0)
            for h in range(H):
                maxima(0, 0, h)
            for name in MAXI:
                maxi(name, 0, 0)

            def step(i, p):
                for h in range(H):
                    if nxt(i, p):
                        for name in PROJ:
                            if PROJ_AT[name] == h:
                                proj(name, *nxt(i, p))
                        for g in range(H):
                            if SCORES_AT[g] == h:
                                maxima(*nxt(i, p), g)
                    if prv(i, p):
                        for name in TAIL_DVE:
                            if TAIL_DVE_AT[name] == h:
                                tail(name, *prv(i, p))
                    if nxt2(i, p):
                        for name in FRONT_DVE:
                            if FRONT_DVE_AT[name] == h:
                                front(name, *nxt2(i, p))
                    if nxt(i, p):
                        for name in MAXI:
                            if MAXI_AT[name] == h:
                                maxi(name, *nxt(i, p))
            pairs(dve, B, step)
            for name in TAIL_DVE:
                tail(name, B // 2 - 1, 1)
    own.release()


def build(nc, A):
    with ExitStack() as ctx:
        def sb(name, shape, dt=F32):
            return ctx.enter_context(nc.sbuf_tensor(name, shape, dt))

        def sem(name):
            return ctx.enter_context(nc.semaphore(name))

        bank = [ctx.enter_context(nc.psum_tensor(f"bank{k}", [P, 512], F32)) for k in range(8)]
        ident = sb("ident", [P, P])
        head_ones = sb("head_ones", [P, P])
        setup_masks(nc, ctx, ident, head_ones)
        scan(nc, ctx, A, ident, head_ones, bank)
        experts = Experts(sb, sem)
        heads = Attention(sb)
        with ExitStack() as tmp, nc.Block() as block:
            setup_attention(nc, ctx, tmp, block, A, heads, ident, head_ones, bank)
            setup_experts(nc, ctx, tmp, block, A, experts, ident, bank)
        ffn(nc, ctx, A, experts, ident, bank, "ffn1", A["x1"], A["x2"])
        attention(nc, ctx, A, heads, ident, bank, A["x2"], A["x3"])
        ffn(nc, ctx, A, experts, ident, bank, "ffn2", A["x3"], A["out"])


INPUTS = dict(x="L0_attn_a_x", Wq="L0_attn_a_Wq", Wk="L0_attn_a_Wk", Wv="L0_attn_a_Wv", Walpha="L0_attn_a_Walpha",
              Wbeta="L0_attn_a_Wbeta", A_log="L0_attn_a_A_log", dt_bias="L0_attn_a_dt_bias",
              Wgate="L0_attn_a_Wgate", Wout="L0_attn_a_Wout", rms_w="L0_attn_a_rms_w",
              W_qkv="L0_attn_b_W_qkv", W_q_lsr="L0_attn_b_W_q_lsr", W_k_lsr="L0_attn_b_W_k_lsr",
              core="L0_attn_b_lsr_core", W_o="L0_attn_b_W_o",
              Wg="L0_ffn_Wg", W1="L0_ffn_W1", b1="L0_ffn_b1", W2="L0_ffn_W2", b2="L0_ffn_b2")


def kernel(**inputs):
    import numpy as np
    import concourse.bacc as bacc
    from concourse.bass_utils import run_bass_kernel_spmd

    nc = bacc.Bacc("TRN2", target_bir_lowering=False, num_devices=1)
    arrays, A = {}, {}
    for name, long_name in INPUTS.items():
        a = np.ascontiguousarray(inputs[long_name])
        arrays[f"in_{name}"] = a
        A[name] = nc.dram_tensor(f"in_{name}", a.shape, mybir.dt.from_np(a.dtype), kind="ExternalInput").ap()
    for name in ("x1", "x2", "x3"):
        A[name] = nc.dram_tensor(name, (B, T, E), F32).ap()
    A["normed"] = nc.dram_tensor("normed", (B * T, E), F32).ap()
    A["picked"] = nc.dram_tensor("picked", (2 * B * T + NS, E), F32).ap()
    A["out"] = nc.dram_tensor("out", (B, T, E), F32, kind="ExternalOutput").ap()
    build(nc, A)
    r = run_bass_kernel_spmd(nc, [arrays], core_ids=[0])
    return r.results[0]["out"]
```
